# Optimizing a Trainium2 kernel written in Bass

```python
import numpy as np
import jax
import jax.numpy as jnp

def _softmax(x, axis=-1):
    return jax.nn.softmax(x, axis=axis)

def _gelu(x):
    return jax.nn.gelu(x, approximate=True)

def _silu(x):
    return jax.nn.silu(x)

def _sigmoid(x):
    return jax.nn.sigmoid(x)

def _layernorm(x, axis=-1, eps=1e-05):
    m = jnp.mean(x, axis=axis, keepdims=True)
    v = jnp.var(x, axis=axis, keepdims=True)
    return (x - m) / jnp.sqrt(v + eps)

def _scatter_add(tgt, idx, src, axis=0):
    return tgt.at[idx].add(src)

def _segment_sum(src, seg, n):
    return jax.ops.segment_sum(src, seg, n)
kernel_name = 'mk_decoder_preln_d1_seqx_r8_b0f582'

def setup_inputs(seed: int=0):
    np.random.seed(seed)
    _w = jnp.asarray

    def _rec_inputs():
        import jax
        import jax.numpy as jnp
        _rk = jax.random.key(seed)
        x = -0.0005207 + 1.001 * jax.random.normal(jax.random.fold_in(_rk, 1), (16, 56, 512), jnp.float32)
        _lenS = 56 - jax.random.randint(jax.random.fold_in(_rk, 7), (16,), 0, max(1, 56 // 4) + 1, jnp.int32)
        _lenS2 = 1500 - jax.random.randint(jax.random.fold_in(_rk, 8), (16,), 0, max(1, 1500 // 4) + 1, jnp.int32)
        _ctx_4096P = jax.random.normal(jax.random.fold_in(_rk, 11), (16, 16, 512), jnp.float32)
        _ctx_4096c = jax.random.dirichlet(jax.random.fold_in(_rk, 511), 0.3 * jnp.ones((16,), jnp.float32), (16, 1500))
        _ctx_4096t = jnp.einsum('bsk,bkd->bsd', _ctx_4096c, _ctx_4096P)
        _ctx_4096t = _ctx_4096t * jax.lax.rsqrt(jnp.mean(jnp.square(_ctx_4096t)) + 1e-12) * 0.953939
        ctx_4096 = -0.00010331 + 0.999899 * (_ctx_4096t + 0.3 * jax.random.normal(jax.random.fold_in(_rk, 611), (16, 1500, 512), jnp.float32))
        return (x, ctx_4096)
    x, ctx_4096 = _rec_inputs()

    def _L0_attn_setup():
        import jax, jax.numpy as jnp
        import numpy as np
        B, T, D = (2, 256, 512)
        H = 32
        HKV = 1
        HD = D // H
        key = jax.random.key(seed)
        ks = jax.random.split(key, 9)
        s = lambda fan_in: 1.0 / np.sqrt(fan_in)
        return {'x': jax.random.normal(ks[0], (B, T, D), dtype=jnp.float32), 'wq_w': jax.random.normal(ks[1], (H * HD, D), dtype=jnp.float32) * s(D), 'wq_b': jax.random.normal(ks[2], (H * HD,), dtype=jnp.float32) * 0.02, 'wk_w': jax.random.normal(ks[3], (HKV * HD, D), dtype=jnp.float32) * s(D), 'wk_b': jax.random.normal(ks[4], (HKV * HD,), dtype=jnp.float32) * 0.02, 'wv_w': jax.random.normal(ks[5], (HKV * HD, D), dtype=jnp.float32) * s(D), 'wv_b': jax.random.normal(ks[6], (HKV * HD,), dtype=jnp.float32) * 0.02, 'wo_w': jax.random.normal(ks[7], (D, H * HD), dtype=jnp.float32) * s(H * HD), 'wo_b': jax.random.normal(ks[8], (D,), dtype=jnp.float32) * 0.02}
    _L0_attn_all = _L0_attn_setup()
    _L0_attn_in = {k: v for k, v in _L0_attn_all.items() if k in ('wq_w', 'wq_b', 'wk_w', 'wk_b', 'wv_w', 'wv_b', 'wo_w', 'wo_b')}
    del _L0_attn_all

    def _L0_xattn_setup():
        import jax, jax.numpy as jnp
        import numpy as np
        import math
        HIDDEN = 512
        N_HEADS = 32
        HEAD_DIM = 128
        N_KV_HEADS = 4
        N_GROUPS = N_HEADS // N_KV_HEADS
        key = jax.random.key(seed)
        ks = jax.random.split(key, 6)
        B, NL, S = (8, 64, 512)
        latents = jax.random.normal(ks[0], (B, NL, HIDDEN), dtype=jnp.float32)
        context = jax.random.normal(ks[1], (B, S, HIDDEN), dtype=jnp.float32)
        scale = 1.0 / math.sqrt(HIDDEN)
        Wq = jax.random.normal(ks[2], (HIDDEN, N_HEADS * HEAD_DIM), dtype=jnp.float32) * scale
        Wk = jax.random.normal(ks[3], (HIDDEN, N_KV_HEADS * HEAD_DIM), dtype=jnp.float32) * scale
        Wv = jax.random.normal(ks[4], (HIDDEN, N_KV_HEADS * HEAD_DIM), dtype=jnp.float32) * scale
        Wo = jax.random.normal(ks[5], (N_HEADS * HEAD_DIM, HIDDEN), dtype=jnp.float32) * scale
        return {'latents': latents, 'context': context, 'Wq': Wq, 'Wk': Wk, 'Wv': Wv, 'Wo': Wo}
    _L0_xattn_all = _L0_xattn_setup()
    _L0_xattn_in = {k: v for k, v in _L0_xattn_all.items() if k in ('Wq', 'Wk', 'Wv', 'Wo')}
    del _L0_xattn_all

    def _L0_ffn_setup():
        import jax, jax.numpy as jnp
        import numpy as np
        BATCH, SEQ, D = (2, 256, 512)
        K, TOPK, RANK = (64, 16, 16)
        ALPHA = 32.0
        SCALING = ALPHA / RANK
        key = jax.random.key(seed)
        k1, k2, k3, k4 = jax.random.split(key, 4)
        x = jax.random.normal(k1, (BATCH, SEQ, D), dtype=jnp.float32)
        A = jax.random.normal(k2, (K, RANK, D), dtype=jnp.float32) * 0.02
        B = jax.random.normal(k3, (K, D, RANK), dtype=jnp.float32) * 0.02
        Wr = jax.random.normal(k4, (K, D), dtype=jnp.float32) * 0.02
        return {'x': x, 'A': A, 'B': B, 'Wr': Wr}
    _L0_ffn_all = _L0_ffn_setup()
    _L0_ffn_in = {k: v for k, v in _L0_ffn_all.items() if k in ('A', 'B', 'Wr')}
    del _L0_ffn_all
    return {'x': x, 'ctx_4096': ctx_4096, 'L0_attn_wq_w': _L0_attn_in['wq_w'], 'L0_attn_wq_b': _L0_attn_in['wq_b'], 'L0_attn_wk_w': _L0_attn_in['wk_w'], 'L0_attn_wk_b': _L0_attn_in['wk_b'], 'L0_attn_wv_w': _L0_attn_in['wv_w'], 'L0_attn_wv_b': _L0_attn_in['wv_b'], 'L0_attn_wo_w': _L0_attn_in['wo_w'], 'L0_attn_wo_b': _L0_attn_in['wo_b'], 'L0_xattn_Wq': _L0_xattn_in['Wq'], 'L0_xattn_Wk': _L0_xattn_in['Wk'], 'L0_xattn_Wv': _L0_xattn_in['Wv'], 'L0_xattn_Wo': _L0_xattn_in['Wo'], 'L0_ffn_A': _L0_ffn_in['A'], 'L0_ffn_B': _L0_ffn_in['B'], 'L0_ffn_Wr': _L0_ffn_in['Wr']}

def reference(x, ctx_4096, L0_attn_wq_w, L0_attn_wq_b, L0_attn_wk_w, L0_attn_wk_b, L0_attn_wv_w, L0_attn_wv_b, L0_attn_wo_w, L0_attn_wo_b, L0_xattn_Wq, L0_xattn_Wk, L0_xattn_Wv, L0_xattn_Wo, L0_ffn_A, L0_ffn_B, L0_ffn_Wr):
    import jax
    import jax.numpy as jnp

    def _L0_attn_ref(x, wq_w, wq_b, wk_w, wk_b, wv_w, wv_b, wo_w, wo_b):
        import jax, jax.numpy as jnp
        import numpy as np
        B, T, D = (2, 256, 512)
        H = 32
        HKV = 1
        HD = D // H
        b, t, d = x.shape
        q = (x @ wq_w.T + wq_b).reshape(b, t, H, HD)
        k = (x @ wk_w.T + wk_b).reshape(b, t, HKV, HD)
        v = (x @ wv_w.T + wv_b).reshape(b, t, HKV, HD)
        k1 = k[:, :, 0, :]
        v1 = v[:, :, 0, :]
        scores = jnp.einsum('bqhd,bkd->bhqk', q, k1) / jnp.sqrt(jnp.float32(HD))
        causal = jnp.tril(jnp.ones((t, t), dtype=bool))
        scores = jnp.where(causal, scores, -jnp.inf)
        weights = jax.nn.softmax(scores, axis=-1)
        attn = jnp.einsum('bhqk,bkd->bqhd', weights, v1)
        attn = attn.reshape(b, t, H * HD)
        return attn @ wo_w.T + wo_b

    def _L0_xattn_ref(latents, context, Wq, Wk, Wv, Wo):
        import jax, jax.numpy as jnp
        import numpy as np
        import math
        HIDDEN = 512
        N_HEADS = 32
        HEAD_DIM = 128
        N_KV_HEADS = 4
        N_GROUPS = N_HEADS // N_KV_HEADS
        b, q_len, _ = latents.shape
        kv_len = q_len + context.shape[1]
        hidden_states = jnp.concatenate([context, latents], axis=1)
        q = (latents @ Wq).reshape(b, q_len, N_KV_HEADS, N_GROUPS, HEAD_DIM)
        k = (hidden_states @ Wk).reshape(b, kv_len, N_KV_HEADS, HEAD_DIM)
        v = (hidden_states @ Wv).reshape(b, kv_len, N_KV_HEADS, HEAD_DIM)
        scale = 1.0 / math.sqrt(HEAD_DIM)
        scores = jnp.einsum('bqhgd,bkhd->bhgqk', q, k) * scale
        attn = jax.nn.softmax(scores.astype(jnp.float32), axis=-1).astype(q.dtype)
        out = jnp.einsum('bhgqk,bkhd->bqhgd', attn, v)
        out = out.reshape(b, q_len, N_HEADS * HEAD_DIM)
        return out @ Wo

    def _L0_ffn_ref(x, A, B, Wr):
        import jax, jax.numpy as jnp
        import numpy as np
        BATCH, SEQ, D = (2, 256, 512)
        K, TOPK, RANK = (64, 16, 16)
        ALPHA = 32.0
        SCALING = ALPHA / RANK
        prefix = x.shape[:-1]
        xf = x.reshape(-1, x.shape[-1])
        N = xf.shape[0]
        scores = xf @ Wr.T
        top_vals, top_idx = jax.lax.top_k(scores, TOPK)
        gates = jax.nn.softmax(top_vals, axis=-1)
        G = jnp.zeros((N, K), xf.dtype).at[jnp.arange(N)[:, None], top_idx].set(gates)
        h = jnp.einsum('nd,krd->nkr', xf, A)
        out = jnp.einsum('nkr,kdr->nd', h * G[:, :, None], B)
        return (out * SCALING).reshape(*prefix, -1)
    x = x + _L0_attn_ref(_layernorm(x, axis=-1), L0_attn_wq_w, L0_attn_wq_b, L0_attn_wk_w, L0_attn_wk_b, L0_attn_wv_w, L0_attn_wv_b, L0_attn_wo_w, L0_attn_wo_b)
    x = x + _L0_xattn_ref(_layernorm(x, axis=-1), ctx_4096, L0_xattn_Wq, L0_xattn_Wk, L0_xattn_Wv, L0_xattn_Wo)
    x = x + _L0_ffn_ref(_layernorm(x, axis=-1), L0_ffn_A, L0_ffn_B, L0_ffn_Wr)
    return x

_drawn_inputs = setup_inputs


def setup_inputs(seed=0):
    import zlib

    import numpy as np

    out = dict(_drawn_inputs(seed))
    spreads = {}
    factors = {'L0_attn_wq_b': 8.0,
     'L0_attn_wk_b': 8.0,
     'L0_attn_wv_b': 4.684,
     'L0_attn_wo_b': 4.671,
     'L0_ffn_A': 5.297,
     'L0_ffn_B': 5.122,
     'L0_ffn_Wr': 5.771}
    for name, (base, spread) in spreads.items():
        noise = np.random.default_rng([zlib.crc32(name.encode()), seed]).standard_normal(out[name].shape)
        drawn = base * np.exp(spread * noise) if base else spread * noise
        out[name] = jnp.asarray(drawn.astype(out[name].dtype))
    for name, factor in factors.items():
        out[name] = (out[name] * factor).astype(out[name].dtype)
    return out
```

```python
from contextlib import ExitStack

import concourse.bass as bass
from concourse import mybir

F32 = mybir.dt.float32
F32R = mybir.dt.float32r
ALU = mybir.AluOpType
ACT = mybir.ActivationFunctionType
AX_X = mybir.AxisListType.X

P = 128
BANK = 512
D = 512
DC = D // P
NB, T, S_CTX = 16, 56, 1500
NTOK = NB * T
PAIR = 2 * T
NPAIR = NTOK // PAIR
EPS = 1e-5
NEG = -1e30
LOWEST = -3e38

H1, HD1 = 32, 16
HPC = P // HD1
VX = HD1 + 2

H2, HD2, KVH = 32, 128, 4
GQ = H2 // KVH
SCALE2 = float(HD2) ** -0.5
NQ = GQ * T
KEYS = S_CTX + T
NCH = -(-KEYS // P)
GROUP = 3 * P
NG = 4
GW = [GROUP] * (NG - 1) + [KEYS - GROUP * (NG - 1)]
GWMAX = GW[-1]
CW = [P] * (NCH - 1) + [KEYS - P * (NCH - 1)]

NE, TOPK, RANK = 64, 16, 16
SCALING = 32.0 / RANK


class Space:

    def __init__(self, nc, ctx, stage):
        self.nc, self.ctx, self.stage, self.sems = nc, ctx, stage, []
        ctx.callback(self.release)

    def sb(self, name, shape, dt=F32):
        return self.ctx.enter_context(self.nc.sbuf_tensor(f"{self.stage}_{name}", shape, dt))

    def ps(self, name, shape):
        return self.ctx.enter_context(self.nc.psum_tensor(f"{self.stage}_{name}", shape, F32))

    def sem(self, name):
        self.sems.append(self.nc.alloc_semaphore(f"{self.stage}_{name}"))
        return self.sems[-1]

    def release(self):
        self.nc.clear_and_free_semaphores(self.sems)
        self.nc.all_engine_barrier()


def mm3(nc, out, a, b, start, stop):
    nc.tensor.matmul(out, a[0], b[0], start=start, stop=False)
    nc.tensor.matmul(out, a[0], b[1], start=False, stop=False)
    return nc.tensor.matmul(out, a[1], b[0], start=False, stop=stop)


def self_attention(nc, x, ident, mask, headmask, w_qkv, b_q, b_k, b_v, w_o, b_o, x1, xn2T):
    with ExitStack() as ctx:
        m = Space(nc, ctx, "sa")
        NW = D + P + HD1
        idn = m.sb("ident", [P, P])
        idn_r = m.sb("ident_r", [PAIR, PAIR], F32R)
        msk = m.sb("mask", [PAIR, 4 * PAIR])
        msk_r = m.sb("mask_r", [PAIR, 4 * PAIR], F32R)
        hmask = m.sb("headmask", [P, HPC])
        wqkv = m.sb("w_qkv", [P, DC, NW])
        wo = m.sb("w_o", [P, DC, D])
        bq = m.sb("b_q", [P, DC])
        bk = m.sb("b_k", [P, 1])
        bv = m.sb("b_v", [PAIR, HD1])
        bo = m.sb("b_o", [PAIR, D])
        neghalf = m.sb("neghalf", [PAIR, 1])
        eps = m.sb("eps", [PAIR, 1])
        xt = m.sb("x", [PAIR, D])
        xb = m.sb("x_bias", [PAIR, D])
        stat = m.sb("stat", [PAIR, 6])
        mv = m.sb("meanvar", [PAIR, 2])
        ve = m.sb("var_eps", [PAIR, 1])
        rstd = m.sb("rstd", [PAIR, 1])
        xn = m.sb("xn", [PAIR, D])
        xnT = m.sb("xnT", [P, DC, PAIR])
        qT = m.sb("qT", [P, DC, PAIR])
        kbd = m.sb("k_blockdiag", [P, HPC, PAIR])
        vx = m.sb("v_ones", [PAIR, VX])
        mx = m.sb("rowmax", [PAIR, 2, 4])
        p0 = m.sb("shifted", [PAIR, 2, 4, PAIR])
        pe_ = m.sb("weights", [PAIR, 2, 4, PAIR])
        pT = m.sb("weightsT", [PAIR, 2, 4, PAIR])
        rc = m.sb("recip", [PAIR, H1])
        at = m.sb("attn", [PAIR, H1, HD1])
        aT = m.sb("attnT", [P, DC, PAIR])
        x1t = m.sb("x1", [PAIR, D])
        xn2 = m.sb("xn2", [PAIR, D])
        x2T = m.sb("xn2T", [P, DC, PAIR])
        m0 = m.ps("misc0", [P, BANK])
        m1 = m.ps("misc1", [P, BANK])
        sc = m.ps("scores", [P, 2, BANK])
        tp = m.ps("transposed", [P, 2, BANK])
        ob = m.ps("out", [P, 2, BANK])

        loaded, ones, rounded = m.sem("weights_loaded"), m.sem("constants_set"), m.sem("mask_rounded")
        x_in, passed = m.sem("x_in"), m.sem("stats_passed")
        stats, meanvar, vareps, rstd_ok, xn_ok = (m.sem(n) for n in ("stats", "meanvar", "vareps", "rstd", "xn"))
        bias_ok, xnT_ps, xnT_ok, q_ps, kv_ps = (m.sem(n) for n in ("x_bias", "xnT_ps", "xnT", "q_ps", "kv_ps"))
        qT_ok, k_ok, v_ok = (m.sem(n) for n in ("qT", "k", "v"))
        s_ps, max_ok, shift_ok, exp_ok = (m.sem(n) for n in ("scores_ps", "max", "shifted", "exp"))
        pT_ps, pT_ok, o_ps = (m.sem(n) for n in ("weightsT_ps", "weightsT", "out_ps"))
        rc_ok, at_ok, aT_ps, aT_ok, wo_ps = (m.sem(n) for n in ("recip", "attn", "attnT_ps", "attnT", "wo_ps"))
        x1_ok, x1_out, stats2, meanvar2, vareps2 = (m.sem(n) for n in ("x1", "x1_out", "stats2", "meanvar2", "vareps2"))
        rstd2_ok, xn2_ok, x2T_ps, x2T_ok, x2T_out = (m.sem(n) for n in ("rstd2", "xn2", "xn2T_ps", "xn2T", "xn2T_out"))
        NS = H1 // 4

        def heads(ap):
            return ap.rearrange("p (h k) -> p h k", h=4)

        block = ctx.enter_context(nc.Block())

        @block.sync
        def _(sp):
            for dst, src in ((idn, ident), (msk, mask), (hmask, headmask), (wqkv, w_qkv), (bq, b_q),
                             (bk, b_k), (bv, b_v), (bo, b_o), (wo, w_o)):
                sp.dma_start(dst[:], src).then_inc(loaded, 16)
            with sp.Fori(0, NPAIR) as i:
                tok = sp.snap(i * PAIR)
                sp.wait_ge(bias_ok, i + 1)
                sp.dma_start(xt[:], x[bass.ds(tok, PAIR)]).then_inc(x_in, 16)
                sp.wait_ge(x1_ok, i + 1)
                sp.dma_start(x1[bass.ds(tok, PAIR)], x1t[:]).then_inc(x1_out, 16)
            sp.wait_ge(x1_out, 16 * (NPAIR + 1))
            sp.wait_ge(x2T_out, 16 * (NPAIR + 1))

        @block.gpsimd
        def _(pool):
            nc.gpsimd.memset(neghalf[:], -0.5).then_inc(ones, 1)
            nc.gpsimd.memset(vx[:], 1.0).then_inc(ones, 1)
            nc.gpsimd.memset(eps[:], EPS).then_inc(ones, 1)
            pool.nop().then_inc(bias_ok, 1)
            pool.wait_ge(ones, 3)
            pool.wait_ge(loaded, 16 * 9)
            with pool.Fori(0, NPAIR) as i:
                pool.wait_ge(meanvar, i + 1)
                nc.gpsimd.tensor_tensor(ve[:], mv[:, 1:2], eps[:], ALU.add).then_inc(vareps, 1)
                pool.wait_ge(vareps, i + 1)
                nc.gpsimd.tensor_tensor(rstd[:], ve[:], neghalf[:], ALU.pow).then_inc(rstd_ok, 1)
                pool.wait_ge(xn_ok, i + 1)
                nc.gpsimd.tensor_tensor(xb[:], xt[:], bo[:], ALU.add).then_inc(bias_ok, 1)
                pool.wait_ge(meanvar2, i + 1)
                nc.gpsimd.tensor_tensor(ve[:], mv[:, 1:2], eps[:], ALU.add).then_inc(vareps2, 1)
                pool.wait_ge(vareps2, i + 1)
                nc.gpsimd.tensor_tensor(rstd[:], ve[:], neghalf[:], ALU.pow).then_inc(rstd2_ok, 1)

        @block.scalar
        def _(act):
            act.wait_ge(loaded, 16 * 9)
            nc.scalar.activation(idn_r[:], idn[0:PAIR, 0:PAIR], ACT.Copy).then_inc(rounded, 1)
            nc.scalar.activation(msk_r[:], msk[:], ACT.Copy).then_inc(rounded, 1)
            act.nop().then_inc(x2T_out, 16)
            with act.Fori(0, NPAIR) as i:
                act.wait_ge(xnT_ps, i + 1)
                nc.scalar.activation(xnT[:].rearrange("p c t -> p (c t)"), m0[:, 0:4 * PAIR], ACT.Copy).then_inc(xnT_ok, 1)
                for s in range(NS):
                    act.wait_ge(shift_ok, i * NS + s + 1)
                    nc.scalar.activation(pe_[:, s % 2], p0[:, s % 2], ACT.Exp, scale=float(HD1) ** -0.5).then_inc(exp_ok, 1)
                    act.wait_ge(pT_ps, i * NS + s + 1)
                    nc.scalar.activation(pT[:, s % 2], heads(tp[0:PAIR, s % 2, 0:4 * PAIR]), ACT.Copy).then_inc(pT_ok, 1)
                act.wait_ge(aT_ps, i + 1)
                nc.scalar.activation(aT[:].rearrange("p c t -> p (c t)"), m0[:, 0:4 * PAIR], ACT.Copy).then_inc(aT_ok, 1)
                act.wait_ge(x2T_ps, i + 1)
                act.wait_ge(x2T_out, i * 16 + 16)
                nc.scalar.activation(x2T[:].rearrange("p c t -> p (c t)"), m0[:, 0:4 * PAIR], ACT.Copy).then_inc(x2T_ok, 1)
                act.wait_ge(x2T_ok, i + 1)
                act.dma_start(xn2T[:, :, bass.ds(i * PAIR, PAIR)], x2T[:]).then_inc(x2T_out, 16)

        @block.vector
        def _(dve):
            dve.wait_ge(loaded, 16 * 9)
            dve.wait_ge(ones, 3)
            dve.nop().then_inc(x1_out, 16)
            with dve.Fori(0, NPAIR) as i:
                dve.wait_ge(x_in, i * 16 + 16)
                nc.vector.bn_stats(stat[:], xt[:]).then_inc(stats, 1)
                dve.wait_ge(stats, i + 1)
                dve.nop().then_inc(passed, 1)
                nc.vector.bn_aggr(mv[:], stat[:]).then_inc(meanvar, 1)
                dve.wait_ge(rstd_ok, i + 1)
                nc.vector.tensor_scalar(xn[:], xt[:], mv[:, 0:1], rstd[:, 0:1], ALU.subtract, ALU.mult).then_inc(xn_ok, 1)
                dve.wait_ge(q_ps, i + 1)
                nc.vector.tensor_tensor(qT[:], m1[:, 0:4 * PAIR].rearrange("p (c t) -> p c t", c=DC),
                                        bq[:].unsqueeze(2).broadcast_to([P, DC, PAIR]), ALU.add).then_inc(qT_ok, 1)
                dve.wait_ge(kv_ps, i + 1)
                nc.vector.scalar_tensor_tensor(kbd[:], m0[:, 0:PAIR].unsqueeze(1).broadcast_to([P, HPC, PAIR]), bk[:, 0:1],
                                               hmask[:].unsqueeze(2).broadcast_to([P, HPC, PAIR]),
                                               ALU.add, ALU.mult).then_inc(k_ok, 1)
                nc.vector.tensor_tensor(vx[:, 0:HD1], m0[0:PAIR, PAIR:PAIR + HD1], bv[:], ALU.add).then_inc(v_ok, 1)
                for s in range(NS):
                    dve.wait_ge(s_ps, i * NS + s + 1)
                    sv = heads(sc[0:PAIR, s % 2, 0:4 * PAIR])
                    nc.vector.tensor_reduce(mx[:, s % 2], sv, AX_X, ALU.max).then_inc(max_ok, 1)
                    dve.wait_ge(max_ok, i * NS + s + 1)
                    if s >= 2:
                        dve.wait_ge(exp_ok, i * NS + s - 1)
                    nc.vector.tensor_tensor(p0[:, s % 2], sv, mx[:, s % 2].unsqueeze(2).broadcast_to([PAIR, 4, PAIR]),
                                            ALU.subtract).then_inc(shift_ok, 1)
                dve.wait_ge(o_ps, i * NS + NS)
                for h in range(2):
                    o = ob[0:PAIR, h, 0:16 * VX].rearrange("p (h v) -> p h v", h=16)
                    nc.vector.reciprocal(rc[:, h * 16:(h + 1) * 16], o[:, :, HD1]).then_inc(rc_ok, 1)
                dve.wait_ge(rc_ok, i * 2 + 2)
                for h in range(2):
                    o = ob[0:PAIR, h, 0:16 * VX].rearrange("p (h v) -> p h v", h=16)
                    nc.vector.tensor_tensor(at[:, h * 16:(h + 1) * 16], o[:, :, 0:HD1],
                                            rc[:, h * 16:(h + 1) * 16].unsqueeze(2).broadcast_to([PAIR, 16, HD1]),
                                            ALU.mult).then_inc(at_ok, 1)
                dve.wait_ge(wo_ps, i + 1)
                dve.wait_ge(bias_ok, i + 2)
                dve.wait_ge(x1_out, i * 16 + 16)
                nc.vector.tensor_tensor(x1t[:], m1[0:PAIR, :], xb[:], ALU.add).then_inc(x1_ok, 1)
                dve.wait_ge(x1_ok, i + 1)
                nc.vector.bn_stats(stat[:], x1t[:]).then_inc(stats2, 1)
                dve.wait_ge(stats2, i + 1)
                dve.nop().then_inc(passed, 1)
                nc.vector.bn_aggr(mv[:], stat[:]).then_inc(meanvar2, 1)
                dve.wait_ge(rstd2_ok, i + 1)
                nc.vector.tensor_scalar(xn2[:], x1t[:], mv[:, 0:1], rstd[:, 0:1], ALU.subtract, ALU.mult).then_inc(xn2_ok, 1)

        @block.tensor
        def _(pe):
            pe.wait_ge(loaded, 16 * 9)
            pe.wait_ge(rounded, 2)
            with pe.Fori(0, NPAIR) as i:
                pe.wait_ge(xn_ok, i + 1)
                for c in range(DC):
                    last = nc.tensor.transpose(m0[:, c * PAIR:(c + 1) * PAIR], xn[:, c * P:(c + 1) * P], idn[0:PAIR, 0:PAIR])
                last.then_inc(xnT_ps, 1)
                pe.wait_ge(xnT_ok, i + 1)
                for cc in range(DC):
                    for c in range(DC):
                        last = nc.tensor.matmul(m1[:, cc * PAIR:(cc + 1) * PAIR], wqkv[:, c, cc * P:(cc + 1) * P],
                                                xnT[:, c], start=(c == 0), stop=(c == DC - 1))
                last.then_inc(q_ps, 1)
                for c in range(DC):
                    nc.tensor.matmul(m0[:, 0:PAIR], wqkv[:, c, D:D + P], xnT[:, c], start=(c == 0), stop=(c == DC - 1))
                for c in range(DC):
                    last = nc.tensor.matmul(m0[0:PAIR, PAIR:PAIR + HD1], xnT[:, c], wqkv[:, c, D + P:NW],
                                            start=(c == 0), stop=(c == DC - 1))
                last.then_inc(kv_ps, 1)

                def scores(s):
                    if s == 0:
                        pe.wait_ge(qT_ok, i + 1)
                        pe.wait_ge(k_ok, i + 1)
                    if s >= 2:
                        pe.wait_ge(shift_ok, i * NS + s - 1)
                    out = sc[0:PAIR, s % 2, 0:4 * PAIR]
                    h = 4 * (s % 2)
                    nc.tensor.matmul(out, qT[:, s // 2], kbd[:, h:h + 4].rearrange("p h k -> p (h k)"), start=True, stop=False)
                    nc.tensor.matmul(out, idn_r[:], msk_r[:], start=False, stop=True).then_inc(s_ps, 1)

                def turn(s):
                    pe.wait_ge(exp_ok, i * NS + s + 1)
                    if s >= 2:
                        pe.wait_ge(pT_ok, i * NS + s - 1)
                    for h in range(4):
                        last = nc.tensor.transpose(tp[0:PAIR, s % 2, h * PAIR:(h + 1) * PAIR], pe_[:, s % 2, h],
                                                   idn[0:PAIR, 0:PAIR])
                    last.then_inc(pT_ps, 1)

                def weighted(s):
                    pe.wait_ge(pT_ok, i * NS + s + 1)
                    if s == 0:
                        pe.wait_ge(v_ok, i + 1)
                    for h in range(4):
                        o = (4 * s + h) % 16 * VX
                        last = nc.tensor.matmul(ob[0:PAIR, s // 4, o:o + VX], pT[:, s % 2, h], vx[:], start=True, stop=True)
                    last.then_inc(o_ps, 1)

                scores(0)
                for s in range(NS):
                    if s + 1 < NS:
                        scores(s + 1)
                    turn(s)
                    if s >= 1:
                        weighted(s - 1)
                weighted(NS - 1)
                pe.wait_ge(at_ok, i * 2 + 2)
                for c in range(DC):
                    last = nc.tensor.transpose(m0[:, c * PAIR:(c + 1) * PAIR],
                                               at[:, c * HPC:(c + 1) * HPC].rearrange("p h v -> p (h v)"),
                                               idn[0:PAIR, 0:PAIR])
                last.then_inc(aT_ps, 1)
                pe.wait_ge(aT_ok, i + 1)
                for c in range(DC):
                    last = nc.tensor.matmul(m1[0:PAIR, :], aT[:, c], wo[:, c], start=(c == 0), stop=(c == DC - 1))
                last.then_inc(wo_ps, 1)
                pe.wait_ge(xn2_ok, i + 1)
                for c in range(DC):
                    last = nc.tensor.transpose(m0[:, c * PAIR:(c + 1) * PAIR], xn2[:, c * P:(c + 1) * P], idn[0:PAIR, 0:PAIR])
                last.then_inc(x2T_ps, 1)
                pe.wait_ge(x2T_ok, i + 1)


def query_projection(nc, xn2T, w_q, qT_dram):
    with ExitStack() as ctx:
        m = Space(nc, ctx, "qp")
        HALF = NTOK // 2
        raw = m.sb("xn_raw", [P, DC, NTOK])
        xh = m.sb("xn_hi", [P, DC, NTOK], F32R)
        xl = m.sb("xn_lo", [P, DC, NTOK], F32R)
        wr = m.sb("w_raw", [P, 2, DC, P])
        wh = m.sb("w_hi", [P, 2, DC, P], F32R)
        wl = m.sb("w_lo", [P, 2, DC, P], F32R)
        st = m.sb("q_stage", [P, 2, NTOK])
        qb = m.ps("q", [P, 4, BANK])
        x_in, x_hi, x_lo = m.sem("xn_in"), m.sem("xn_hi"), m.sem("xn_lo")
        w_in = [m.sem(f"w_in{k}") for k in range(2)]
        w_hi, w_lo, q_ps, lo_half, hi_half = (m.sem(n) for n in ("w_hi", "w_lo", "q_ps", "left_staged", "right_staged"))
        stored = [m.sem(f"stored{k}") for k in range(2)]
        block = ctx.enter_context(nc.Block())

        @block.sync
        def _(sp):
            sp.dma_start(raw[:], xn2T).then_inc(x_in, 16)
            for k in range(2):
                sp.dma_start(wr[:, k], w_q[k]).then_inc(w_in[k], 16)
            with sp.Fori(0, H2 // 2 - 1) as i:
                for k in range(2):
                    sp.wait_ge(w_lo, i * 2 + k + 1)
                    sp.dma_start(wr[:, k], w_q[i * 2 + (k + 2)]).then_inc(w_in[k], 16)

        @block.gpsimd
        def _(pool):
            for c in range(DC):
                pool.wait_ge(x_hi, c + 1)
                nc.gpsimd.tensor_tensor(xl[:, c], raw[:, c], xh[:, c].bitcast(F32), ALU.subtract).then_inc(x_lo, 1)
            pool.nop().then_inc(q_ps, 2)
            with pool.Fori(0, H2 // 2) as i:
                for k in range(2):
                    pool.wait_ge(w_hi, i * 2 + k + 1)
                    pool.wait_ge(q_ps, i * 2 + k + 1)
                    nc.gpsimd.tensor_tensor(wl[:, k], wr[:, k], wh[:, k].bitcast(F32), ALU.subtract).then_inc(w_lo, 1)

        @block.scalar
        def _(act):
            act.wait_ge(x_in, 16)
            for k in range(2):
                act.nop().then_inc(hi_half, 1)
            for c in range(DC):
                nc.scalar.activation(xh[:, c], raw[:, c], ACT.Copy).then_inc(x_hi, 1)
            for k in range(2):
                act.wait_ge(w_in[k], 16)
                nc.scalar.activation(wh[:, k], wr[:, k], ACT.Copy).then_inc(w_hi, 1)

            def two_heads(i, more):
                for k in range(2):
                    act.wait_ge(q_ps, i * 2 + k + 3)
                    act.wait_ge(stored[k], i * 16 + 16)
                    nc.scalar.activation(st[:, k, HALF:NTOK], qb[:, 2 * k + 1, 0:HALF], ACT.Copy, scale=SCALE2).then_inc(hi_half, 1)
                    act.wait_ge(lo_half, i * 2 + k + 3)
                    act.wait_ge(hi_half, i * 2 + k + 3)
                    act.dma_start(qT_dram[:, i * 2 + k], st[:, k]).then_inc(stored[k], 16)
                    if more:
                        act.wait_ge(w_in[k], i * 16 + 32)
                        nc.scalar.activation(wh[:, k], wr[:, k], ACT.Copy).then_inc(w_hi, 1)

            with act.Fori(0, H2 // 2 - 1) as i:
                two_heads(i, True)
            two_heads(H2 // 2 - 1, False)
            for k in range(2):
                act.wait_ge(stored[k], 16 * (H2 // 2 + 1))

        @block.vector
        def _(dve):
            for k in range(2):
                dve.nop().then_inc(stored[k], 16)
                dve.nop().then_inc(lo_half, 1)
            with dve.Fori(0, H2 // 2) as i:
                for k in range(2):
                    dve.wait_ge(q_ps, i * 2 + k + 3)
                    dve.wait_ge(stored[k], i * 16 + 16)
                    nc.vector.tensor_scalar(st[:, k, 0:HALF], qb[:, 2 * k, 0:HALF], SCALE2, None, ALU.mult).then_inc(lo_half, 1)

        @block.tensor
        def _(pe):
            pe.wait_ge(x_lo, DC)
            with pe.Fori(0, H2 // 2) as i:
                for k in range(2):
                    pe.wait_ge(w_lo, i * 2 + k + 1)
                    pe.wait_ge(lo_half, i * 2 + k + 1)
                    pe.wait_ge(hi_half, i * 2 + k + 1)
                    for h in range(2):
                        cols = slice(h * HALF, (h + 1) * HALF)
                        for c in range(DC):
                            last = mm3(nc, qb[:, 2 * k + h, 0:HALF], (wh[:, k, c], wl[:, k, c]),
                                       (xh[:, c, cols], xl[:, c, cols]), start=(c == 0), stop=(c == DC - 1))
                    last.then_inc(q_ps, 1)


HPS = KVH // 2
NT = 4 * HPS
NS2 = NT * NG
KV = [s for g in range(NG) for s in
      [("K", g, j) for j in range(HPS)] + [("V", g, c) for c in range(3 * g, min(3 * g + 3, NCH) + (g == NG - 1))]]
NKV = len(KV)
K_DONE = KV.index(("K", NG - 1, HPS - 1)) + 1
GROUP_DONE = [max(n for n, s in enumerate(KV) if s[1] == g) + 1 for g in range(NG)]
LAG = 2


def score_steps(first, end):
    steps = []
    for n in range(first, end):
        steps.append([("S", n)])
        if n % NG == 0 and n > first:
            steps[-1].append(("F", n // NG - 1))
    steps[-1].append(("F", end // NG - 1))
    return steps


def value_steps(j, others):
    order, n = [], 0
    slots = NCH + LAG
    for m in range(slots):
        if m < NCH:
            order.append(("T", j, m))
        if m >= LAG:
            order.append(("PV", j, m - LAG))
        while n < len(others) and (n + 1) * slots <= (m + 1) * len(others) + slots:
            step = others[n]
            if step[0][0] == "KV" and KV[step[0][1]][0] == "V" and KV[step[0][1]][2] + LAG > m:
                break
            order += step
            n += 1
    for step in others[n:]:
        order += step
    order.append(("O", j))
    return order


PROJECT = [("KV", n) for n in range(NKV)]
SCORES_0 = [s for step in score_steps(0, NS2 // 2) for s in step]
VALUES_0 = value_steps(0, score_steps(NS2 // 2, NS2))
VALUES_1 = value_steps(1, [[s] for s in PROJECT])
VALUES_1_LAST = value_steps(1, [])


def need(eng, sem, unit, per, k):
    i, ahead = unit
    if isinstance(i, int):
        if (i + ahead) * per + k > 0:
            eng.wait_ge(sem, (i + ahead) * per + k)
    else:
        assert ahead * per + k > 0
        eng.wait_ge(sem, i * per + (ahead * per + k))


def cross_attention(nc, half, ident, ctx_dram, xn2T, qT_dram, w_k, w_v, oT_dram):
    with ExitStack() as stack:
        m = Space(nc, stack, f"ca{half}")
        WC = HPS * HD2
        HQ = HPS * GQ
        idn = m.sb("ident", [P, P])
        w_raw = m.sb("w_raw", [P, 2, DC, WC])
        w_hi = m.sb("w_hi", [P, 2, DC, WC], F32R)
        w_lo = m.sb("w_lo", [P, 2, DC, WC], F32R)
        craw = m.sb("ctx_raw", [P, 2, DC, GWMAX])
        chi = m.sb("ctx_hi", [P, 2, DC, GWMAX], F32R)
        clo = m.sb("ctx_lo", [P, 2, DC, GWMAX], F32R)
        qraw = m.sb("q_raw", [P, HQ * T])
        qhi = m.sb("q_hi", [P, HQ * T], F32R)
        qlo = m.sb("q_lo", [P, HQ * T], F32R)
        khi = m.sb("k_hi", [P, HPS, KEYS], F32R)
        klo = m.sb("k_lo", [P, HPS, KEYS], F32R)
        vhi = m.sb("v_hi", [P, NCH, WC], F32R)
        vlo = m.sb("v_lo", [P, NCH, WC], F32R)
        pr = m.sb("weights", [PAIR, NT, KEYS])
        ptl = m.sb("weightsT_lo", [P, 3, NQ], F32R)
        pth = m.sb("weightsT_hi", [P, 3, NQ], F32R)
        nmax = m.sb("neg_groupmax", [PAIR, NT, NG])
        nrow = m.sb("neg_rowmax", [PAIR, NT])
        gsum = m.sb("groupsum", [PAIR, NT, NG])
        corr = m.sb("correction", [PAIR, NT, NG])
        junk = m.sb("product", [PAIR, NT, NG])
        rsum = m.sb("rowsum", [PAIR, NT])
        rinv = m.sb("inv_rowsum", [PAIR, NT])
        fac = m.sb("factor", [PAIR, NT, NG])
        ost = m.sb("out_stage", [P, HPS, NQ])
        bank = m.ps("scores", [P, 4, BANK])
        tb = m.ps("turned", [P, 2, BANK])
        acc = m.ps("out", [P, HPS, BANK])

        w_in, w_hi_ok, w_lo_ok = m.sem("w_in"), m.sem("w_hi"), m.sem("w_lo")
        raw_in = [m.sem(f"ctx_in{r}") for r in range(2)]
        c_hi, c_lo, q_in, q_hi, q_lo = (m.sem(n) for n in ("ctx_hi", "ctx_lo", "q_in", "q_hi", "q_lo"))
        kv_ps, kv_hi, kv_lo = (m.sem(n) for n in ("kv_ps", "kv_hi", "kv_lo"))
        s_ps, gmax_ok, rmax_ok, exp_ok, corr_ok = (m.sem(n) for n in ("scores_ps", "groupmax", "rowmax", "exp", "correction"))
        sum_ok, inv_ok, fac_ok, p_ok = (m.sem(n) for n in ("rowsum", "inv_rowsum", "factor", "weights"))
        t_ps, t_hi, t_lo, pv_ok, o_ok = (m.sem(n) for n in ("turned_ps", "turned_hi", "turned_lo", "pv", "out_staged"))
        o_out = [m.sem(f"out_stored{j}") for j in range(HPS)]
        issue, go = m.sem("load_issued"), m.sem("copy_issued")

        def chunk_of(c):
            g = min(c // 3, NG - 1)
            return g % 2, (c - 3 * g) * P

        block = stack.enter_context(nc.Block())

        @block.sync
        def _(sp):
            sp.dma_start(idn[:], ident).then_inc(w_in, 16)
            sp.dma_start(w_raw[:, 0], w_k[:, :, half * WC:(half + 1) * WC]).then_inc(w_in, 16)
            sp.dma_start(w_raw[:, 1], w_v[:, :, half * WC:(half + 1) * WC]).then_inc(w_in, 16)

            def load(i):
                unit = (i, 0)
                for g in range(NG):
                    if g == 0:
                        need(sp, q_lo, unit, 1, 1)
                        sp.nop().then_inc(issue, 1)
                        sp.dma_start(qraw[:].rearrange("p (h t) -> p h t", h=HQ),
                                     qT_dram[:, half * HQ:(half + 1) * HQ, bass.ds(i * T, T)]).then_inc(q_in, 16)
                    need(sp, c_lo, unit, NG, g + 1)
                    sp.nop().then_inc(issue, 1)
                    w = min(GW[g], S_CTX - g * GROUP)
                    sp.dma_start(craw[:, g % 2, :, 0:w], ctx_dram[i, :, :, g * GROUP:g * GROUP + w]).then_inc(raw_in[g % 2], 16)
                    if g == NG - 1:
                        sp.dma_start(craw[:, g % 2, :, w:w + T], xn2T[:, :, bass.ds(i * T, T)]).then_inc(raw_in[g % 2], 16)

            with sp.Fori(0, NB) as i:
                load(i)

        @block.gpsimd
        def _(pool):
            for k in range(2):
                pool.nop().then_inc(c_lo, 1)
            pool.nop().then_inc(q_lo, 1)
            pool.wait_ge(w_hi_ok, 2)
            for k in range(2):
                nc.gpsimd.tensor_tensor(w_lo[:, k], w_raw[:, k], w_hi[:, k].bitcast(F32), ALU.subtract).then_inc(w_lo_ok, 1)

            def split_queries(unit):
                need(pool, q_in, unit, 16, 16)
                need(pool, s_ps, unit, NS2, 0)
                pool.nop().then_inc(go, 1)
                nc.gpsimd.tensor_copy(qhi[:], qraw[:]).then_inc(q_hi, 1)
                need(pool, q_hi, unit, 1, 1)
                nc.gpsimd.tensor_tensor(qlo[:], qraw[:], qhi[:].bitcast(F32), ALU.subtract).then_inc(q_lo, 1)

            def split_group(unit, g):
                w, r = GW[g], g % 2
                need(pool, raw_in[r], unit, 32 + 16 * r, 16 * (g // 2 + 1) + 16 * (g == NG - 1))
                need(pool, kv_ps, unit, NKV, GROUP_DONE[g - 2] if g >= 2 else GROUP_DONE[g + 2] - NKV)
                pool.nop().then_inc(go, 1)
                nc.gpsimd.tensor_copy(chi[:, r, :, 0:w], craw[:, r, :, 0:w]).then_inc(c_hi, 1)
                need(pool, c_hi, unit, NG, g + 1)
                nc.gpsimd.tensor_tensor(clo[:, r, :, 0:w], craw[:, r, :, 0:w], chi[:, r, :, 0:w].bitcast(F32),
                                        ALU.subtract).then_inc(c_lo, 1)

            def scale(unit, k):
                need(pool, fac_ok, unit, NT, k + 1)
                a = pr[:, k, 0:3 * GROUP].rearrange("p (g w) -> p g w", g=3)
                nc.gpsimd.tensor_tensor(a, a, fac[:, k, 0:3].unsqueeze(2).broadcast_to([PAIR, 3, GROUP]), ALU.mult)
                b = pr[:, k, 3 * GROUP:KEYS]
                nc.gpsimd.tensor_tensor(b, b, fac[:, k, 3:4].broadcast_to([PAIR, GW[3]]), ALU.mult).then_inc(p_ok, 1)

            split_queries((0, 0))
            for g in range(NG):
                split_group((0, 0), g)

            def sequence(i, more):
                for k in range(NT):
                    scale((i, 0), k)
                    if more and k in (3, 4):
                        split_group((i, 1), k - 3)
                if more:
                    split_queries((i, 1))
                    for g in range(2, NG):
                        split_group((i, 1), g)

            with pool.Fori(0, NB - 1) as i:
                sequence(i, True)
            sequence(NB - 1, False)

        @block.scalar
        def _(act):
            for j in range(HPS):
                act.nop().then_inc(o_ok, 1)
                act.nop().then_inc(o_out[j], 16)
            act.wait_ge(w_in, 48)
            for k in range(2):
                nc.scalar.activation(w_hi[:, k], w_raw[:, k], ACT.Copy).then_inc(w_hi_ok, 1)

            def run(order, i):
                for step in order:
                    if step[0] == "S":
                        n, unit = step[1], (i, 0)
                        k, g = n // NG, n % NG
                        need(act, gmax_ok, unit, NS2, n + 1)
                        nc.scalar.activation(pr[:, k, g * GROUP:g * GROUP + GW[g]], bank[0:PAIR, g, 0:GW[g]], ACT.Exp,
                                             bias=nmax[:, k, g:g + 1], accum_out=gsum[:, k, g:g + 1]).then_inc(exp_ok, 1)
                        if g == NG - 1:
                            need(act, rmax_ok, unit, NT, k + 1)
                            nc.scalar.activation(corr[:, k], nmax[:, k], ACT.Exp, bias=nrow[:, k:k + 1],
                                                 scale=-1.0).then_inc(corr_ok, 1)
                    elif step[0] == "T":
                        _, j, c = step
                        need(act, t_ps, (i, 0), 2 * NCH, NCH * j + c + 1)
                        nc.scalar.activation(pth[0:CW[c], c % 3, :], tb[0:CW[c], (NCH * j + c) % 2, 0:NQ],
                                             ACT.Copy).then_inc(t_hi, 1)
                    elif step[0] == "KV":
                        unit = (i, 1)
                        need(act, kv_ps, unit, NKV, step[1] + 1)
                        kind, g, x = KV[step[1]]
                        b = step[1] % 4
                        if kind == "K":
                            nc.scalar.activation(khi[:, x, g * GROUP:g * GROUP + GW[g]], bank[:, b, 0:GW[g]], ACT.Copy).then_inc(kv_hi, 1)
                        else:
                            nc.scalar.activation(vhi[0:CW[x], x], bank[0:CW[x], b, 0:WC], ACT.Copy).then_inc(kv_hi, 1)
                    elif step[0] == "O":
                        j = step[1]
                        need(act, pv_ok, (i, 0), 2 * NCH, NCH * (j + 1))
                        need(act, o_out[j], (i, 0), 16, 16)
                        nc.scalar.activation(ost[:, j], acc[:, j, 0:NQ], ACT.Copy).then_inc(o_ok, 1)
                        need(act, o_ok, (i, 0), HPS, HPS + j + 1)
                        act.dma_start(oT_dram[:, half * HQ + j * GQ:half * HQ + (j + 1) * GQ, bass.ds(i * T, T)],
                                      ost[:, j].rearrange("p (h t) -> p h t", h=GQ)).then_inc(o_out[j], 16)

            run(PROJECT, -1)
            with act.Fori(0, NB - 1) as i:
                run(SCORES_0, i)
                run(VALUES_0, i)
                run(VALUES_1, i)
            run(SCORES_0, NB - 1)
            run(VALUES_0, NB - 1)
            run(VALUES_1_LAST, NB - 1)
            for j in range(HPS):
                act.wait_ge(o_out[j], 16 * (NB + 1))

        @block.vector
        def _(dve):
            for k in range(2):
                dve.nop().then_inc(t_lo, 1)

            def run(order, i):
                for step in order:
                    if step[0] == "S":
                        n, unit = step[1], (i, 0)
                        k, g = n // NG, n % NG
                        need(dve, s_ps, unit, NS2, n + 1)
                        nc.vector.tensor_reduce(nmax[:, k, g:g + 1], bank[0:PAIR, g, 0:GW[g]], AX_X, ALU.max,
                                                negate=True).then_inc(gmax_ok, 1)
                        if g == NG - 1:
                            need(dve, gmax_ok, unit, NS2, n + 1)
                            nc.vector.tensor_reduce(nrow[:, k:k + 1], nmax[:, k], AX_X, ALU.min).then_inc(rmax_ok, 1)
                    elif step[0] == "F":
                        k, unit = step[1], (i, 0)
                        need(dve, corr_ok, unit, NT, k + 1)
                        nc.vector.tensor_tensor_reduce(junk[:, k], gsum[:, k], corr[:, k], 1.0, 0.0, ALU.mult, ALU.add,
                                                       rsum[:, k:k + 1]).then_inc(sum_ok, 1)
                        need(dve, sum_ok, unit, NT, k + 1)
                        nc.vector.reciprocal(rinv[:, k:k + 1], rsum[:, k:k + 1]).then_inc(inv_ok, 1)
                        need(dve, inv_ok, unit, NT, k + 1)
                        nc.vector.tensor_scalar(fac[:, k], corr[:, k], rinv[:, k:k + 1], None, ALU.mult).then_inc(fac_ok, 1)
                    elif step[0] == "T":
                        _, j, c = step
                        need(dve, t_hi, (i, 0), 2 * NCH, NCH * j + c + 1)
                        nc.vector.tensor_tensor(ptl[0:CW[c], c % 3, :], tb[0:CW[c], (NCH * j + c) % 2, 0:NQ],
                                                pth[0:CW[c], c % 3, :].bitcast(F32), ALU.subtract).then_inc(t_lo, 1)
                    elif step[0] == "KV":
                        need(dve, kv_hi, (i, 1), NKV, step[1] + 1)
                        kind, g, x = KV[step[1]]
                        b = step[1] % 4
                        if kind == "K":
                            s = slice(g * GROUP, g * GROUP + GW[g])
                            nc.vector.tensor_tensor(klo[:, x, s], bank[:, b, 0:GW[g]], khi[:, x, s].bitcast(F32),
                                                    ALU.subtract).then_inc(kv_lo, 1)
                        else:
                            nc.vector.tensor_tensor(vlo[0:CW[x], x], bank[0:CW[x], b, 0:WC], vhi[0:CW[x], x].bitcast(F32),
                                                    ALU.subtract).then_inc(kv_lo, 1)

            run(PROJECT, -1)
            with dve.Fori(0, NB - 1) as i:
                run(SCORES_0, i)
                run(VALUES_0, i)
                run(VALUES_1, i)
            run(SCORES_0, NB - 1)
            run(VALUES_0, NB - 1)
            run(VALUES_1_LAST, NB - 1)

        @block.tensor
        def _(pe):
            pe.wait_ge(w_lo_ok, 2)

            def run(order, i):
                for step in order:
                    if step[0] == "S":
                        n, unit = step[1], (i, 0)
                        k, g = n // NG, n % NG
                        if n == 0:
                            need(pe, q_lo, unit, 1, 2)
                            need(pe, kv_lo, unit, NKV, K_DONE)
                        if n < 4:
                            need(pe, kv_lo, unit, NKV, max(x for x in range(NKV) if x % 4 == n) + 1)
                        else:
                            need(pe, exp_ok, unit, NS2, n - 3)
                        j, cols = k // 4, slice(k * PAIR, (k + 1) * PAIR)
                        s = slice(g * GROUP, g * GROUP + GW[g])
                        mm3(nc, bank[0:PAIR, g, 0:GW[g]], (qhi[:, cols], qlo[:, cols]), (khi[:, j, s], klo[:, j, s]),
                            True, True).then_inc(s_ps, 1)
                    elif step[0] == "T":
                        _, j, c = step
                        if c == 0:
                            need(pe, p_ok, (i, 0), NT, 4 * (j + 1))
                        need(pe, t_lo, (i, 0), 2 * NCH, NCH * j + c + 1)
                        for q in range(4):
                            last = nc.tensor.transpose(tb[0:CW[c], (NCH * j + c) % 2, q * PAIR:(q + 1) * PAIR],
                                                       pr[:, 4 * j + q, c * P:c * P + CW[c]], idn[0:PAIR, 0:PAIR])
                        last.then_inc(t_ps, 1)
                    elif step[0] == "PV":
                        _, j, c = step
                        if c == 0:
                            need(pe, kv_lo, (i, 0), NKV, NKV)
                            need(pe, o_ok, (i, 0), HPS, j + 1)
                        need(pe, t_lo, (i, 0), 2 * NCH, NCH * j + c + 3)
                        w, s = CW[c], slice(j * HD2, (j + 1) * HD2)
                        mm3(nc, acc[:, j, 0:NQ], (vhi[0:w, c, s], vlo[0:w, c, s]), (pth[0:w, c % 3], ptl[0:w, c % 3]),
                            c == 0, c == NCH - 1).then_inc(pv_ok, 1)
                    elif step[0] == "KV":
                        n, unit = step[1], (i, 1)
                        if n < 4:
                            need(pe, exp_ok, unit, NS2, n - 3)
                        else:
                            need(pe, kv_lo, unit, NKV, n - 3)
                        kind, g, x = KV[n]
                        if (kind, x) == ("K", 0):
                            need(pe, c_lo, unit, NG, g + 3)
                        for c in range(DC):
                            st, sp_ = c == 0, c == DC - 1
                            if kind == "K":
                                s = slice(x * HD2, (x + 1) * HD2)
                                last = mm3(nc, bank[:, n % 4, 0:GW[g]], (w_hi[:, 0, c, s], w_lo[:, 0, c, s]),
                                           (chi[:, g % 2, c, 0:GW[g]], clo[:, g % 2, c, 0:GW[g]]), st, sp_)
                            else:
                                o = (x - 3 * g) * P
                                s = slice(o, o + CW[x])
                                last = mm3(nc, bank[0:CW[x], n % 4, 0:WC], (chi[:, g % 2, c, s], clo[:, g % 2, c, s]),
                                           (w_hi[:, 1, c], w_lo[:, 1, c]), st, sp_)
                        last.then_inc(kv_ps, 1)

            run(PROJECT, -1)
            with pe.Fori(0, NB - 1) as i:
                run(SCORES_0, i)
                run(VALUES_0, i)
                run(VALUES_1, i)
            run(SCORES_0, NB - 1)
            run(VALUES_0, NB - 1)
            run(VALUES_1_LAST, NB - 1)


def output_and_experts(nc, ident, x1, oT_dram, w_o, w_er, w_eb, out):
    with ExitStack() as ctx:
        m = Space(nc, ctx, "oe")
        NTT = NTOK // P
        KR = NE * RANK
        KC = KR // P
        NR = KR + NE
        idn = m.sb("ident", [P, P])
        zero = m.sb("zero", [P, D], F32R)
        wr = m.sb("wo_raw", [P, 2, D])
        wh = m.sb("wo_hi", [P, 2, D], F32R)
        wl = m.sb("wo_lo", [P, 2, D], F32R)
        orw = m.sb("o_raw", [P, 2, NTOK])
        oh = m.sb("o_hi", [P, 2, NTOK], F32R)
        ol = m.sb("o_lo", [P, 2, NTOK], F32R)
        er = m.sb("er_raw", [P, DC, NR])
        erh = m.sb("er_hi", [P, DC, NR], F32R)
        erl = m.sb("er_lo", [P, DC, NR], F32R)
        eb = m.sb("eb_raw", [P, KC, D])
        ebh = m.sb("eb_hi", [P, KC, D], F32R)
        ebl = m.sb("eb_lo", [P, KC, D], F32R)
        x2 = m.sb("x2", [P, NTT, D])
        xt = m.sb("x2_tile", [P, D])
        neghalf, eps = m.sb("neghalf", [P, 1]), m.sb("eps", [P, 1])
        stat, mv, ve, rstd = m.sb("stat", [P, 6]), m.sb("meanvar", [P, 2]), m.sb("var_eps", [P, 1]), m.sb("rstd", [P, 1])
        xn = m.sb("xn", [P, D])
        xh = m.sb("xnT_hi", [P, DC, P], F32R)
        xl = m.sb("xnT_lo", [P, DC, P], F32R)
        rs = m.sb("router", [P, NE])
        top = m.sb("top", [P, 2, 8])
        rest = m.sb("rest", [P, 2, NE])
        ntop = m.sb("neg_top", [P, 1])
        ex = m.sb("exp", [P, NE])
        chosen = m.sb("chosen", [P, NE])
        gate0, gsum, ginv = m.sb("gate0", [P, NE]), m.sb("gatesum", [P, 1]), m.sb("gateinv", [P, 1])
        gate = m.sb("gate", [P, NE])
        hg = m.sb("gated", [P, NE, RANK])
        gh = m.sb("gatedT_hi", [P, KC, P], F32R)
        gl = m.sb("gatedT_lo", [P, KC, P], F32R)
        res = m.sb("result", [P, D])
        ps = m.ps("ps", [P, 8, BANK])

        x_in, e_in, x2_ok = (m.sem(n) for n in ("x1_in", "experts_in", "x2"))
        w_in = [m.sem(f"wo_in{k}") for k in range(2)]
        w_hi, w_lo, o_lo, head_ok, acc_ok = (m.sem(n) for n in ("wo_hi", "wo_lo", "o_lo", "head", "accumulated"))
        zero_ok, load_go = m.sem("zeros_set"), m.sem("load_issued")
        e_hi, e_lo = m.sem("experts_hi"), m.sem("experts_lo")
        t_in, stats, passed, meanvar, vareps, rstd_ok, xn_ok = (m.sem(n) for n in (
            "tile_in", "stats", "stats_passed", "meanvar", "vareps", "rstd", "xn"))
        xt_ps, xt_hi, xt_lo, r_ps, h_ps, r_ok = (m.sem(n) for n in ("xnT_ps", "xnT_hi", "xnT_lo", "router_ps", "h_ps", "router"))
        top1, rest1, top2, rest2, go = (m.sem(n) for n in ("top1", "rest1", "top2", "rest2", "max_passed"))
        ntop_ok, ex_ok, chosen_ok, sum_ok, inv_ok, gate_ok, hg_ok = (m.sem(n) for n in (
            "negtop", "exp", "chosen", "gatesum", "gateinv", "gate", "gated"))
        gt_ps, gt_hi, gt_lo, y_ps, res_ok, stored = (m.sem(n) for n in (
            "gatedT_ps", "gatedT_hi", "gatedT_lo", "y_ps", "result", "stored"))
        out_rows = out.rearrange("b t d -> (b t) d")

        block = ctx.enter_context(nc.Block())

        @block.sync
        def _(sp):
            for k in range(2):
                sp.dma_start(wr[:, k], w_o[k]).then_inc(w_in[k], 16)
                sp.dma_start(orw[:, k], oT_dram[:, k]).then_inc(w_in[k], 16)
            sp.dma_start(idn[:], ident).then_inc(e_in, 16)
            sp.dma_start(er[:], w_er).then_inc(e_in, 16)
            sp.dma_start(eb[:], w_eb).then_inc(e_in, 16)
            sp.dma_start(x2[:], x1.rearrange("(n p) d -> p n d", p=P)).then_inc(x_in, 16)
            with sp.Fori(0, H2 // 2 - 1) as i:
                for k in range(2):
                    sp.wait_ge(w_lo, i * 2 + k + 1)
                    sp.wait_ge(o_lo, i * 2 + k + 1)
                    sp.dma_start(wr[:, k], w_o[i * 2 + (k + 2)]).then_inc(w_in[k], 16)
                    sp.dma_start(orw[:, k], oT_dram[:, i * 2 + (k + 2)]).then_inc(w_in[k], 16)
            sp.wait_ge(x2_ok, NTT)
            with sp.Fori(0, NTT) as i:
                sp.wait_ge(res_ok, i + 1)
                sp.nop().then_inc(load_go, 1)
                sp.dma_start(xt[:], x2[:, i]).then_inc(t_in, 16)
                sp.wait_ge(res_ok, i + 2)
                sp.nop().then_inc(load_go, 1)
                sp.dma_start(out_rows[bass.ds(i * P, P)], res[:]).then_inc(stored, 16)
            sp.wait_ge(stored, 16 * (NTT + 1))

        @block.gpsimd
        def _(pool):
            nc.gpsimd.memset(zero[:].bitcast(F32), 0.0).then_inc(zero_ok, 1)
            nc.gpsimd.memset(neghalf[:], -0.5)
            nc.gpsimd.memset(eps[:], EPS)
            with pool.Fori(0, H2 // 2) as i:
                for k in range(2):
                    pool.wait_ge(w_hi, i * 4 + (2 * k + 1))
                    nc.gpsimd.tensor_tensor(wl[:, k], wr[:, k], wh[:, k].bitcast(F32), ALU.subtract).then_inc(w_lo, 1)
            for c in range(DC):
                pool.wait_ge(e_hi, c + 1)
                nc.gpsimd.tensor_tensor(erl[:, c], er[:, c], erh[:, c].bitcast(F32), ALU.subtract).then_inc(e_lo, 1)
            for c in range(KC):
                pool.wait_ge(e_hi, DC + c + 1)
                nc.gpsimd.tensor_tensor(ebl[:, c], eb[:, c], ebh[:, c].bitcast(F32), ALU.subtract).then_inc(e_lo, 1)
            with pool.Fori(0, NTT) as i:
                pool.wait_ge(meanvar, i + 1)
                nc.gpsimd.tensor_tensor(ve[:], mv[:, 1:2], eps[:], ALU.add).then_inc(vareps, 1)
                pool.wait_ge(vareps, i + 1)
                nc.gpsimd.tensor_tensor(rstd[:], ve[:], neghalf[:], ALU.pow).then_inc(rstd_ok, 1)

        @block.scalar
        def _(act):
            with act.Fori(0, H2 // 2) as i:
                for k in range(2):
                    act.wait_ge(w_in[k], i * 32 + 32)
                    act.wait_ge(head_ok, i * 2 + k + 1)
                    nc.scalar.activation(wh[:, k], wr[:, k], ACT.Copy).then_inc(w_hi, 1)
                    nc.scalar.activation(oh[:, k], orw[:, k], ACT.Copy).then_inc(w_hi, 1)
            act.wait_ge(e_in, 48)
            for c in range(DC):
                nc.scalar.activation(erh[:, c], er[:, c], ACT.Copy).then_inc(e_hi, 1)
            for c in range(KC):
                nc.scalar.activation(ebh[:, c], eb[:, c], ACT.Copy).then_inc(e_hi, 1)
            with act.Fori(0, NTT) as i:
                act.wait_ge(xt_ps, i + 1)
                nc.scalar.activation(xh[:].rearrange("p c t -> p (c t)"), ps[:, 0], ACT.Copy).then_inc(xt_hi, 1)
                act.wait_ge(r_ps, i + 1)
                nc.scalar.activation(rs[:], ps[:, 3, 0:NE], ACT.Copy).then_inc(r_ok, 1)
                act.wait_ge(ntop_ok, i + 1)
                act.wait_ge(r_ok, i + 1)
                nc.scalar.activation(ex[:], rs[:], ACT.Exp, bias=ntop[:, 0:1]).then_inc(ex_ok, 1)
                for h in range(2):
                    act.wait_ge(gt_ps, i * 2 + h + 1)
                    nc.scalar.activation(gh[:, 4 * h:4 * h + 4].rearrange("p c t -> p (c t)"), ps[:, 4 + h], ACT.Copy).then_inc(gt_hi, 1)

        @block.vector
        def _(dve):
            dve.nop().then_inc(res_ok, 1)
            with dve.Fori(0, H2 // 2) as i:
                for k in range(2):
                    dve.wait_ge(w_hi, i * 4 + (2 * k + 2))
                    nc.vector.tensor_tensor(ol[:, k], orw[:, k], oh[:, k].bitcast(F32), ALU.subtract).then_inc(o_lo, 1)
            dve.wait_ge(x_in, 16)
            dve.wait_ge(acc_ok, 1)
            for t in range(NTT):
                nc.vector.tensor_tensor(x2[:, t], ps[:, t], x2[:, t], ALU.add).then_inc(x2_ok, 1)
            dve.wait_ge(e_lo, DC + KC)
            with dve.Fori(0, NTT) as i:
                dve.wait_ge(t_in, i * 16 + 16)
                nc.vector.bn_stats(stat[:], xt[:]).then_inc(stats, 1)
                dve.wait_ge(stats, i + 1)
                dve.nop().then_inc(passed, 1)
                nc.vector.bn_aggr(mv[:], stat[:]).then_inc(meanvar, 1)
                dve.wait_ge(rstd_ok, i + 1)
                nc.vector.tensor_scalar(xn[:], xt[:], mv[:, 0:1], rstd[:, 0:1], ALU.subtract, ALU.mult).then_inc(xn_ok, 1)
                dve.wait_ge(xt_hi, i + 1)
                nc.vector.tensor_tensor(xl[:].rearrange("p c t -> p (c t)"), ps[:, 0],
                                        xh[:].rearrange("p c t -> p (c t)").bitcast(F32), ALU.subtract).then_inc(xt_lo, 1)
                dve.wait_ge(r_ok, i + 1)
                dve.nop().then_inc(go, 1)
                nc.vector.max(top[:, 0], rs[:]).then_inc(top1, 1)
                dve.wait_ge(top1, i + 1)
                nc.vector.tensor_scalar(ntop[:], top[:, 0, 0:1], -1.0, None, ALU.mult).then_inc(ntop_ok, 1)
                nc.vector.match_replace(rest[:, 0], top[:, 0], rs[:], LOWEST).then_inc(rest1, 1)
                dve.wait_ge(rest1, i + 1)
                dve.nop().then_inc(go, 1)
                nc.vector.max(top[:, 1], rest[:, 0]).then_inc(top2, 1)
                dve.wait_ge(top2, i + 1)
                dve.nop().then_inc(go, 1)
                nc.vector.match_replace(rest[:, 1], top[:, 1], rest[:, 0], LOWEST).then_inc(rest2, 1)
                dve.wait_ge(rest2, i + 1)
                nc.vector.tensor_tensor(chosen[:], rest[:, 1], rs[:], ALU.not_equal).then_inc(chosen_ok, 1)
                dve.wait_ge(chosen_ok, i + 1)
                dve.wait_ge(ex_ok, i + 1)
                nc.vector.tensor_tensor_reduce(gate0[:], ex[:], chosen[:], 1.0, 0.0, ALU.mult, ALU.add, gsum[:]).then_inc(sum_ok, 1)
                dve.wait_ge(sum_ok, i + 1)
                nc.vector.reciprocal(ginv[:], gsum[:]).then_inc(inv_ok, 1)
                dve.wait_ge(inv_ok, i + 1)
                nc.vector.tensor_scalar(gate[:], gate0[:], ginv[:, 0:1], SCALING, ALU.mult, ALU.mult).then_inc(gate_ok, 1)
                dve.wait_ge(gate_ok, i + 1)
                for h in range(2):
                    dve.wait_ge(h_ps, i * 2 + h + 1)
                    e = slice(h * NE // 2, (h + 1) * NE // 2)
                    nc.vector.tensor_tensor(hg[:, e], ps[:, 1 + h].rearrange("p (e r) -> p e r", r=RANK),
                                            gate[:, e].unsqueeze(2).broadcast_to([P, NE // 2, RANK]), ALU.mult).then_inc(hg_ok, 1)
                for h in range(2):
                    dve.wait_ge(gt_hi, i * 2 + h + 1)
                    nc.vector.tensor_tensor(gl[:, 4 * h:4 * h + 4].rearrange("p c t -> p (c t)"), ps[:, 4 + h],
                                            gh[:, 4 * h:4 * h + 4].rearrange("p c t -> p (c t)").bitcast(F32),
                                            ALU.subtract).then_inc(gt_lo, 1)
                dve.wait_ge(y_ps, i + 1)
                dve.wait_ge(stored, i * 16 + 16)
                nc.vector.tensor_tensor(res[:], ps[:, 6], xt[:], ALU.add).then_inc(res_ok, 1)

        @block.tensor
        def _(pe):
            for _ in range(2):
                pe.nop().then_inc(head_ok, 1)
            pe.nop().then_inc(stored, 16)
            pe.wait_ge(zero_ok, 1)
            for t in range(NTT):
                nc.tensor.matmul(ps[:, t], zero[:, 0:P], zero[:], start=True, stop=False)
            with pe.Fori(0, H2 // 2) as i:
                for k in range(2):
                    pe.wait_ge(w_lo, i * 2 + k + 1)
                    pe.wait_ge(o_lo, i * 2 + k + 1)
                    for t in range(NTT):
                        s = slice(t * P, (t + 1) * P)
                        last = mm3(nc, ps[:, t], (oh[:, k, s], ol[:, k, s]), (wh[:, k], wl[:, k]), False, False)
                    last.then_inc(head_ok, 1)
            for t in range(NTT):
                last = nc.tensor.matmul(ps[:, t], zero[:, 0:P], zero[:], start=False, stop=True)
            last.then_inc(acc_ok, 1)
            pe.wait_ge(e_in, 48)
            pe.wait_ge(x2_ok, NTT)
            pe.wait_ge(e_lo, DC + KC)
            with pe.Fori(0, NTT) as i:
                pe.wait_ge(xn_ok, i + 1)
                for c in range(DC):
                    last = nc.tensor.transpose(ps[:, 0, c * P:(c + 1) * P], xn[:, c * P:(c + 1) * P], idn[:])
                last.then_inc(xt_ps, 1)
                pe.wait_ge(xt_lo, i + 1)
                for c in range(DC):
                    last = mm3(nc, ps[:, 3, 0:NE], (xh[:, c], xl[:, c]), (erh[:, c, KR:NR], erl[:, c, KR:NR]), c == 0, c == DC - 1)
                last.then_inc(r_ps, 1)
                for h in range(2):
                    s = slice(h * KR // 2, (h + 1) * KR // 2)
                    for c in range(DC):
                        last = mm3(nc, ps[:, 1 + h], (xh[:, c], xl[:, c]), (erh[:, c, s], erl[:, c, s]), c == 0, c == DC - 1)
                    last.then_inc(h_ps, 1)
                for h in range(2):
                    pe.wait_ge(hg_ok, i * 2 + h + 1)
                    for c in range(4):
                        e = (4 * h + c) * (P // RANK)
                        last = nc.tensor.transpose(ps[:, 4 + h, c * P:(c + 1) * P],
                                                   hg[:, e:e + P // RANK].rearrange("p e r -> p (e r)"), idn[:])
                    last.then_inc(gt_ps, 1)
                pe.wait_ge(gt_lo, i * 2 + 2)
                for c in range(KC):
                    last = mm3(nc, ps[:, 6], (gh[:, c], gl[:, c]), (ebh[:, c], ebl[:, c]), c == 0, c == KC - 1)
                last.then_inc(y_ps, 1)


def build(nc, x, mats, out):
    self_attention(nc, x, mats["ident"], mats["mask"], mats["headmask"], mats["w_qkv"], mats["b_q"], mats["b_k"],
                   mats["b_v"], mats["w_o"], mats["b_o"], mats["x1"], mats["xn2T"])
    query_projection(nc, mats["xn2T"], mats["w_q"], mats["qT"])
    for half in range(2):
        cross_attention(nc, half, mats["ident"], mats["ctx"], mats["xn2T"], mats["qT"], mats["w_k"], mats["w_v"], mats["oT"])
    output_and_experts(nc, mats["ident"], mats["x1"], mats["oT"], mats["w_o2"], mats["w_er"], mats["w_eb"], out)


def kernel(**inputs):
    import numpy as np
    import concourse.bacc as bacc
    from concourse.bass_utils import run_bass_kernel_spmd as run

    a = {k: np.asarray(v) for k, v in inputs.items()}

    def rows(w):
        return np.ascontiguousarray(w.reshape(-1, P, w.shape[1]).transpose(1, 0, 2))

    t = np.arange(PAIR)
    allowed = (t[:, None] // T == t[None] // T) & (t[:, None] >= t[None])
    lay = {
        "x": a["x"].reshape(NTOK, D),
        "ident": np.eye(P, dtype=np.float32),
        "mask": np.tile(np.where(allowed, 0.0, NEG).astype(np.float32), (1, 4)),
        "headmask": np.repeat(np.eye(HPC, dtype=np.float32), HD1, 0),
        "w_qkv": rows(np.concatenate([a["L0_attn_wq_w"].T, np.tile(a["L0_attn_wk_w"].T, (1, HPC)), a["L0_attn_wv_w"].T], 1)),
        "b_q": a["L0_attn_wq_b"].reshape(DC, P).T,
        "b_k": np.tile(a["L0_attn_wk_b"], HPC).reshape(P, 1),
        "b_v": np.tile(a["L0_attn_wv_b"], (PAIR, 1)),
        "w_o": rows(a["L0_attn_wo_w"].T),
        "b_o": np.tile(a["L0_attn_wo_b"], (PAIR, 1)),
        "w_q": a["L0_xattn_Wq"].reshape(DC, P, H2, HD2).transpose(2, 1, 0, 3),
        "w_k": rows(a["L0_xattn_Wk"]),
        "w_v": rows(a["L0_xattn_Wv"]),
        "w_o2": a["L0_xattn_Wo"].reshape(H2, HD2, D),
        "ctx": a["ctx_4096"].reshape(NB, S_CTX, DC, P).transpose(0, 3, 2, 1),
        "w_er": rows(np.concatenate([a["L0_ffn_A"].reshape(NE * RANK, D).T, a["L0_ffn_Wr"].T], 1)),
        "w_eb": rows(a["L0_ffn_B"].transpose(0, 2, 1).reshape(NE * RANK, D)),
    }
    lay = {k: np.ascontiguousarray(v) for k, v in lay.items()}
    nc = bacc.Bacc("TRN2", target_bir_lowering=False, num_devices=1)
    mats = {k: nc.dram_tensor(k, v.shape, mybir.dt.float32, kind="ExternalInput").ap() for k, v in lay.items()}
    for name, shape in (("x1", (NTOK, D)), ("xn2T", (P, DC, NTOK)), ("qT", (P, H2, NTOK)), ("oT", (P, H2, NTOK))):
        mats[name] = nc.dram_tensor(name, shape, mybir.dt.float32, kind="Internal").ap()
    out = nc.dram_tensor("out_0", (NB, T, D), mybir.dt.float32, kind="ExternalOutput").ap()
    build(nc, mats["x"], mats, out)
    r = run(nc, [lay], core_ids=[0])
    return r.results[0]["out_0"]
```

```python
from contextlib import ExitStack

import concourse.bass as bass
from concourse import mybir

F32 = mybir.dt.float32
F32R = mybir.dt.float32r
ALU = mybir.AluOpType
ACT = mybir.ActivationFunctionType
AX_X = mybir.AxisListType.X

P = 128
BANK = 512
D = 512
DC = D // P
NB, T, S_CTX = 16, 56, 1500
NTOK = NB * T
PAIR = 2 * T
NPAIR = NTOK // PAIR
EPS = 1e-5
NEG = -1e30
LOWEST = -3e38

H1, HD1 = 32, 16
HPC = P // HD1
VX = HD1 + 2

H2, HD2, KVH = 32, 128, 4
GQ = H2 // KVH
SCALE2 = float(HD2) ** -0.5
NQ = GQ * T
KEYS = S_CTX + T
NCH = -(-KEYS // P)
GROUP = 3 * P
NG = 4
GW = [GROUP] * (NG - 1) + [KEYS - GROUP * (NG - 1)]
GWMAX = GW[-1]
CW = [P] * (NCH - 1) + [KEYS - P * (NCH - 1)]

NE, TOPK, RANK = 64, 16, 16
SCALING = 32.0 / RANK


class Space:

    def __init__(self, nc, ctx, stage):
        self.nc, self.ctx, self.stage, self.sems = nc, ctx, stage, []
        ctx.callback(self.release)

    def sb(self, name, shape, dt=F32):
        return self.ctx.enter_context(self.nc.sbuf_tensor(f"{self.stage}_{name}", shape, dt))

    def ps(self, name, shape):
        return self.ctx.enter_context(self.nc.psum_tensor(f"{self.stage}_{name}", shape, F32))

    def sem(self, name):
        self.sems.append(self.nc.alloc_semaphore(f"{self.stage}_{name}"))
        return self.sems[-1]

    def release(self):
        self.nc.clear_and_free_semaphores(self.sems)
        self.nc.all_engine_barrier()


def mm3(nc, out, a, b, start, stop):
    nc.tensor.matmul(out, a[0], b[0], start=start, stop=False)
    nc.tensor.matmul(out, a[0], b[1], start=False, stop=False)
    return nc.tensor.matmul(out, a[1], b[0], start=False, stop=stop)


def self_attention(nc, x, ident, mask, headmask, w_qkv, b_q, b_k, b_v, w_o, b_o, x1, xn2T):
    with ExitStack() as ctx:
        m = Space(nc, ctx, "sa")
        NW = D + P + HD1
        idn = m.sb("ident", [P, P])
        idn_r = m.sb("ident_r", [PAIR, PAIR], F32R)
        msk = m.sb("mask", [PAIR, 4 * PAIR])
        msk_r = m.sb("mask_r", [PAIR, 4 * PAIR], F32R)
        hmask = m.sb("headmask", [P, HPC])
        wqkv = m.sb("w_qkv", [P, DC, NW])
        wo = m.sb("w_o", [P, DC, D])
        bq = m.sb("b_q", [P, DC])
        bk = m.sb("b_k", [P, 1])
        bv = m.sb("b_v", [PAIR, HD1])
        bo = m.sb("b_o", [PAIR, D])
        neghalf = m.sb("neghalf", [PAIR, 1])
        eps = m.sb("eps", [PAIR, 1])
        xt = m.sb("x", [PAIR, D])
        xb = m.sb("x_bias", [PAIR, D])
        stat = m.sb("stat", [PAIR, 6])
        mv = m.sb("meanvar", [PAIR, 2])
        ve = m.sb("var_eps", [PAIR, 1])
        rstd = m.sb("rstd", [PAIR, 1])
        xn = m.sb("xn", [PAIR, D])
        xnT = m.sb("xnT", [P, DC, PAIR])
        qT = m.sb("qT", [P, DC, PAIR])
        kbd = m.sb("k_blockdiag", [P, HPC, PAIR])
        vx = m.sb("v_ones", [PAIR, VX])
        mx = m.sb("rowmax", [PAIR, 2, 4])
        p0 = m.sb("shifted", [PAIR, 2, 4, PAIR])
        pe_ = m.sb("weights", [PAIR, 2, 4, PAIR])
        pT = m.sb("weightsT", [PAIR, 2, 4, PAIR])
        rc = m.sb("recip", [PAIR, H1])
        at = m.sb("attn", [PAIR, H1, HD1])
        aT = m.sb("attnT", [P, DC, PAIR])
        x1t = m.sb("x1", [PAIR, D])
        xn2 = m.sb("xn2", [PAIR, D])
        x2T = m.sb("xn2T", [P, DC, PAIR])
        m0 = m.ps("misc0", [P, BANK])
        m1 = m.ps("misc1", [P, BANK])
        sc = m.ps("scores", [P, 2, BANK])
        tp = m.ps("transposed", [P, 2, BANK])
        ob = m.ps("out", [P, 2, BANK])

        loaded, ones, rounded = m.sem("weights_loaded"), m.sem("constants_set"), m.sem("mask_rounded")
        x_in, passed = m.sem("x_in"), m.sem("stats_passed")
        stats, meanvar, vareps, rstd_ok, xn_ok = (m.sem(n) for n in ("stats", "meanvar", "vareps", "rstd", "xn"))
        bias_ok, xnT_ps, xnT_ok, q_ps, kv_ps = (m.sem(n) for n in ("x_bias", "xnT_ps", "xnT", "q_ps", "kv_ps"))
        qT_ok, k_ok, v_ok = (m.sem(n) for n in ("qT", "k", "v"))
        s_ps, max_ok, shift_ok, exp_ok = (m.sem(n) for n in ("scores_ps", "max", "shifted", "exp"))
        pT_ps, pT_ok, o_ps = (m.sem(n) for n in ("weightsT_ps", "weightsT", "out_ps"))
        rc_ok, at_ok, aT_ps, aT_ok, wo_ps = (m.sem(n) for n in ("recip", "attn", "attnT_ps", "attnT", "wo_ps"))
        x1_ok, x1_out, stats2, meanvar2, vareps2 = (m.sem(n) for n in ("x1", "x1_out", "stats2", "meanvar2", "vareps2"))
        rstd2_ok, xn2_ok, x2T_ps, x2T_ok, x2T_out = (m.sem(n) for n in ("rstd2", "xn2", "xn2T_ps", "xn2T", "xn2T_out"))
        NS = H1 // 4

        def heads(ap):
            return ap.rearrange("p (h k) -> p h k", h=4)

        block = ctx.enter_context(nc.Block())

        @block.sync
        def _(sp):
            for dst, src in ((idn, ident), (msk, mask), (hmask, headmask), (wqkv, w_qkv), (bq, b_q),
                             (bk, b_k), (bv, b_v), (bo, b_o), (wo, w_o)):
                sp.dma_start(dst[:], src).then_inc(loaded, 16)
            with sp.Fori(0, NPAIR) as i:
                tok = sp.snap(i * PAIR)
                sp.wait_ge(bias_ok, i + 1)
                sp.dma_start(xt[:], x[bass.ds(tok, PAIR)]).then_inc(x_in, 16)
                sp.wait_ge(x1_ok, i + 1)
                sp.dma_start(x1[bass.ds(tok, PAIR)], x1t[:]).then_inc(x1_out, 16)
            sp.wait_ge(x1_out, 16 * (NPAIR + 1))
            sp.wait_ge(x2T_out, 16 * (NPAIR + 1))

        @block.gpsimd
        def _(pool):
            nc.gpsimd.memset(neghalf[:], -0.5).then_inc(ones, 1)
            nc.gpsimd.memset(vx[:], 1.0).then_inc(ones, 1)
            nc.gpsimd.memset(eps[:], EPS).then_inc(ones, 1)
            pool.nop().then_inc(bias_ok, 1)
            pool.wait_ge(ones, 3)
            pool.wait_ge(loaded, 16 * 9)
            with pool.Fori(0, NPAIR) as i:
                pool.wait_ge(meanvar, i + 1)
                nc.gpsimd.tensor_tensor(ve[:], mv[:, 1:2], eps[:], ALU.add).then_inc(vareps, 1)
                pool.wait_ge(vareps, i + 1)
                nc.gpsimd.tensor_tensor(rstd[:], ve[:], neghalf[:], ALU.pow).then_inc(rstd_ok, 1)
                pool.wait_ge(xn_ok, i + 1)
                nc.gpsimd.tensor_tensor(xb[:], xt[:], bo[:], ALU.add).then_inc(bias_ok, 1)
                pool.wait_ge(meanvar2, i + 1)
                nc.gpsimd.tensor_tensor(ve[:], mv[:, 1:2], eps[:], ALU.add).then_inc(vareps2, 1)
                pool.wait_ge(vareps2, i + 1)
                nc.gpsimd.tensor_tensor(rstd[:], ve[:], neghalf[:], ALU.pow).then_inc(rstd2_ok, 1)

        @block.scalar
        def _(act):
            act.wait_ge(loaded, 16 * 9)
            nc.scalar.activation(idn_r[:], idn[0:PAIR, 0:PAIR], ACT.Copy).then_inc(rounded, 1)
            nc.scalar.activation(msk_r[:], msk[:], ACT.Copy).then_inc(rounded, 1)
            act.nop().then_inc(x2T_out, 16)
            with act.Fori(0, NPAIR) as i:
                act.wait_ge(xnT_ps, i + 1)
                nc.scalar.activation(xnT[:].rearrange("p c t -> p (c t)"), m0[:, 0:4 * PAIR], ACT.Copy).then_inc(xnT_ok, 1)
                for s in range(NS):
                    act.wait_ge(shift_ok, i * NS + s + 1)
                    nc.scalar.activation(pe_[:, s % 2], p0[:, s % 2], ACT.Exp, scale=float(HD1) ** -0.5).then_inc(exp_ok, 1)
                    act.wait_ge(pT_ps, i * NS + s + 1)
                    nc.scalar.activation(pT[:, s % 2], heads(tp[0:PAIR, s % 2, 0:4 * PAIR]), ACT.Copy).then_inc(pT_ok, 1)
                act.wait_ge(aT_ps, i + 1)
                nc.scalar.activation(aT[:].rearrange("p c t -> p (c t)"), m0[:, 0:4 * PAIR], ACT.Copy).then_inc(aT_ok, 1)
                act.wait_ge(x2T_ps, i + 1)
                act.wait_ge(x2T_out, i * 16 + 16)
                nc.scalar.activation(x2T[:].rearrange("p c t -> p (c t)"), m0[:, 0:4 * PAIR], ACT.Copy).then_inc(x2T_ok, 1)
                act.wait_ge(x2T_ok, i + 1)
                act.dma_start(xn2T[:, :, bass.ds(i * PAIR, PAIR)], x2T[:]).then_inc(x2T_out, 16)

        @block.vector
        def _(dve):
            dve.wait_ge(loaded, 16 * 9)
            dve.wait_ge(ones, 3)
            dve.nop().then_inc(x1_out, 16)
            with dve.Fori(0, NPAIR) as i:
                dve.wait_ge(x_in, i * 16 + 16)
                nc.vector.bn_stats(stat[:], xt[:]).then_inc(stats, 1)
                dve.wait_ge(stats, i + 1)
                dve.nop().then_inc(passed, 1)
                nc.vector.bn_aggr(mv[:], stat[:]).then_inc(meanvar, 1)
                dve.wait_ge(rstd_ok, i + 1)
                nc.vector.tensor_scalar(xn[:], xt[:], mv[:, 0:1], rstd[:, 0:1], ALU.subtract, ALU.mult).then_inc(xn_ok, 1)
                dve.wait_ge(q_ps, i + 1)
                nc.vector.tensor_tensor(qT[:], m1[:, 0:4 * PAIR].rearrange("p (c t) -> p c t", c=DC),
                                        bq[:].unsqueeze(2).broadcast_to([P, DC, PAIR]), ALU.add).then_inc(qT_ok, 1)
                dve.wait_ge(kv_ps, i + 1)
                nc.vector.scalar_tensor_tensor(kbd[:], m0[:, 0:PAIR].unsqueeze(1).broadcast_to([P, HPC, PAIR]), bk[:, 0:1],
                                               hmask[:].unsqueeze(2).broadcast_to([P, HPC, PAIR]),
                                               ALU.add, ALU.mult).then_inc(k_ok, 1)
                nc.vector.tensor_tensor(vx[:, 0:HD1], m0[0:PAIR, PAIR:PAIR + HD1], bv[:], ALU.add).then_inc(v_ok, 1)
                for s in range(NS):
                    dve.wait_ge(s_ps, i * NS + s + 1)
                    sv = heads(sc[0:PAIR, s % 2, 0:4 * PAIR])
                    nc.vector.tensor_reduce(mx[:, s % 2], sv, AX_X, ALU.max).then_inc(max_ok, 1)
                    dve.wait_ge(max_ok, i * NS + s + 1)
                    if s >= 2:
                        dve.wait_ge(exp_ok, i * NS + s - 1)
                    nc.vector.tensor_tensor(p0[:, s % 2], sv, mx[:, s % 2].unsqueeze(2).broadcast_to([PAIR, 4, PAIR]),
                                            ALU.subtract).then_inc(shift_ok, 1)
                dve.wait_ge(o_ps, i * NS + NS)
                for h in range(2):
                    o = ob[0:PAIR, h, 0:16 * VX].rearrange("p (h v) -> p h v", h=16)
                    nc.vector.reciprocal(rc[:, h * 16:(h + 1) * 16], o[:, :, HD1]).then_inc(rc_ok, 1)
                dve.wait_ge(rc_ok, i * 2 + 2)
                for h in range(2):
                    o = ob[0:PAIR, h, 0:16 * VX].rearrange("p (h v) -> p h v", h=16)
                    nc.vector.tensor_tensor(at[:, h * 16:(h + 1) * 16], o[:, :, 0:HD1],
                                            rc[:, h * 16:(h + 1) * 16].unsqueeze(2).broadcast_to([PAIR, 16, HD1]),
                                            ALU.mult).then_inc(at_ok, 1)
                dve.wait_ge(wo_ps, i + 1)
                dve.wait_ge(bias_ok, i + 2)
                dve.wait_ge(x1_out, i * 16 + 16)
                nc.vector.tensor_tensor(x1t[:], m1[0:PAIR, :], xb[:], ALU.add).then_inc(x1_ok, 1)
                dve.wait_ge(x1_ok, i + 1)
                nc.vector.bn_stats(stat[:], x1t[:]).then_inc(stats2, 1)
                dve.wait_ge(stats2, i + 1)
                dve.nop().then_inc(passed, 1)
                nc.vector.bn_aggr(mv[:], stat[:]).then_inc(meanvar2, 1)
                dve.wait_ge(rstd2_ok, i + 1)
                nc.vector.tensor_scalar(xn2[:], x1t[:], mv[:, 0:1], rstd[:, 0:1], ALU.subtract, ALU.mult).then_inc(xn2_ok, 1)

        @block.tensor
        def _(pe):
            pe.wait_ge(loaded, 16 * 9)
            pe.wait_ge(rounded, 2)
            with pe.Fori(0, NPAIR) as i:
                pe.wait_ge(xn_ok, i + 1)
                for c in range(DC):
                    last = nc.tensor.transpose(m0[:, c * PAIR:(c + 1) * PAIR], xn[:, c * P:(c + 1) * P], idn[0:PAIR, 0:PAIR])
                last.then_inc(xnT_ps, 1)
                pe.wait_ge(xnT_ok, i + 1)
                for cc in range(DC):
                    for c in range(DC):
                        last = nc.tensor.matmul(m1[:, cc * PAIR:(cc + 1) * PAIR], wqkv[:, c, cc * P:(cc + 1) * P],
                                                xnT[:, c], start=(c == 0), stop=(c == DC - 1))
                last.then_inc(q_ps, 1)
                for c in range(DC):
                    nc.tensor.matmul(m0[:, 0:PAIR], wqkv[:, c, D:D + P], xnT[:, c], start=(c == 0), stop=(c == DC - 1))
                for c in range(DC):
                    last = nc.tensor.matmul(m0[0:PAIR, PAIR:PAIR + HD1], xnT[:, c], wqkv[:, c, D + P:NW],
                                            start=(c == 0), stop=(c == DC - 1))
                last.then_inc(kv_ps, 1)

                def scores(s):
                    if s == 0:
                        pe.wait_ge(qT_ok, i + 1)
                        pe.wait_ge(k_ok, i + 1)
                    if s >= 2:
                        pe.wait_ge(shift_ok, i * NS + s - 1)
                    out = sc[0:PAIR, s % 2, 0:4 * PAIR]
                    h = 4 * (s % 2)
                    nc.tensor.matmul(out, qT[:, s // 2], kbd[:, h:h + 4].rearrange("p h k -> p (h k)"), start=True, stop=False)
                    nc.tensor.matmul(out, idn_r[:], msk_r[:], start=False, stop=True).then_inc(s_ps, 1)

                def turn(s):
                    pe.wait_ge(exp_ok, i * NS + s + 1)
                    if s >= 2:
                        pe.wait_ge(pT_ok, i * NS + s - 1)
                    for h in range(4):
                        last = nc.tensor.transpose(tp[0:PAIR, s % 2, h * PAIR:(h + 1) * PAIR], pe_[:, s % 2, h],
                                                   idn[0:PAIR, 0:PAIR])
                    last.then_inc(pT_ps, 1)

                def weighted(s):
                    pe.wait_ge(pT_ok, i * NS + s + 1)
                    if s == 0:
                        pe.wait_ge(v_ok, i + 1)
                    for h in range(4):
                        o = (4 * s + h) % 16 * VX
                        last = nc.tensor.matmul(ob[0:PAIR, s // 4, o:o + VX], pT[:, s % 2, h], vx[:], start=True, stop=True)
                    last.then_inc(o_ps, 1)

                scores(0)
                for s in range(NS):
                    if s + 1 < NS:
                        scores(s + 1)
                    turn(s)
                    if s >= 1:
                        weighted(s - 1)
                weighted(NS - 1)
                pe.wait_ge(at_ok, i * 2 + 2)
                for c in range(DC):
                    last = nc.tensor.transpose(m0[:, c * PAIR:(c + 1) * PAIR],
                                               at[:, c * HPC:(c + 1) * HPC].rearrange("p h v -> p (h v)"),
                                               idn[0:PAIR, 0:PAIR])
                last.then_inc(aT_ps, 1)
                pe.wait_ge(aT_ok, i + 1)
                for c in range(DC):
                    last = nc.tensor.matmul(m1[0:PAIR, :], aT[:, c], wo[:, c], start=(c == 0), stop=(c == DC - 1))
                last.then_inc(wo_ps, 1)
                pe.wait_ge(xn2_ok, i + 1)
                for c in range(DC):
                    last = nc.tensor.transpose(m0[:, c * PAIR:(c + 1) * PAIR], xn2[:, c * P:(c + 1) * P], idn[0:PAIR, 0:PAIR])
                last.then_inc(x2T_ps, 1)
                pe.wait_ge(x2T_ok, i + 1)


def query_projection(nc, xn2T, w_q, qT_dram):
    with ExitStack() as ctx:
        m = Space(nc, ctx, "qp")
        HALF = NTOK // 2
        raw = m.sb("xn_raw", [P, DC, NTOK])
        xh = m.sb("xn_hi", [P, DC, NTOK], F32R)
        xl = m.sb("xn_lo", [P, DC, NTOK], F32R)
        wr = m.sb("w_raw", [P, 2, DC, P])
        wh = m.sb("w_hi", [P, 2, DC, P], F32R)
        wl = m.sb("w_lo", [P, 2, DC, P], F32R)
        st = m.sb("q_stage", [P, 2, NTOK])
        qb = m.ps("q", [P, 4, BANK])
        x_in, x_hi, x_lo = m.sem("xn_in"), m.sem("xn_hi"), m.sem("xn_lo")
        w_in = [m.sem(f"w_in{k}") for k in range(2)]
        w_hi, w_lo, q_ps, lo_half, hi_half = (m.sem(n) for n in ("w_hi", "w_lo", "q_ps", "left_staged", "right_staged"))
        stored = [m.sem(f"stored{k}") for k in range(2)]
        block = ctx.enter_context(nc.Block())

        @block.sync
        def _(sp):
            sp.dma_start(raw[:], xn2T).then_inc(x_in, 16)
            for k in range(2):
                sp.dma_start(wr[:, k], w_q[k]).then_inc(w_in[k], 16)
            with sp.Fori(0, H2 // 2 - 1) as i:
                for k in range(2):
                    sp.wait_ge(w_lo, i * 2 + k + 1)
                    sp.dma_start(wr[:, k], w_q[i * 2 + (k + 2)]).then_inc(w_in[k], 16)

        @block.gpsimd
        def _(pool):
            for c in range(DC):
                pool.wait_ge(x_hi, c + 1)
                nc.gpsimd.tensor_tensor(xl[:, c], raw[:, c], xh[:, c].bitcast(F32), ALU.subtract).then_inc(x_lo, 1)
            pool.nop().then_inc(q_ps, 2)
            with pool.Fori(0, H2 // 2) as i:
                for k in range(2):
                    pool.wait_ge(w_hi, i * 2 + k + 1)
                    pool.wait_ge(q_ps, i * 2 + k + 1)
                    nc.gpsimd.tensor_tensor(wl[:, k], wr[:, k], wh[:, k].bitcast(F32), ALU.subtract).then_inc(w_lo, 1)

        @block.scalar
        def _(act):
            act.wait_ge(x_in, 16)
            for k in range(2):
                act.nop().then_inc(hi_half, 1)
            for c in range(DC):
                nc.scalar.activation(xh[:, c], raw[:, c], ACT.Copy).then_inc(x_hi, 1)
            for k in range(2):
                act.wait_ge(w_in[k], 16)
                nc.scalar.activation(wh[:, k], wr[:, k], ACT.Copy).then_inc(w_hi, 1)

            def two_heads(i, more):
                for k in range(2):
                    act.wait_ge(q_ps, i * 2 + k + 3)
                    act.wait_ge(stored[k], i * 16 + 16)
                    nc.scalar.activation(st[:, k, HALF:NTOK], qb[:, 2 * k + 1, 0:HALF], ACT.Copy, scale=SCALE2).then_inc(hi_half, 1)
                    act.wait_ge(lo_half, i * 2 + k + 3)
                    act.wait_ge(hi_half, i * 2 + k + 3)
                    act.dma_start(qT_dram[:, i * 2 + k], st[:, k]).then_inc(stored[k], 16)
                    if more:
                        act.wait_ge(w_in[k], i * 16 + 32)
                        nc.scalar.activation(wh[:, k], wr[:, k], ACT.Copy).then_inc(w_hi, 1)

            with act.Fori(0, H2 // 2 - 1) as i:
                two_heads(i, True)
            two_heads(H2 // 2 - 1, False)
            for k in range(2):
                act.wait_ge(stored[k], 16 * (H2 // 2 + 1))

        @block.vector
        def _(dve):
            for k in range(2):
                dve.nop().then_inc(stored[k], 16)
                dve.nop().then_inc(lo_half, 1)
            with dve.Fori(0, H2 // 2) as i:
                for k in range(2):
                    dve.wait_ge(q_ps, i * 2 + k + 3)
                    dve.wait_ge(stored[k], i * 16 + 16)
                    nc.vector.tensor_scalar(st[:, k, 0:HALF], qb[:, 2 * k, 0:HALF], SCALE2, None, ALU.mult).then_inc(lo_half, 1)

        @block.tensor
        def _(pe):
            pe.wait_ge(x_lo, DC)
            with pe.Fori(0, H2 // 2) as i:
                for k in range(2):
                    pe.wait_ge(w_lo, i * 2 + k + 1)
                    pe.wait_ge(lo_half, i * 2 + k + 1)
                    pe.wait_ge(hi_half, i * 2 + k + 1)
                    for h in range(2):
                        cols = slice(h * HALF, (h + 1) * HALF)
                        for c in range(DC):
                            last = mm3(nc, qb[:, 2 * k + h, 0:HALF], (wh[:, k, c], wl[:, k, c]),
                                       (xh[:, c, cols], xl[:, c, cols]), start=(c == 0), stop=(c == DC - 1))
                    last.then_inc(q_ps, 1)


HPS = KVH // 2
NT = 4 * HPS
NS2 = NT * NG


def group_chunks(g):
    return range(3 * g, min(3 * g + 3, NCH) + (g == NG - 1))


KV = [s for g in range(NG) for s in [("K", g, j) for j in range(HPS)] + [("V", g, c) for c in group_chunks(g) if g < 2]]
KV += [("V", g, c) for g in range(2, NG) for c in group_chunks(g)]
NKV = len(KV)
K_DONE = KV.index(("K", NG - 1, HPS - 1)) + 1
GROUP_DONE = [max(n for n, s in enumerate(KV) if s[1] == g) + 1 for g in range(NG)]
LAG = 3
NTB = 3



def spread(rows, others, lead=0):
    order, n = [], 0
    for m in range(-1, len(rows)):
        if m >= 0:
            order += rows[m]
        while n < len(others) and n < lead + (m + 1) * (len(others) - lead) / len(rows):
            kv = [KV[x[1]] for x in others[n] if x[0] == "KV"]
            if kv and kv[0][0] == "V" and ("PV", 1, kv[0][2]) in sum(rows[m + 1:], []):
                break
            order += others[n]
            n += 1
    return order + [x for step in others[n:] for x in step]


def score_steps():
    steps = [[("S", n)] for n in range(NS2)] + [[] for _ in range(3)]
    for k in range(NT):
        for f, x in enumerate([("F1", k), ("F2", k), ("F3", k)] + [("W", k, g) for g in range(NG) if k % 4 == 3]):
            steps[min(NG * (k + 1) + f, NS2 + 2)].append(x)
    return steps[:NS2] + [[x for step in steps[NS2:] for x in step]]


def value_rows(j):
    rows = [[("T", j, m)] * (m < NCH) + [("PV", j, m - LAG)] * (m >= LAG) for m in range(NCH + LAG)]
    rows[-1].append(("O", j))
    return rows


NAHEAD = K_DONE
PROJECT = [[("KV", n, 1)] for n in range(NAHEAD)]
for n, x in ((4, ("CX", 2, 0)), (5, ("CX", 2, 1)), (6, ("CX", 2, 2)), (7, ("CX", 2, 3)),
             (9, ("CX", 3, 0)), (9, ("CX", 3, 1)), (10, ("CX", 3, 2)), (10, ("CX", 3, 3))):
    assert n >= GROUP_DONE[x[1] - 2] - 1 and KV.index(("K", x[1], 0)) > n
    PROJECT[n].append(x)
SCORES = score_steps()
ALONE = 26
SPLIT_AT = {n: ("CX", g, c) for g, at in ((0, (16, 18, 20, 22)), (1, (26, 27, 28, 29))) for c, n in enumerate(at)}
SCORES_NEXT = [step + ([SPLIT_AT[n]] if n in SPLIT_AT else []) for n, step in enumerate(SCORES)]
REST = [[("KV", n, 0)] for n in range(NAHEAD, NKV)]
FIRST = [("QX",)] + [("CX", g, c) for g in range(2) for c in range(DC)] + [x for step in PROJECT for x in step]
STEADY = spread(SCORES_NEXT[:ALONE], REST, 1) + spread(value_rows(0), SCORES_NEXT[ALONE:]) + [("QX",)] + spread(value_rows(1), PROJECT, 2)
LAST = spread(SCORES[:ALONE], REST, 1) + spread(value_rows(0), SCORES[ALONE:]) + spread(value_rows(1), [])

RING = [x for x in STEADY if x[0] in ("S", "KV")]
BANK_OF = {x: r % 4 for r, x in enumerate(RING)}
BEFORE = {x: (RING[r - 4], 0) if r >= 4 else (max(y for y in enumerate(RING) if y[0] % 4 == r)[1], -1)
          for r, x in enumerate(RING)}


def scalar_order(order):
    done, late = [], []
    for x in order:
        if x[0] in ("S", "KV", "QX", "CX", "O"):
            done += late
            late = []
        if x[0] == "S":
            late = [x]
        else:
            done.append(x)
        if x[0] == "T":
            done += late
            late = []
    return done + late


def vector_order(order):
    done, late = [], []
    for x in order:
        if x[0] != "S" and late:
            done += late
            late = []
        if x[0] == "KV" and x[2] == 0:
            late = [x]
        else:
            done.append(x)
        if x[0] == "S":
            done += late
            late = []
    return done + late


def need(eng, sem, unit, per, k):
    i, ahead = unit
    if isinstance(i, int):
        if (i + ahead) * per + k > 0:
            eng.wait_ge(sem, (i + ahead) * per + k)
    else:
        assert ahead * per + k > 0
        eng.wait_ge(sem, i * per + (ahead * per + k))


def cross_attention(nc, half, ident, ctx_dram, xn2T, qT_dram, w_k, w_v, oT_dram):
    with ExitStack() as stack:
        m = Space(nc, stack, f"ca{half}")
        WC = HPS * HD2
        HQ = HPS * GQ
        idn = m.sb("ident", [P, P])
        w_raw = m.sb("w_raw", [P, 2, DC, WC])
        w_hi = m.sb("w_hi", [P, 2, DC, WC], F32R)
        w_lo = m.sb("w_lo", [P, 2, DC, WC], F32R)
        craw = m.sb("ctx_raw", [P, 2, DC, GWMAX])
        chi = m.sb("ctx_hi", [P, 2, DC, GWMAX], F32R)
        clo = m.sb("ctx_lo", [P, 2, DC, GWMAX], F32R)
        qraw = m.sb("q_raw", [P, HQ * T])
        qhi = m.sb("q_hi", [P, HQ * T], F32R)
        qlo = m.sb("q_lo", [P, HQ * T], F32R)
        khi = m.sb("k_hi", [P, HPS, KEYS], F32R)
        klo = m.sb("k_lo", [P, HPS, KEYS], F32R)
        vhi = m.sb("v_hi", [P, NCH, WC], F32R)
        vlo = m.sb("v_lo", [P, NCH, WC], F32R)
        pr = m.sb("weights", [PAIR, NT, KEYS])
        ptl = m.sb("weightsT_lo", [P, 4, NQ], F32R)
        pth = m.sb("weightsT_hi", [P, 4, NQ], F32R)
        nmax = m.sb("neg_groupmax", [PAIR, NT, NG])
        nrow = m.sb("neg_rowmax", [PAIR, NT])
        gsum = m.sb("groupsum", [PAIR, NT, NG])
        corr = m.sb("correction", [PAIR, NT, NG])
        junk = m.sb("product", [PAIR, NT, NG])
        rsum = m.sb("rowsum", [PAIR, NT])
        rinv = m.sb("inv_rowsum", [PAIR, NT])
        fac = m.sb("factor", [PAIR, NT, NG])
        ost = m.sb("out_stage", [P, HPS, NQ])
        bank = m.ps("scores", [P, 4, BANK])
        tb = m.ps("turned", [P, NTB, BANK])
        acc = m.ps("out", [P, BANK])

        w_in, w_hi_ok, w_lo_ok = m.sem("w_in"), m.sem("w_hi"), m.sem("w_lo")
        raw_in = [m.sem(f"ctx_in{r}") for r in range(2)]
        c_hi, c_lo, q_in, q_hi, q_lo = (m.sem(n) for n in ("ctx_hi", "ctx_lo", "q_in", "q_hi", "q_lo"))
        kv_ps, kv_hi, kv_lo = (m.sem(n) for n in ("kv_ps", "kv_hi", "kv_lo"))
        s_ps, gmax_ok, rmax_ok, exp_ok, corr_ok = (m.sem(n) for n in ("scores_ps", "groupmax", "rowmax", "exp", "correction"))
        sum_ok, inv_ok, fac_ok, p_ok = (m.sem(n) for n in ("rowsum", "inv_rowsum", "factor", "weights"))
        t_ps, t_hi, t_lo, pv_ok, o_ok = (m.sem(n) for n in ("turned_ps", "turned_hi", "turned_lo", "pv", "out_staged"))
        o_out = [m.sem(f"out_stored{j}") for j in range(HPS)]
        issue, p_last = m.sem("load_issued"), m.sem("last_weights")

        def chunk_of(c):
            g = min(c // 3, NG - 1)
            return g % 2, (c - 3 * g) * P

        block = stack.enter_context(nc.Block())

        @block.sync
        def _(sp):
            sp.dma_start(idn[:], ident).then_inc(w_in, 16)
            sp.dma_start(w_raw[:, 0], w_k[:, :, half * WC:(half + 1) * WC]).then_inc(w_in, 16)
            sp.dma_start(w_raw[:, 1], w_v[:, :, half * WC:(half + 1) * WC]).then_inc(w_in, 16)

            def load(i):
                unit = (i, 0)
                for g in range(NG):
                    if g == 0:
                        need(sp, q_lo, unit, 1, 1)
                        sp.nop().then_inc(issue, 1)
                        sp.dma_start(qraw[:].rearrange("p (h t) -> p h t", h=HQ),
                                     qT_dram[:, half * HQ:(half + 1) * HQ, bass.ds(i * T, T)]).then_inc(q_in, 16)
                    need(sp, c_lo, unit, NG * DC, (g + 1) * DC)
                    sp.nop().then_inc(issue, 1)
                    w = min(GW[g], S_CTX - g * GROUP)
                    sp.dma_start(craw[:, g % 2, :, 0:w], ctx_dram[i, :, :, g * GROUP:g * GROUP + w]).then_inc(raw_in[g % 2], 16)
                    if g == NG - 1:
                        sp.dma_start(craw[:, g % 2, :, w:w + T], xn2T[:, :, bass.ds(i * T, T)]).then_inc(raw_in[g % 2], 16)

            with sp.Fori(0, NB) as i:
                load(i)

        @block.gpsimd
        def _(pool):
            pool.nop().then_inc(c_lo, 2 * DC)
            pool.nop().then_inc(q_lo, 1)
            pool.wait_ge(w_hi_ok, 2)
            for k in range(2):
                nc.gpsimd.tensor_tensor(w_lo[:, k], w_raw[:, k], w_hi[:, k].bitcast(F32), ALU.subtract).then_inc(w_lo_ok, 1)

            def run(order, i):
                for step in order:
                    unit = (i, 1)
                    if step[0] == "F3" and step[1] % 4 != 3:
                        k = step[1]
                        need(pool, fac_ok, (i, 0), NT, k + 1)
                        a = pr[:, k, 0:3 * GROUP].rearrange("p (g w) -> p g w", g=3)
                        nc.gpsimd.tensor_tensor(a, a, fac[:, k, 0:3].unsqueeze(2).broadcast_to([PAIR, 3, GROUP]), ALU.mult)
                        b = pr[:, k, 3 * GROUP:KEYS]
                        nc.gpsimd.tensor_tensor(b, b, fac[:, k, 3:4].broadcast_to([PAIR, GW[3]]), ALU.mult).then_inc(p_ok, 1)
                    elif step[0] == "QX":
                        need(pool, q_hi, unit, 1, 1)
                        nc.gpsimd.tensor_tensor(qlo[:], qraw[:], qhi[:].bitcast(F32), ALU.subtract).then_inc(q_lo, 1)
                    elif step[0] == "CX":
                        _, g, c = step
                        w, r = GW[g], g % 2
                        need(pool, c_hi, unit, NG * DC, g * DC + c + 1)
                        nc.gpsimd.tensor_tensor(clo[:, r, c, 0:w], craw[:, r, c, 0:w], chi[:, r, c, 0:w].bitcast(F32),
                                                ALU.subtract).then_inc(c_lo, 1)

            run(FIRST, -1)
            with pool.Fori(0, NB - 1) as i:
                run(STEADY, i)
            run(LAST, NB - 1)

        @block.scalar
        def _(act):
            act.nop().then_inc(o_ok, 1)
            for j in range(HPS):
                act.nop().then_inc(o_out[j], 16)
            act.wait_ge(w_in, 48)
            for k in range(2):
                nc.scalar.activation(w_hi[:, k], w_raw[:, k], ACT.Copy).then_inc(w_hi_ok, 1)

            def run(order, i):
                for step in scalar_order(order):
                    if step[0] == "S":
                        n, unit = step[1], (i, 0)
                        k, g = n // NG, n % NG
                        need(act, gmax_ok, unit, NS2, n + 1)
                        nc.scalar.activation(pr[:, k, g * GROUP:g * GROUP + GW[g]], bank[0:PAIR, BANK_OF[step], 0:GW[g]], ACT.Exp,
                                             bias=nmax[:, k, g:g + 1], accum_out=gsum[:, k, g:g + 1]).then_inc(exp_ok, 1)
                        if g == NG - 1:
                            need(act, rmax_ok, unit, NT, k + 1)
                            nc.scalar.activation(corr[:, k], nmax[:, k], ACT.Exp, bias=nrow[:, k:k + 1],
                                                 scale=-1.0).then_inc(corr_ok, 1)
                    elif step[0] == "T":
                        _, j, c = step
                        need(act, t_ps, (i, 0), 2 * NCH, NCH * j + c + 1)
                        nc.scalar.activation(pth[0:CW[c], c % 4, :], tb[0:CW[c], c % NTB, 0:NQ],
                                             ACT.Copy).then_inc(t_hi, 1)
                    elif step[0] == "QX":
                        need(act, q_in, (i, 1), 16, 16)
                        need(act, s_ps, (i, 1), NS2, 0)
                        nc.scalar.activation(qhi[:], qraw[:], ACT.Copy).then_inc(q_hi, 1)
                    elif step[0] == "CX":
                        _, g, c = step
                        w, r, unit = GW[g], g % 2, (i, 1)
                        if c == 0:
                            need(act, raw_in[r], unit, 32 + 16 * r, 16 * (g // 2 + 1) + 16 * (g == NG - 1))
                            need(act, kv_ps, unit, NKV, GROUP_DONE[g - 2] if g >= 2 else GROUP_DONE[g + 2] - NKV)
                        nc.scalar.activation(chi[:, r, c, 0:w], craw[:, r, c, 0:w], ACT.Copy).then_inc(c_hi, 1)
                    elif step[0] == "KV":
                        unit = (i, step[2])
                        need(act, kv_ps, unit, NKV, step[1] + 1)
                        kind, g, x = KV[step[1]]
                        b = BANK_OF[step]
                        if kind == "K":
                            nc.scalar.activation(khi[:, x, g * GROUP:g * GROUP + GW[g]], bank[:, b, 0:GW[g]], ACT.Copy).then_inc(kv_hi, 1)
                        else:
                            nc.scalar.activation(vhi[0:CW[x], x], bank[0:CW[x], b, 0:WC], ACT.Copy).then_inc(kv_hi, 1)
                    elif step[0] == "O":
                        j = step[1]
                        need(act, pv_ok, (i, 0), 2 * NCH, NCH * (j + 1))
                        need(act, o_out[j], (i, 0), 16, 16)
                        nc.scalar.activation(ost[:, j], acc[:, 0:NQ], ACT.Copy).then_inc(o_ok, 1)
                        need(act, o_ok, (i, 0), HPS, j + 2)
                        act.dma_start(oT_dram[:, half * HQ + j * GQ:half * HQ + (j + 1) * GQ, bass.ds(i * T, T)],
                                      ost[:, j].rearrange("p (h t) -> p h t", h=GQ)).then_inc(o_out[j], 16)

            run(FIRST, -1)
            with act.Fori(0, NB - 1) as i:
                run(STEADY, i)
            run(LAST, NB - 1)
            for j in range(HPS):
                act.wait_ge(o_out[j], 16 * (NB + 1))

        @block.vector
        def _(dve):
            def run(order, i):
                for step in vector_order(order):
                    if step[0] == "S":
                        n, unit = step[1], (i, 0)
                        k, g = n // NG, n % NG
                        need(dve, s_ps, unit, NS2, n + 1)
                        nc.vector.tensor_reduce(nmax[:, k, g:g + 1], bank[0:PAIR, BANK_OF[step], 0:GW[g]], AX_X, ALU.max,
                                                negate=True).then_inc(gmax_ok, 1)
                        if g == NG - 1:
                            need(dve, gmax_ok, unit, NS2, n + 1)
                            nc.vector.tensor_reduce(nrow[:, k:k + 1], nmax[:, k], AX_X, ALU.min).then_inc(rmax_ok, 1)
                    elif step[0] == "F1":
                        k = step[1]
                        need(dve, corr_ok, (i, 0), NT, k + 1)
                        nc.vector.tensor_tensor_reduce(junk[:, k], gsum[:, k], corr[:, k], 1.0, 0.0, ALU.mult, ALU.add,
                                                       rsum[:, k:k + 1]).then_inc(sum_ok, 1)
                    elif step[0] == "F2":
                        k = step[1]
                        need(dve, sum_ok, (i, 0), NT, k + 1)
                        nc.vector.reciprocal(rinv[:, k:k + 1], rsum[:, k:k + 1]).then_inc(inv_ok, 1)
                    elif step[0] == "F3":
                        k, unit = step[1], (i, 0)
                        need(dve, inv_ok, unit, NT, k + 1)
                        nc.vector.tensor_scalar(fac[:, k], corr[:, k], rinv[:, k:k + 1], None, ALU.mult).then_inc(fac_ok, 1)
                    elif step[0] == "W":
                        _, k, g = step
                        w = pr[:, k, g * GROUP:g * GROUP + GW[g]]
                        need(dve, fac_ok, (i, 0), NT, k + 1)
                        last = nc.vector.tensor_scalar(w, w, fac[:, k, g:g + 1], None, ALU.mult)
                        if g == NG - 1:
                            last.then_inc(p_last, 1)
                    elif step[0] == "T":
                        _, j, c = step
                        need(dve, t_hi, (i, 0), 2 * NCH, NCH * j + c + 1)
                        nc.vector.tensor_tensor(ptl[0:CW[c], c % 4, :], tb[0:CW[c], c % NTB, 0:NQ],
                                                pth[0:CW[c], c % 4, :].bitcast(F32), ALU.subtract).then_inc(t_lo, 1)
                    elif step[0] == "KV":
                        need(dve, kv_hi, (i, step[2]), NKV, step[1] + 1)
                        kind, g, x = KV[step[1]]
                        b = BANK_OF[step]
                        if kind == "K":
                            s = slice(g * GROUP, g * GROUP + GW[g])
                            nc.vector.tensor_tensor(klo[:, x, s], bank[:, b, 0:GW[g]], khi[:, x, s].bitcast(F32),
                                                    ALU.subtract).then_inc(kv_lo, 1)
                        else:
                            nc.vector.tensor_tensor(vlo[0:CW[x], x], bank[0:CW[x], b, 0:WC], vhi[0:CW[x], x].bitcast(F32),
                                                    ALU.subtract).then_inc(kv_lo, 1)

            run(FIRST, -1)
            with dve.Fori(0, NB - 1) as i:
                run(STEADY, i)
            run(LAST, NB - 1)

        @block.tensor
        def _(pe):
            pe.wait_ge(w_lo_ok, 2)

            def bank_free(step, i):
                user, back = BEFORE[step]
                if user[0] == "S":
                    need(pe, exp_ok, (i, back), NS2, user[1] + 1)
                else:
                    need(pe, kv_lo, (i, back + user[2]), NKV, user[1] + 1)

            def run(order, i):
                for step in order:
                    if step[0] == "S":
                        n, unit = step[1], (i, 0)
                        k, g = n // NG, n % NG
                        if n == 0:
                            need(pe, q_lo, unit, 1, 2)
                            need(pe, kv_lo, unit, NKV, K_DONE)
                        bank_free(step, i)
                        j, cols = k // 4, slice(k * PAIR, (k + 1) * PAIR)
                        s = slice(g * GROUP, g * GROUP + GW[g])
                        mm3(nc, bank[0:PAIR, BANK_OF[step], 0:GW[g]], (qhi[:, cols], qlo[:, cols]), (khi[:, j, s], klo[:, j, s]),
                            True, True).then_inc(s_ps, 1)
                    elif step[0] == "T":
                        _, j, c = step
                        if c == 0:
                            need(pe, p_ok, (i, 0), NT - HPS, 3 * (j + 1))
                            need(pe, p_last, (i, 0), HPS, j + 1)
                        if c >= NTB:
                            need(pe, t_lo, (i, 0), 2 * NCH, NCH * j + c - NTB + 1)
                        for q in range(4):
                            last = nc.tensor.transpose(tb[0:CW[c], c % NTB, q * PAIR:(q + 1) * PAIR],
                                                       pr[:, 4 * j + q, c * P:c * P + CW[c]], idn[0:PAIR, 0:PAIR])
                        last.then_inc(t_ps, 1)
                    elif step[0] == "PV":
                        _, j, c = step
                        if c == 0:
                            need(pe, kv_lo, (i, 0), NKV, NKV)
                            need(pe, o_ok, (i, 0), HPS, j + 1)
                        need(pe, t_lo, (i, 0), 2 * NCH, NCH * j + c + 1)
                        w, s = CW[c], slice(j * HD2, (j + 1) * HD2)
                        mm3(nc, acc[:, 0:NQ], (vhi[0:w, c, s], vlo[0:w, c, s]), (pth[0:w, c % 4], ptl[0:w, c % 4]),
                            c == 0, c == NCH - 1).then_inc(pv_ok, 1)
                    elif step[0] == "KV":
                        n, unit = step[1], (i, step[2])
                        bank_free(step, i)
                        kind, g, x = KV[n]
                        if (kind, x) == ("K", 0):
                            need(pe, c_lo, unit, NG * DC, (g + 3) * DC)
                        for c in range(DC):
                            st, sp_ = c == 0, c == DC - 1
                            if kind == "K":
                                s = slice(x * HD2, (x + 1) * HD2)
                                last = mm3(nc, bank[:, BANK_OF[step], 0:GW[g]], (w_hi[:, 0, c, s], w_lo[:, 0, c, s]),
                                           (chi[:, g % 2, c, 0:GW[g]], clo[:, g % 2, c, 0:GW[g]]), st, sp_)
                            else:
                                o = (x - 3 * g) * P
                                s = slice(o, o + CW[x])
                                last = mm3(nc, bank[0:CW[x], BANK_OF[step], 0:WC], (chi[:, g % 2, c, s], clo[:, g % 2, c, s]),
                                           (w_hi[:, 1, c], w_lo[:, 1, c]), st, sp_)
                        last.then_inc(kv_ps, 1)

            run(FIRST, -1)
            with pe.Fori(0, NB - 1) as i:
                run(STEADY, i)
            run(LAST, NB - 1)


def output_and_experts(nc, ident, x1, oT_dram, w_o, w_er, w_eb, out):
    with ExitStack() as ctx:
        m = Space(nc, ctx, "oe")
        NTT = NTOK // P
        KR = NE * RANK
        KC = KR // P
        NR = KR + NE
        idn = m.sb("ident", [P, P])
        zero = m.sb("zero", [P, D], F32R)
        wr = m.sb("wo_raw", [P, 2, D])
        wh = m.sb("wo_hi", [P, 2, D], F32R)
        wl = m.sb("wo_lo", [P, 2, D], F32R)
        orw = m.sb("o_raw", [P, 2, NTOK])
        oh = m.sb("o_hi", [P, 2, NTOK], F32R)
        ol = m.sb("o_lo", [P, 2, NTOK], F32R)
        er = m.sb("er_raw", [P, DC, NR])
        erh = m.sb("er_hi", [P, DC, NR], F32R)
        erl = m.sb("er_lo", [P, DC, NR], F32R)
        eb = m.sb("eb_raw", [P, KC, D])
        ebh = m.sb("eb_hi", [P, KC, D], F32R)
        ebl = m.sb("eb_lo", [P, KC, D], F32R)
        x2 = m.sb("x2", [P, NTT, D])
        xt = m.sb("x2_tile", [P, D])
        xres = m.sb("x2_residual", [P, D])
        neghalf, eps = m.sb("neghalf", [P, 1]), m.sb("eps", [P, 1])
        stat, mv, ve, rstd = m.sb("stat", [P, 6]), m.sb("meanvar", [P, 2]), m.sb("var_eps", [P, 1]), m.sb("rstd", [P, 1])
        xn = m.sb("xn", [P, D])
        xh = m.sb("xnT_hi", [P, DC, P], F32R)
        xl = m.sb("xnT_lo", [P, DC, P], F32R)
        rs = m.sb("router", [P, NE])
        top = m.sb("top", [P, 2, 8])
        rest = m.sb("rest", [P, 2, NE])
        ntop = m.sb("neg_top", [P, 1])
        ex = m.sb("exp", [P, NE])
        chosen = m.sb("chosen", [P, NE])
        gate0, gsum, ginv = m.sb("gate0", [P, NE]), m.sb("gatesum", [P, 1]), m.sb("gateinv", [P, 1])
        gate = m.sb("gate", [P, NE])
        hg = m.sb("gated", [P, NE, RANK])
        gh = m.sb("gatedT_hi", [P, KC, P], F32R)
        gl = m.sb("gatedT_lo", [P, KC, P], F32R)
        res = m.sb("result", [P, D])
        ps = m.ps("ps", [P, 8, BANK])

        x_in, e_in, x2_ok = (m.sem(n) for n in ("x1_in", "experts_in", "x2"))
        w_in = [m.sem(f"wo_in{k}") for k in range(2)]
        w_hi, w_lo, o_lo, head_ok, acc_ok = (m.sem(n) for n in ("wo_hi", "wo_lo", "o_lo", "head", "accumulated"))
        zero_ok, load_go, res_in = m.sem("zeros_set"), m.sem("load_issued"), m.sem("residual_in")
        e_hi, e_lo = m.sem("experts_hi"), m.sem("experts_lo")
        t_in, stats, passed, meanvar, vareps, rstd_ok, xn_ok = (m.sem(n) for n in (
            "tile_in", "stats", "stats_passed", "meanvar", "vareps", "rstd", "xn"))
        xt_ps, xt_hi, xt_lo, r_ps, h_ps, r_ok = (m.sem(n) for n in ("xnT_ps", "xnT_hi", "xnT_lo", "router_ps", "h_ps", "router"))
        top1, rest1, top2, rest2, go = (m.sem(n) for n in ("top1", "rest1", "top2", "rest2", "max_passed"))
        ntop_ok, ex_ok, chosen_ok, sum_ok, inv_ok, gate_ok, hg_ok = (m.sem(n) for n in (
            "negtop", "exp", "chosen", "gatesum", "gateinv", "gate", "gated"))
        gt_ps, gt_hi, gt_lo, y_ps, res_ok, stored = (m.sem(n) for n in (
            "gatedT_ps", "gatedT_hi", "gatedT_lo", "y_ps", "result", "stored"))
        out_rows = out.rearrange("b t d -> (b t) d")

        block = ctx.enter_context(nc.Block())

        @block.sync
        def _(sp):
            for k in range(2):
                sp.dma_start(wr[:, k], w_o[k]).then_inc(w_in[k], 16)
                sp.dma_start(orw[:, k], oT_dram[:, k]).then_inc(w_in[k], 16)
            sp.dma_start(idn[:], ident).then_inc(e_in, 16)
            sp.dma_start(er[:], w_er).then_inc(e_in, 16)
            sp.dma_start(eb[:], w_eb).then_inc(e_in, 16)
            sp.dma_start(x2[:], x1.rearrange("(n p) d -> p n d", p=P)).then_inc(x_in, 16)
            with sp.Fori(0, H2 // 2 - 1) as i:
                for k in range(2):
                    sp.wait_ge(w_lo, i * 2 + k + 1)
                    sp.wait_ge(o_lo, i * 2 + k + 1)
                    sp.dma_start(wr[:, k], w_o[i * 2 + (k + 2)]).then_inc(w_in[k], 16)
                    sp.dma_start(orw[:, k], oT_dram[:, i * 2 + (k + 2)]).then_inc(w_in[k], 16)
            sp.wait_ge(x2_ok, NTT)
            sp.nop().then_inc(load_go, 1)
            sp.dma_start(xt[:], x2[:, 0]).then_inc(t_in, 16)
            sp.wait_ge(xn_ok, 1)
            sp.nop().then_inc(load_go, 1)
            sp.dma_start(xt[:], x2[:, 1]).then_inc(t_in, 16)

            def tile(i, more):
                sp.wait_ge(res_ok, i + 1)
                sp.nop().then_inc(load_go, 1)
                sp.dma_start(xres[:], x2[:, i]).then_inc(res_in, 16)
                if more:
                    sp.wait_ge(xn_ok, i + 2)
                    sp.nop().then_inc(load_go, 1)
                    sp.dma_start(xt[:], x2[:, i + 2]).then_inc(t_in, 16)
                sp.wait_ge(res_ok, i + 2)
                sp.nop().then_inc(load_go, 1)
                sp.dma_start(out_rows[bass.ds(i * P, P)], res[:]).then_inc(stored, 16)

            with sp.Fori(0, NTT - 2) as i:
                tile(i, True)
            for t in range(NTT - 2, NTT):
                tile(t, False)
            sp.wait_ge(stored, 16 * (NTT + 1))

        @block.gpsimd
        def _(pool):
            nc.gpsimd.memset(zero[:].bitcast(F32), 0.0).then_inc(zero_ok, 1)
            nc.gpsimd.memset(neghalf[:], -0.5)
            nc.gpsimd.memset(eps[:], EPS)
            with pool.Fori(0, H2 // 2) as i:
                for k in range(2):
                    pool.wait_ge(w_hi, i * 4 + (2 * k + 1))
                    nc.gpsimd.tensor_tensor(wl[:, k], wr[:, k], wh[:, k].bitcast(F32), ALU.subtract).then_inc(w_lo, 1)
            for c in range(DC):
                pool.wait_ge(e_hi, c + 1)
                nc.gpsimd.tensor_tensor(erl[:, c], er[:, c], erh[:, c].bitcast(F32), ALU.subtract).then_inc(e_lo, 1)
            for c in range(KC):
                pool.wait_ge(e_hi, DC + c + 1)
                nc.gpsimd.tensor_tensor(ebl[:, c], eb[:, c], ebh[:, c].bitcast(F32), ALU.subtract).then_inc(e_lo, 1)
            with pool.Fori(0, NTT) as i:
                pool.wait_ge(meanvar, i + 1)
                nc.gpsimd.tensor_tensor(ve[:], mv[:, 1:2], eps[:], ALU.add).then_inc(vareps, 1)
                pool.wait_ge(vareps, i + 1)
                nc.gpsimd.tensor_tensor(rstd[:], ve[:], neghalf[:], ALU.pow).then_inc(rstd_ok, 1)

        @block.scalar
        def _(act):
            with act.Fori(0, H2 // 2) as i:
                for k in range(2):
                    act.wait_ge(w_in[k], i * 32 + 32)
                    act.wait_ge(head_ok, i * 2 + k + 1)
                    nc.scalar.activation(wh[:, k], wr[:, k], ACT.Copy).then_inc(w_hi, 1)
                    nc.scalar.activation(oh[:, k], orw[:, k], ACT.Copy).then_inc(w_hi, 1)
            act.wait_ge(e_in, 48)
            for c in range(DC):
                nc.scalar.activation(erh[:, c], er[:, c], ACT.Copy).then_inc(e_hi, 1)
            for c in range(KC):
                nc.scalar.activation(ebh[:, c], eb[:, c], ACT.Copy).then_inc(e_hi, 1)

            def front(t):
                act.wait_ge(r_ps, t + 1)
                nc.scalar.activation(rs[:], ps[:, 3, 0:NE], ACT.Copy).then_inc(r_ok, 1)
                act.wait_ge(ntop_ok, t + 1)
                act.wait_ge(r_ok, t + 1)
                nc.scalar.activation(ex[:], rs[:], ACT.Exp, bias=ntop[:, 0:1]).then_inc(ex_ok, 1)

            def tokens(t):
                act.wait_ge(xt_ps, t + 1)
                nc.scalar.activation(xh[:].rearrange("p c t -> p (c t)"), ps[:, 0], ACT.Copy).then_inc(xt_hi, 1)

            def back(i):
                for h in range(2):
                    act.wait_ge(gt_ps, i * 2 + h + 1)
                    nc.scalar.activation(gh[:, 4 * h:4 * h + 4].rearrange("p c t -> p (c t)"), ps[:, 4 + h], ACT.Copy).then_inc(gt_hi, 1)

            tokens(0)
            front(0)
            with act.Fori(0, NTT - 1) as i:
                back(i)
                tokens(i + 1)
                front(i + 1)
            back(NTT - 1)

        @block.vector
        def _(dve):
            dve.nop().then_inc(res_ok, 1)
            with dve.Fori(0, H2 // 2) as i:
                for k in range(2):
                    dve.wait_ge(w_hi, i * 4 + (2 * k + 2))
                    nc.vector.tensor_tensor(ol[:, k], orw[:, k], oh[:, k].bitcast(F32), ALU.subtract).then_inc(o_lo, 1)
            dve.wait_ge(x_in, 16)
            dve.wait_ge(acc_ok, 1)
            for t in range(NTT):
                nc.vector.tensor_tensor(x2[:, t], ps[:, t], x2[:, t], ALU.add).then_inc(x2_ok, 1)
            dve.wait_ge(e_lo, DC + KC)

            def normalize(i):
                dve.wait_ge(t_in, i * 16 + 16)
                nc.vector.bn_stats(stat[:], xt[:]).then_inc(stats, 1)
                dve.wait_ge(stats, i + 1)
                dve.nop().then_inc(passed, 1)
                nc.vector.bn_aggr(mv[:], stat[:]).then_inc(meanvar, 1)
                dve.wait_ge(rstd_ok, i + 1)
                nc.vector.tensor_scalar(xn[:], xt[:], mv[:, 0:1], rstd[:, 0:1], ALU.subtract, ALU.mult).then_inc(xn_ok, 1)

            def tokens(i):
                dve.wait_ge(xt_hi, i + 1)
                nc.vector.tensor_tensor(xl[:].rearrange("p c t -> p (c t)"), ps[:, 0],
                                        xh[:].rearrange("p c t -> p (c t)").bitcast(F32), ALU.subtract).then_inc(xt_lo, 1)

            def route(i):
                dve.wait_ge(r_ok, i + 1)
                dve.nop().then_inc(go, 1)
                nc.vector.max(top[:, 0], rs[:]).then_inc(top1, 1)
                dve.wait_ge(top1, i + 1)
                nc.vector.tensor_scalar(ntop[:], top[:, 0, 0:1], -1.0, None, ALU.mult).then_inc(ntop_ok, 1)
                nc.vector.match_replace(rest[:, 0], top[:, 0], rs[:], LOWEST).then_inc(rest1, 1)
                dve.wait_ge(rest1, i + 1)
                dve.nop().then_inc(go, 1)
                nc.vector.max(top[:, 1], rest[:, 0]).then_inc(top2, 1)
                dve.wait_ge(top2, i + 1)
                dve.nop().then_inc(go, 1)
                nc.vector.match_replace(rest[:, 1], top[:, 1], rest[:, 0], LOWEST).then_inc(rest2, 1)
                dve.wait_ge(rest2, i + 1)
                nc.vector.tensor_tensor(chosen[:], rest[:, 1], rs[:], ALU.not_equal).then_inc(chosen_ok, 1)
                dve.wait_ge(chosen_ok, i + 1)
                dve.wait_ge(ex_ok, i + 1)
                nc.vector.tensor_tensor_reduce(gate0[:], ex[:], chosen[:], 1.0, 0.0, ALU.mult, ALU.add, gsum[:]).then_inc(sum_ok, 1)
                dve.wait_ge(sum_ok, i + 1)
                nc.vector.reciprocal(ginv[:], gsum[:]).then_inc(inv_ok, 1)
                dve.wait_ge(inv_ok, i + 1)
                nc.vector.tensor_scalar(gate[:], gate0[:], ginv[:, 0:1], SCALING, ALU.mult, ALU.mult).then_inc(gate_ok, 1)
                dve.wait_ge(gate_ok, i + 1)

            def gated(i):
                for h in range(2):
                    dve.wait_ge(h_ps, i * 2 + h + 1)
                    e = slice(h * NE // 2, (h + 1) * NE // 2)
                    nc.vector.tensor_tensor(hg[:, e], ps[:, 1 + h].rearrange("p (e r) -> p e r", r=RANK),
                                            gate[:, e].unsqueeze(2).broadcast_to([P, NE // 2, RANK]), ALU.mult).then_inc(hg_ok, 1)

            def gated_low(i):
                for h in range(2):
                    dve.wait_ge(gt_hi, i * 2 + h + 1)
                    nc.vector.tensor_tensor(gl[:, 4 * h:4 * h + 4].rearrange("p c t -> p (c t)"), ps[:, 4 + h],
                                            gh[:, 4 * h:4 * h + 4].rearrange("p c t -> p (c t)").bitcast(F32),
                                            ALU.subtract).then_inc(gt_lo, 1)

            def result(i):
                dve.wait_ge(y_ps, i + 1)
                dve.wait_ge(res_in, i * 16 + 16)
                dve.wait_ge(stored, i * 16 + 16)
                nc.vector.tensor_tensor(res[:], ps[:, 6], xres[:], ALU.add).then_inc(res_ok, 1)

            normalize(0)
            tokens(0)
            route(0)
            with dve.Fori(0, NTT - 1) as i:
                normalize(i + 1)
                gated(i)
                gated_low(i)
                tokens(i + 1)
                result(i)
                route(i + 1)
            gated(NTT - 1)
            gated_low(NTT - 1)
            result(NTT - 1)

        @block.tensor
        def _(pe):
            for _ in range(2):
                pe.nop().then_inc(head_ok, 1)
            pe.nop().then_inc(stored, 16)
            pe.wait_ge(zero_ok, 1)
            for t in range(NTT):
                nc.tensor.matmul(ps[:, t], zero[:, 0:P], zero[:], start=True, stop=False)
            with pe.Fori(0, H2 // 2) as i:
                for k in range(2):
                    pe.wait_ge(w_lo, i * 2 + k + 1)
                    pe.wait_ge(o_lo, i * 2 + k + 1)
                    for t in range(NTT):
                        s = slice(t * P, (t + 1) * P)
                        last = mm3(nc, ps[:, t], (oh[:, k, s], ol[:, k, s]), (wh[:, k], wl[:, k]), False, False)
                    last.then_inc(head_ok, 1)
            for t in range(NTT):
                last = nc.tensor.matmul(ps[:, t], zero[:, 0:P], zero[:], start=False, stop=True)
            last.then_inc(acc_ok, 1)
            pe.wait_ge(e_in, 48)
            pe.wait_ge(x2_ok, NTT)
            pe.wait_ge(e_lo, DC + KC)

            def turn_tokens(i):
                pe.wait_ge(xn_ok, i + 1)
                for c in range(DC):
                    last = nc.tensor.transpose(ps[:, 0, c * P:(c + 1) * P], xn[:, c * P:(c + 1) * P], idn[:])
                last.then_inc(xt_ps, 1)

            def router_and_h(i):
                pe.wait_ge(xt_lo, i + 1)
                for c in range(DC):
                    last = mm3(nc, ps[:, 3, 0:NE], (xh[:, c], xl[:, c]), (erh[:, c, KR:NR], erl[:, c, KR:NR]), c == 0, c == DC - 1)
                last.then_inc(r_ps, 1)
                for h in range(2):
                    s = slice(h * KR // 2, (h + 1) * KR // 2)
                    for c in range(DC):
                        last = mm3(nc, ps[:, 1 + h], (xh[:, c], xl[:, c]), (erh[:, c, s], erl[:, c, s]), c == 0, c == DC - 1)
                    last.then_inc(h_ps, 1)

            def turn_gated(i):
                for h in range(2):
                    pe.wait_ge(hg_ok, i * 2 + h + 1)
                    for c in range(4):
                        e = (4 * h + c) * (P // RANK)
                        last = nc.tensor.transpose(ps[:, 4 + h, c * P:(c + 1) * P],
                                                   hg[:, e:e + P // RANK].rearrange("p e r -> p (e r)"), idn[:])
                    last.then_inc(gt_ps, 1)

            def experts_out(i):
                for c in range(KC):
                    if c % 4 == 0:
                        pe.wait_ge(gt_lo, i * 2 + c // 4 + 1)
                    last = mm3(nc, ps[:, 6], (gh[:, c], gl[:, c]), (ebh[:, c], ebl[:, c]), c == 0, c == KC - 1)
                last.then_inc(y_ps, 1)

            turn_tokens(0)
            router_and_h(0)
            with pe.Fori(0, NTT - 1) as i:
                turn_tokens(i + 1)
                turn_gated(i)
                experts_out(i)
                router_and_h(i + 1)
            turn_gated(NTT - 1)
            experts_out(NTT - 1)


def build(nc, x, mats, out):
    self_attention(nc, x, mats["ident"], mats["mask"], mats["headmask"], mats["w_qkv"], mats["b_q"], mats["b_k"],
                   mats["b_v"], mats["w_o"], mats["b_o"], mats["x1"], mats["xn2T"])
    query_projection(nc, mats["xn2T"], mats["w_q"], mats["qT"])
    for half in range(2):
        cross_attention(nc, half, mats["ident"], mats["ctx"], mats["xn2T"], mats["qT"], mats["w_k"], mats["w_v"], mats["oT"])
    output_and_experts(nc, mats["ident"], mats["x1"], mats["oT"], mats["w_o2"], mats["w_er"], mats["w_eb"], out)


def kernel(**inputs):
    import numpy as np
    import concourse.bacc as bacc
    from concourse.bass_utils import run_bass_kernel_spmd as run

    a = {k: np.asarray(v) for k, v in inputs.items()}

    def rows(w):
        return np.ascontiguousarray(w.reshape(-1, P, w.shape[1]).transpose(1, 0, 2))

    t = np.arange(PAIR)
    allowed = (t[:, None] // T == t[None] // T) & (t[:, None] >= t[None])
    lay = {
        "x": a["x"].reshape(NTOK, D),
        "ident": np.eye(P, dtype=np.float32),
        "mask": np.tile(np.where(allowed, 0.0, NEG).astype(np.float32), (1, 4)),
        "headmask": np.repeat(np.eye(HPC, dtype=np.float32), HD1, 0),
        "w_qkv": rows(np.concatenate([a["L0_attn_wq_w"].T, np.tile(a["L0_attn_wk_w"].T, (1, HPC)), a["L0_attn_wv_w"].T], 1)),
        "b_q": a["L0_attn_wq_b"].reshape(DC, P).T,
        "b_k": np.tile(a["L0_attn_wk_b"], HPC).reshape(P, 1),
        "b_v": np.tile(a["L0_attn_wv_b"], (PAIR, 1)),
        "w_o": rows(a["L0_attn_wo_w"].T),
        "b_o": np.tile(a["L0_attn_wo_b"], (PAIR, 1)),
        "w_q": a["L0_xattn_Wq"].reshape(DC, P, H2, HD2).transpose(2, 1, 0, 3),
        "w_k": rows(a["L0_xattn_Wk"]),
        "w_v": rows(a["L0_xattn_Wv"]),
        "w_o2": a["L0_xattn_Wo"].reshape(H2, HD2, D),
        "ctx": a["ctx_4096"].reshape(NB, S_CTX, DC, P).transpose(0, 3, 2, 1),
        "w_er": rows(np.concatenate([a["L0_ffn_A"].reshape(NE * RANK, D).T, a["L0_ffn_Wr"].T], 1)),
        "w_eb": rows(a["L0_ffn_B"].transpose(0, 2, 1).reshape(NE * RANK, D)),
    }
    lay = {k: np.ascontiguousarray(v) for k, v in lay.items()}
    nc = bacc.Bacc("TRN2", target_bir_lowering=False, num_devices=1)
    mats = {k: nc.dram_tensor(k, v.shape, mybir.dt.float32, kind="ExternalInput").ap() for k, v in lay.items()}
    for name, shape in (("x1", (NTOK, D)), ("xn2T", (P, DC, NTOK)), ("qT", (P, H2, NTOK)), ("oT", (P, H2, NTOK))):
        mats[name] = nc.dram_tensor(name, shape, mybir.dt.float32, kind="Internal").ap()
    out = nc.dram_tensor("out_0", (NB, T, D), mybir.dt.float32, kind="ExternalOutput").ap()
    build(nc, mats["x"], mats, out)
    r = run(nc, [lay], core_ids=[0])
    return r.results[0]["out_0"]
```

```python
from contextlib import ExitStack

import concourse.bass as bass
from concourse import mybir

F32 = mybir.dt.float32
F32R = mybir.dt.float32r
ALU = mybir.AluOpType
ACT = mybir.ActivationFunctionType
AX_X = mybir.AxisListType.X

P = 128
BANK = 512
D = 512
DC = D // P
NB, T, S_CTX = 16, 56, 1500
NTOK = NB * T
PAIR = 2 * T
NPAIR = NTOK // PAIR
EPS = 1e-5
NEG = -1e30
LOWEST = -3e38

H1, HD1 = 32, 16
HPC = P // HD1
VX = HD1 + 2

H2, HD2, KVH = 32, 128, 4
GQ = H2 // KVH
SCALE2 = float(HD2) ** -0.5
NQ = GQ * T
KEYS = S_CTX + T
NCH = -(-KEYS // P)
GROUP = 3 * P
NG = 4
GW = [GROUP] * (NG - 1) + [KEYS - GROUP * (NG - 1)]
GWMAX = GW[-1]
CW = [P] * (NCH - 1) + [KEYS - P * (NCH - 1)]

NE, TOPK, RANK = 64, 16, 16
SCALING = 32.0 / RANK

HPS = KVH // 2
WC = HPS * HD2


class Space:

    def __init__(self, nc, ctx, stage):
        self.nc, self.ctx, self.stage, self.sems = nc, ctx, stage, []
        ctx.callback(self.release)

    def sb(self, name, shape, dt=F32):
        return self.ctx.enter_context(self.nc.sbuf_tensor(f"{self.stage}_{name}", shape, dt))

    def ps(self, name, shape):
        return self.ctx.enter_context(self.nc.psum_tensor(f"{self.stage}_{name}", shape, F32))

    def sem(self, name):
        self.sems.append(self.nc.alloc_semaphore(f"{self.stage}_{name}"))
        return self.sems[-1]

    def release(self):
        if self.sems:
            self.nc.clear_and_free_semaphores(self.sems)
            self.nc.all_engine_barrier()


def mm3(nc, out, a, b, start, stop):
    nc.tensor.matmul(out, a[0], b[0], start=start, stop=False)
    nc.tensor.matmul(out, a[0], b[1], start=False, stop=False)
    return nc.tensor.matmul(out, a[1], b[0], start=False, stop=stop)


def need(eng, sem, unit, per, k):
    i, ahead = unit
    if isinstance(i, int):
        if (i + ahead) * per + k > 0:
            eng.wait_ge(sem, (i + ahead) * per + k)
    else:
        assert ahead * per + k > 0
        eng.wait_ge(sem, i * per + (ahead * per + k))


def self_attention(nc, x, ident, mask, headmask, w_qkv, b_q, b_k, b_v, w_o, b_o, x1, xn2T):
    with ExitStack() as ctx:
        m = Space(nc, ctx, "sa")
        NW = D + P + HD1
        idn = m.sb("ident", [P, P])
        idn_r = m.sb("ident_r", [PAIR, PAIR], F32R)
        msk = m.sb("mask", [PAIR, 4 * PAIR])
        msk_r = m.sb("mask_r", [PAIR, 4 * PAIR], F32R)
        hmask = m.sb("headmask", [P, HPC])
        wqkv = m.sb("w_qkv", [P, DC, NW])
        wo = m.sb("w_o", [P, DC, D])
        bq = m.sb("b_q", [P, DC])
        bk = m.sb("b_k", [P, 1])
        bv = m.sb("b_v", [PAIR, HD1])
        bo = m.sb("b_o", [PAIR, D])
        neghalf = m.sb("neghalf", [PAIR, 1])
        eps = m.sb("eps", [PAIR, 1])
        xt = m.sb("x", [PAIR, D])
        xr = m.sb("x_residual", [PAIR, D])
        xb = m.sb("x_bias", [PAIR, D])
        stat = m.sb("stat", [PAIR, 6])
        mv = m.sb("meanvar", [PAIR, 2])
        ve = m.sb("var_eps", [PAIR, 1])
        rstd = m.sb("rstd", [PAIR, 1])
        xn = m.sb("xn", [PAIR, D])
        xnT = m.sb("xnT", [P, DC, PAIR])
        qT = m.sb("qT", [P, DC, PAIR])
        kbd = m.sb("k_blockdiag", [P, HPC, PAIR])
        vx = m.sb("v_ones", [PAIR, VX])
        mx = m.sb("rowmax", [PAIR, 2, 4])
        p0 = m.sb("shifted", [PAIR, 2, 4, PAIR])
        pe_ = m.sb("weights", [PAIR, 2, 4, PAIR])
        pT = m.sb("weightsT", [PAIR, 2, 4, PAIR])
        rc = m.sb("recip", [PAIR, H1])
        at = m.sb("attn", [PAIR, H1, HD1])
        aT = m.sb("attnT", [P, DC, PAIR])
        x1t = m.sb("x1", [PAIR, D])
        xn2 = m.sb("xn2", [PAIR, D])
        x2T = m.sb("xn2T", [P, DC, PAIR])
        m0 = m.ps("misc0", [P, BANK])
        m1 = m.ps("misc1", [P, BANK])
        sc = m.ps("scores", [P, 2, BANK])
        tp = m.ps("transposed", [P, 2, BANK])
        ob = m.ps("out", [P, 2, BANK])
        kv = ob[:, 0, 16 * VX:16 * VX + PAIR + HD1]

        loaded, ones, rounded = m.sem("weights_loaded"), m.sem("constants_set"), m.sem("mask_rounded")
        x_in, r_in, issue, passed = m.sem("x_in"), m.sem("residual_in"), m.sem("load_issued"), m.sem("stats_passed")
        stats, meanvar, vareps, rstd_ok, xn_ok = (m.sem(n) for n in ("stats", "meanvar", "vareps", "rstd", "xn"))
        bias_ok, xnT_ps, xnT_ok, q_ps, kv_ps = (m.sem(n) for n in ("x_bias", "xnT_ps", "xnT", "q_ps", "kv_ps"))
        qT_ok, k_ok, v_ok = (m.sem(n) for n in ("qT", "k", "v"))
        s_ps, max_ok, shift_ok, exp_ok = (m.sem(n) for n in ("scores_ps", "max", "shifted", "exp"))
        pT_ps, pT_ok, o_ps = (m.sem(n) for n in ("weightsT_ps", "weightsT", "out_ps"))
        rc_ok, at_ok, aT_ps, aT_ok, wo_ps = (m.sem(n) for n in ("recip", "attn", "attnT_ps", "attnT", "wo_ps"))
        x1_ok, x1_out, stats2, meanvar2, vareps2 = (m.sem(n) for n in ("x1", "x1_out", "stats2", "meanvar2", "vareps2"))
        rstd2_ok, xn2_ok, x2T_ps, x2T_ok, x2T_out = (m.sem(n) for n in ("rstd2", "xn2", "xn2T_ps", "xn2T", "xn2T_out"))
        NS = H1 // 4

        def heads(ap):
            return ap.rearrange("p (h k) -> p h k", h=4)

        def rounds(eng, run):
            run(-1, False, True)
            with eng.Fori(0, NPAIR - 2) as i:
                run(i, True, True)
            run(NPAIR - 2, True, False)

        block = ctx.enter_context(nc.Block())

        @block.sync
        def _(sp):
            sp.dma_start(xt[:], x[0:PAIR]).then_inc(x_in, 16)
            for dst, src in ((idn, ident), (msk, mask), (hmask, headmask), (wqkv, w_qkv), (bq, b_q),
                             (bk, b_k), (bv, b_v), (bo, b_o), (wo, w_o)):
                sp.dma_start(dst[:], src).then_inc(loaded, 16)

            def residual(i):
                need(sp, bias_ok, (i, 0), 1, 1)
                sp.nop().then_inc(issue, 1)
                sp.dma_start(xr[:], x[bass.ds(i * PAIR, PAIR)]).then_inc(r_in, 16)

            def store(i):
                need(sp, x1_ok, (i, 0), 1, 1)
                sp.nop().then_inc(issue, 1)
                sp.dma_start(x1[bass.ds(i * PAIR, PAIR)], x1t[:]).then_inc(x1_out, 16)

            def run(i, leaves, enters):
                if enters:
                    need(sp, xn_ok, (i, 1), 1, 1)
                    sp.nop().then_inc(issue, 1)
                    sp.dma_start(xt[:], x[bass.ds((i + 2) * PAIR, PAIR)]).then_inc(x_in, 16)
                if leaves:
                    residual(i)
                    store(i)

            rounds(sp, run)
            residual(NPAIR - 1)
            store(NPAIR - 1)
            sp.wait_ge(x1_out, 16 * (NPAIR + 1))
            sp.wait_ge(x2T_out, 16 * (NPAIR + 1))

        @block.gpsimd
        def _(pool):
            nc.gpsimd.memset(neghalf[:], -0.5).then_inc(ones, 1)
            nc.gpsimd.memset(vx[:], 1.0).then_inc(ones, 1)
            nc.gpsimd.memset(eps[:], EPS).then_inc(ones, 1)
            pool.nop().then_inc(bias_ok, 1)
            pool.wait_ge(ones, 3)

            def reciprocal_std(unit, of, added, done):
                need(pool, of, unit, 1, 1)
                nc.gpsimd.tensor_tensor(ve[:], mv[:, 1:2], eps[:], ALU.add).then_inc(added, 1)
                need(pool, added, unit, 1, 1)
                nc.gpsimd.tensor_tensor(rstd[:], ve[:], neghalf[:], ALU.pow).then_inc(done, 1)

            def bias(i):
                need(pool, r_in, (i, 0), 16, 16)
                nc.gpsimd.tensor_tensor(xb[:], xr[:], bo[:], ALU.add).then_inc(bias_ok, 1)

            def run(i, leaves, enters):
                if leaves:
                    bias(i)
                if enters:
                    reciprocal_std((i, 2), meanvar, vareps, rstd_ok)
                if leaves:
                    reciprocal_std((i, 0), meanvar2, vareps2, rstd2_ok)

            reciprocal_std((0, 0), meanvar, vareps, rstd_ok)
            pool.wait_ge(loaded, 16 * 9)
            rounds(pool, run)
            bias(NPAIR - 1)
            reciprocal_std((NPAIR - 1, 0), meanvar2, vareps2, rstd2_ok)

        @block.scalar
        def _(act):
            act.wait_ge(loaded, 16 * 9)
            nc.scalar.activation(idn_r[:], idn[0:PAIR, 0:PAIR], ACT.Copy).then_inc(rounded, 1)
            nc.scalar.activation(msk_r[:], msk[:], ACT.Copy).then_inc(rounded, 1)
            act.nop().then_inc(x2T_out, 16)

            def copy_xnT(unit):
                need(act, xnT_ps, unit, 1, 1)
                nc.scalar.activation(xnT[:].rearrange("p c t -> p (c t)"), m0[:, 0:4 * PAIR], ACT.Copy).then_inc(xnT_ok, 1)

            def copy_attnT(i):
                need(act, aT_ps, (i, 0), 1, 1)
                nc.scalar.activation(aT[:].rearrange("p c t -> p (c t)"), m0[:, 0:4 * PAIR], ACT.Copy).then_inc(aT_ok, 1)

            def store_xn2T(i):
                need(act, x2T_ps, (i, 0), 1, 1)
                need(act, x2T_out, (i, 0), 16, 16)
                nc.scalar.activation(x2T[:].rearrange("p c t -> p (c t)"), m0[:, 0:4 * PAIR], ACT.Copy).then_inc(x2T_ok, 1)
                need(act, x2T_ok, (i, 0), 1, 1)
                act.dma_start(xn2T[:, :, bass.ds(i * PAIR, PAIR)], x2T[:]).then_inc(x2T_out, 16)

            def run(i, leaves, enters):
                unit = (i, 1)
                for s in range(NS + 1):
                    if s < NS:
                        need(act, shift_ok, unit, NS, s + 1)
                        nc.scalar.activation(pe_[:, s % 2], p0[:, s % 2], ACT.Exp, scale=float(HD1) ** -0.5).then_inc(exp_ok, 1)
                    if s >= 1:
                        r = s - 1
                        need(act, pT_ps, unit, NS, r + 1)
                        nc.scalar.activation(pT[:, r % 2], heads(tp[0:PAIR, r % 2, 0:4 * PAIR]), ACT.Copy).then_inc(pT_ok, 1)
                    if s == 2 and leaves:
                        copy_attnT(i)
                    if s == 5 and enters:
                        copy_xnT((i, 2))
                    if s == NS and leaves:
                        store_xn2T(i)

            copy_xnT((0, 0))
            rounds(act, run)
            copy_attnT(NPAIR - 1)
            store_xn2T(NPAIR - 1)

        @block.vector
        def _(dve):
            dve.nop().then_inc(x1_out, 16)

            def statistics(unit, src, half, done):
                nc.vector.bn_stats(stat[:], src[:]).then_inc(half, 1)
                need(dve, half, unit, 1, 1)
                dve.nop().then_inc(passed, 1)
                nc.vector.bn_aggr(mv[:], stat[:]).then_inc(done, 1)

            def start_norm(unit):
                need(dve, x_in, unit, 16, 16)
                statistics(unit, xt, stats, meanvar)

            def normalize(unit):
                need(dve, rstd_ok, unit, 1, 1)
                nc.vector.tensor_scalar(xn[:], xt[:], mv[:, 0:1], rstd[:, 0:1], ALU.subtract, ALU.mult).then_inc(xn_ok, 1)

            def queries_keys(unit):
                need(dve, kv_ps, unit, 1, 1)
                nc.vector.scalar_tensor_tensor(kbd[:], kv[:, 0:PAIR].unsqueeze(1).broadcast_to([P, HPC, PAIR]), bk[:, 0:1],
                                               hmask[:].unsqueeze(2).broadcast_to([P, HPC, PAIR]),
                                               ALU.add, ALU.mult).then_inc(k_ok, 1)
                need(dve, q_ps, unit, 1, 1)
                nc.vector.tensor_tensor(qT[:], m1[:, 0:4 * PAIR].rearrange("p (c t) -> p c t", c=DC),
                                        bq[:].unsqueeze(2).broadcast_to([P, DC, PAIR]), ALU.add).then_inc(qT_ok, 1)

            def divide(i):
                for h in range(2):
                    o = ob[0:PAIR, h, 0:16 * VX].rearrange("p (h v) -> p h v", h=16)
                    nc.vector.reciprocal(rc[:, h * 16:(h + 1) * 16], o[:, :, HD1]).then_inc(rc_ok, 1)
                need(dve, rc_ok, (i, 0), 2, 2)
                for h in range(2):
                    o = ob[0:PAIR, h, 0:16 * VX].rearrange("p (h v) -> p h v", h=16)
                    nc.vector.tensor_tensor(at[:, h * 16:(h + 1) * 16], o[:, :, 0:HD1],
                                            rc[:, h * 16:(h + 1) * 16].unsqueeze(2).broadcast_to([PAIR, 16, HD1]),
                                            ALU.mult).then_inc(at_ok, 1)

            def residual(i):
                need(dve, wo_ps, (i, 0), 1, 1)
                need(dve, bias_ok, (i, 0), 1, 2)
                need(dve, x1_out, (i, 0), 16, 16)
                nc.vector.tensor_tensor(x1t[:], m1[0:PAIR, :], xb[:], ALU.add).then_inc(x1_ok, 1)
                need(dve, x1_ok, (i, 0), 1, 1)
                statistics((i, 0), x1t, stats2, meanvar2)

            def normalize_x1(i):
                need(dve, rstd2_ok, (i, 0), 1, 1)
                nc.vector.tensor_scalar(xn2[:], x1t[:], mv[:, 0:1], rstd[:, 0:1], ALU.subtract, ALU.mult).then_inc(xn2_ok, 1)

            def run(i, leaves, enters):
                unit = (i, 1)
                for s in range(NS):
                    need(dve, s_ps, unit, NS, s + 1)
                    sv = heads(sc[0:PAIR, s % 2, 0:4 * PAIR])
                    nc.vector.tensor_reduce(mx[:, s % 2], sv, AX_X, ALU.max).then_inc(max_ok, 1)
                    need(dve, max_ok, unit, NS, s + 1)
                    need(dve, exp_ok, unit, NS, s - 1)
                    nc.vector.tensor_tensor(p0[:, s % 2], sv, mx[:, s % 2].unsqueeze(2).broadcast_to([PAIR, 4, PAIR]),
                                            ALU.subtract).then_inc(shift_ok, 1)
                    if s == 0:
                        if leaves:
                            need(dve, o_ps, (i, 0), NS, NS)
                        nc.vector.tensor_tensor(vx[:, 0:HD1], kv[0:PAIR, PAIR:PAIR + HD1], bv[:], ALU.add).then_inc(v_ok, 1)
                        if leaves:
                            divide(i)
                    if s == 2 and enters:
                        start_norm((i, 2))
                    if s == 3 and enters:
                        normalize((i, 2))
                    if s == 5 and leaves:
                        residual(i)
                    if s == 6 and leaves:
                        normalize_x1(i)
                if enters:
                    queries_keys((i, 2))

            start_norm((0, 0))
            normalize((0, 0))
            dve.wait_ge(loaded, 16 * 9)
            dve.wait_ge(ones, 3)
            queries_keys((0, 0))
            rounds(dve, run)
            dve.wait_ge(o_ps, NPAIR * NS)
            divide(NPAIR - 1)
            residual(NPAIR - 1)
            normalize_x1(NPAIR - 1)

        @block.tensor
        def _(pe):
            pe.wait_ge(loaded, 16 * 9)
            pe.wait_ge(rounded, 2)

            def turn_x(unit):
                need(pe, xn_ok, unit, 1, 1)
                for c in range(DC):
                    last = nc.tensor.transpose(m0[:, c * PAIR:(c + 1) * PAIR], xn[:, c * P:(c + 1) * P], idn[0:PAIR, 0:PAIR])
                last.then_inc(xnT_ps, 1)

            def project_q(unit, chunks):
                need(pe, xnT_ok, unit, 1, 1)
                for cc in chunks:
                    for c in range(DC):
                        last = nc.tensor.matmul(m1[:, cc * PAIR:(cc + 1) * PAIR], wqkv[:, c, cc * P:(cc + 1) * P],
                                                xnT[:, c], start=(c == 0), stop=(c == DC - 1))
                if DC - 1 in chunks:
                    last.then_inc(q_ps, 1)

            def project_kv(unit):
                need(pe, xnT_ok, unit, 1, 1)
                for c in range(DC):
                    nc.tensor.matmul(kv[:, 0:PAIR], wqkv[:, c, D:D + P], xnT[:, c], start=(c == 0), stop=(c == DC - 1))
                for c in range(DC):
                    last = nc.tensor.matmul(kv[0:PAIR, PAIR:PAIR + HD1], xnT[:, c], wqkv[:, c, D + P:NW],
                                            start=(c == 0), stop=(c == DC - 1))
                last.then_inc(kv_ps, 1)

            def turn_attn(i):
                need(pe, at_ok, (i, 0), 2, 2)
                for c in range(DC):
                    last = nc.tensor.transpose(m0[:, c * PAIR:(c + 1) * PAIR],
                                               at[:, c * HPC:(c + 1) * HPC].rearrange("p h v -> p (h v)"),
                                               idn[0:PAIR, 0:PAIR])
                last.then_inc(aT_ps, 1)

            def project_out(i, chunks):
                need(pe, aT_ok, (i, 0), 1, 1)
                for c in chunks:
                    last = nc.tensor.matmul(m1[0:PAIR, :], aT[:, c], wo[:, c], start=(c == 0), stop=(c == DC - 1))
                if DC - 1 in chunks:
                    last.then_inc(wo_ps, 1)

            def turn_xn2(i):
                need(pe, xn2_ok, (i, 0), 1, 1)
                for c in range(DC):
                    last = nc.tensor.transpose(m0[:, c * PAIR:(c + 1) * PAIR], xn2[:, c * P:(c + 1) * P], idn[0:PAIR, 0:PAIR])
                last.then_inc(x2T_ps, 1)

            def scores(unit, s):
                if s == 0:
                    need(pe, qT_ok, unit, 1, 1)
                    need(pe, k_ok, unit, 1, 1)
                need(pe, shift_ok, unit, NS, s - 1)
                out = sc[0:PAIR, s % 2, 0:4 * PAIR]
                h = 4 * (s % 2)
                nc.tensor.matmul(out, qT[:, s // 2], kbd[:, h:h + 4].rearrange("p h k -> p (h k)"), start=True, stop=False)
                nc.tensor.matmul(out, idn_r[:], msk_r[:], start=False, stop=True).then_inc(s_ps, 1)

            def run(i, leaves, enters):
                unit = (i, 1)

                def turn(s):
                    need(pe, exp_ok, unit, NS, s + 1)
                    need(pe, pT_ok, unit, NS, s - 1)
                    for h in range(4):
                        last = nc.tensor.transpose(tp[0:PAIR, s % 2, h * PAIR:(h + 1) * PAIR], pe_[:, s % 2, h],
                                                   idn[0:PAIR, 0:PAIR])
                    last.then_inc(pT_ps, 1)

                def weighted(s):
                    need(pe, pT_ok, unit, NS, s + 1)
                    if s == 0:
                        need(pe, v_ok, unit, 1, 1)
                        if leaves:
                            need(pe, at_ok, (i, 0), 2, 2)
                    for h in range(4):
                        o = (4 * s + h) % 16 * VX
                        last = nc.tensor.matmul(ob[0:PAIR, s // 4, o:o + VX], pT[:, s % 2, h], vx[:], start=True, stop=True)
                    last.then_inc(o_ps, 1)

                for s in range(NS):
                    turn(s)
                    if s + 2 < NS:
                        scores(unit, s + 2)
                    if s >= 1:
                        weighted(s - 1)
                    if s == 1 and leaves:
                        turn_attn(i)
                    if s in (2, 3) and leaves:
                        project_out(i, range(2 * s - 4, 2 * s - 2))
                    if s == 4 and enters:
                        turn_x((i, 2))
                    if s == 5 and enters:
                        project_kv((i, 2))
                    if s in (5, 6) and enters:
                        if leaves:
                            need(pe, x1_ok, (i, 0), 1, 1)
                        project_q((i, 2), range(2 * s - 10, 2 * s - 8))
                    if s == 7 and leaves:
                        turn_xn2(i)
                if enters:
                    scores((i, 2), 0)
                weighted(NS - 1)
                if enters:
                    scores((i, 2), 1)

            turn_x((0, 0))
            project_q((0, 0), range(DC))
            project_kv((0, 0))
            scores((0, 0), 0)
            scores((0, 0), 1)
            rounds(pe, run)
            pe.wait_ge(x2T_ok, NPAIR - 1)
            turn_attn(NPAIR - 1)
            project_out(NPAIR - 1, range(DC))
            turn_xn2(NPAIR - 1)


class Split:

    def __init__(self, m):
        self.w_raw = m.sb("w_raw", [P, 2, DC, WC])
        self.w_hi = m.sb("w_hi", [P, 2, DC, WC], F32R)
        self.w_lo = m.sb("w_lo", [P, 2, DC, WC], F32R)
        self.c_raw = m.sb("ctx_raw", [P, 2, DC, GWMAX])
        self.c_hi = m.sb("ctx_hi", [P, 2, DC, GWMAX], F32R)
        self.c_lo = m.sb("ctx_lo", [P, 2, DC, GWMAX], F32R)


def query_projection(nc, xn2T, w_q, qT_dram, split, w_k, w_v, ctx_dram):
    with ExitStack() as ctx:
        m = Space(nc, ctx, "qp")
        HALF = NTOK // 2
        raw = m.sb("xn_raw", [P, DC, NTOK])
        xh = m.sb("xn_hi", [P, DC, NTOK], F32R)
        xl = m.sb("xn_lo", [P, DC, NTOK], F32R)
        wr = m.sb("w_raw", [P, 2, DC, P])
        wh = m.sb("w_hi", [P, 2, DC, P], F32R)
        wl = m.sb("w_lo", [P, 2, DC, P], F32R)
        st = m.sb("q_stage", [P, 2, NTOK])
        qb = m.ps("q", [P, 4, BANK])
        x_in, x_hi, x_lo = m.sem("xn_in"), m.sem("xn_hi"), m.sem("xn_lo")
        w_in = [m.sem(f"w_in{k}") for k in range(2)]
        w_hi, w_lo, q_ps, lo_half, hi_half = (m.sem(n) for n in ("w_hi", "w_lo", "q_ps", "left_staged", "right_staged"))
        stored = [m.sem(f"stored{k}") for k in range(2)]
        next_in, next_w_hi, next_w_lo, next_c_hi, next_c_lo = (m.sem(n) for n in (
            "next_in", "next_w_hi", "next_w_lo", "next_ctx_hi", "next_ctx_lo"))
        block = ctx.enter_context(nc.Block())

        @block.sync
        def _(sp):
            sp.dma_start(raw[:], xn2T).then_inc(x_in, 16)
            for k in range(2):
                sp.dma_start(wr[:, k], w_q[k]).then_inc(w_in[k], 16)
            for k, w in enumerate((w_k, w_v)):
                sp.dma_start(split.w_raw[:, k], w[:, :, 0:WC]).then_inc(next_in, 16)
            for g in range(2):
                sp.dma_start(split.c_raw[:, g, :, 0:GROUP], ctx_dram[0, :, :, g * GROUP:(g + 1) * GROUP]).then_inc(next_in, 16)
            with sp.Fori(0, H2 // 2 - 1) as i:
                for k in range(2):
                    sp.wait_ge(w_lo, i * 2 + k + 1)
                    sp.dma_start(wr[:, k], w_q[i * 2 + (k + 2)]).then_inc(w_in[k], 16)

        @block.gpsimd
        def _(pool):
            pool.nop().then_inc(q_ps, 2)
            with pool.Fori(0, H2 // 2) as i:
                for k in range(2):
                    pool.wait_ge(w_hi, i * 2 + k + 1)
                    pool.wait_ge(q_ps, i * 2 + k + 1)
                    nc.gpsimd.tensor_tensor(wl[:, k], wr[:, k], wh[:, k].bitcast(F32), ALU.subtract).then_inc(w_lo, 1)
            for n in range(2 * DC):
                g, c = n // DC, n % DC
                pool.wait_ge(next_c_hi, n + 1)
                nc.gpsimd.tensor_tensor(split.c_lo[:, g, c, 0:GROUP], split.c_raw[:, g, c, 0:GROUP],
                                        split.c_hi[:, g, c, 0:GROUP].bitcast(F32), ALU.subtract).then_inc(next_c_lo, 1)

        @block.scalar
        def _(act):
            act.wait_ge(x_in, 16)
            for k in range(2):
                act.nop().then_inc(hi_half, 1)
            for c in range(DC):
                nc.scalar.activation(xh[:, c], raw[:, c], ACT.Copy).then_inc(x_hi, 1)
            for k in range(2):
                act.wait_ge(w_in[k], 16)
                nc.scalar.activation(wh[:, k], wr[:, k], ACT.Copy).then_inc(w_hi, 1)

            def two_heads(i, more):
                for k in range(2):
                    act.wait_ge(q_ps, i * 2 + k + 3)
                    act.wait_ge(stored[k], i * 16 + 16)
                    nc.scalar.activation(st[:, k, HALF:NTOK], qb[:, 2 * k + 1, 0:HALF], ACT.Copy, scale=SCALE2).then_inc(hi_half, 1)
                    act.wait_ge(lo_half, i * 2 + k + 3)
                    act.wait_ge(hi_half, i * 2 + k + 3)
                    act.dma_start(qT_dram[:, i * 2 + k], st[:, k]).then_inc(stored[k], 16)
                    if more:
                        act.wait_ge(w_in[k], i * 16 + 32)
                        nc.scalar.activation(wh[:, k], wr[:, k], ACT.Copy).then_inc(w_hi, 1)

            with act.Fori(0, H2 // 2 - 1) as i:
                two_heads(i, True)
            act.wait_ge(next_in, 64)
            for k in range(2):
                nc.scalar.activation(split.w_hi[:, k], split.w_raw[:, k], ACT.Copy).then_inc(next_w_hi, 1)
            for g in range(2):
                for c in range(DC):
                    nc.scalar.activation(split.c_hi[:, g, c, 0:GROUP], split.c_raw[:, g, c, 0:GROUP], ACT.Copy).then_inc(next_c_hi, 1)
            two_heads(H2 // 2 - 1, False)
            for k in range(2):
                act.wait_ge(stored[k], 16 * (H2 // 2 + 1))

        @block.vector
        def _(dve):
            for c in range(DC):
                dve.wait_ge(x_hi, c + 1)
                nc.vector.tensor_tensor(xl[:, c], raw[:, c], xh[:, c].bitcast(F32), ALU.subtract).then_inc(x_lo, 1)
            for k in range(2):
                dve.nop().then_inc(stored[k], 16)
                dve.nop().then_inc(lo_half, 1)

            def left_halves(i):
                for k in range(2):
                    dve.wait_ge(q_ps, i * 2 + k + 3)
                    dve.wait_ge(stored[k], i * 16 + 16)
                    nc.vector.tensor_scalar(st[:, k, 0:HALF], qb[:, 2 * k, 0:HALF], SCALE2, None, ALU.mult).then_inc(lo_half, 1)

            with dve.Fori(0, H2 // 2 - 1) as i:
                left_halves(i)
            for k in range(2):
                dve.wait_ge(next_w_hi, k + 1)
                nc.vector.tensor_tensor(split.w_lo[:, k], split.w_raw[:, k], split.w_hi[:, k].bitcast(F32),
                                        ALU.subtract).then_inc(next_w_lo, 1)
            left_halves(H2 // 2 - 1)

        @block.tensor
        def _(pe):
            pe.wait_ge(x_lo, DC)
            with pe.Fori(0, H2 // 2) as i:
                for k in range(2):
                    pe.wait_ge(w_lo, i * 2 + k + 1)
                    pe.wait_ge(lo_half, i * 2 + k + 1)
                    pe.wait_ge(hi_half, i * 2 + k + 1)
                    for h in range(2):
                        cols = slice(h * HALF, (h + 1) * HALF)
                        for c in range(DC):
                            last = mm3(nc, qb[:, 2 * k + h, 0:HALF], (wh[:, k, c], wl[:, k, c]),
                                       (xh[:, c, cols], xl[:, c, cols]), start=(c == 0), stop=(c == DC - 1))
                    last.then_inc(q_ps, 1)


NT = 4 * HPS
NS2 = NT * NG


def group_chunks(g):
    return range(3 * g, min(3 * g + 3, NCH) + (g == NG - 1))


SCORE = [(k, g) for g in range(NG) for k in range(4)] + [(k, g) for k in range(4, NT) for g in range(NG)]

KV = [s for g in range(NG) for s in [("K", g, j) for j in range(HPS)] + [("V", g, c) for c in group_chunks(g) if g < 2]]
KV += [("V", g, c) for g in range(2, NG) for c in group_chunks(g)]
NKV = len(KV)
K_DONE = KV.index(("K", NG - 1, HPS - 1)) + 1
GROUP_DONE = [max(n for n, s in enumerate(KV) if s[1] == g) + 1 for g in range(NG)]
LAG = 3
NTB = 3

LAST_TILE = NT - 1
NAHEAD = K_DONE - 1
SAHEAD = 4 * (NG - 1)


def spread(rows, others, lead=0):
    order, n = [], 0
    for m in range(-1, len(rows)):
        if m >= 0:
            order += rows[m]
        while n < len(others) and n < lead + (m + 1) * (len(others) - lead) / len(rows):
            kv = [KV[x[1]] for x in others[n] if x[0] == "KV"]
            if kv and kv[0][0] == "V" and ("PV", 1, kv[0][2]) in sum(rows[m + 1:], []):
                break
            order += others[n]
            n += 1
    return order + [x for step in others[n:] for x in step]


def score_steps():
    steps = [[("S", n, 0)] for n in range(SAHEAD, NS2)]
    for k in range(NT):
        chain = [("F1", k), ("F2", k), ("F3", k)] + [("W", k, g) for g in range(NG) if k == LAST_TILE]
        at = SCORE.index((k, NG - 1)) - SAHEAD + 1
        for f, x in enumerate(chain):
            while len(steps) <= at + f:
                steps.append([])
            steps[at + f].append(x)
    tail = NS2 - SAHEAD + 2
    return steps[:tail] + [[x for step in steps[tail:] for x in step]]


def value_rows(j):
    rows = [[("T", j, m)] * (m < NCH) + [("PV", j, m - LAG)] * (m >= LAG) for m in range(NCH + LAG)]
    rows[-1].append(("O", j))
    return rows


AHEAD = [[("KV", n, 1)] for n in range(NAHEAD)]
for n, x in ((1, ("CX", 1, 0)), (1, ("CX", 1, 1)), (2, ("CX", 1, 2)), (2, ("CX", 1, 3)),
             (4, ("CX", 2, 0)), (5, ("CX", 2, 1)), (6, ("CX", 2, 2)), (7, ("CX", 2, 3)),
             (9, ("CX", 3, 0)), (9, ("CX", 3, 1)), (10, ("CX", 3, 2)), (10, ("CX", 3, 3))):
    assert x[1] < 2 or n >= GROUP_DONE[x[1] - 2] - 1
    assert KV.index(("K", x[1], 0)) > n
    AHEAD[n].append(x)
SCORES_AHEAD = (2, 2, 3, 4, 6, 7, 8, 9, 11, 12, 12, 12)
for n, at in enumerate(SCORES_AHEAD):
    assert KV.index(("K", SCORE[n][1], 0)) < at
    AHEAD[at].append(("S", n, 1))
ALONE = 16
SCORES = score_steps()
REST = [[("KV", n, 0)] for n in range(NAHEAD, NKV)]
QUERIES = [("QX",)]
SCORES_NEXT = [step + [("CX", 0, n - ALONE)] * (0 <= n - ALONE < DC) + QUERIES * (n == NS2 - SAHEAD)
               for n, step in enumerate(SCORES)]
FIRST = [("CX", 0, c) for c in range(DC)] + QUERIES + [x for step in AHEAD for x in step]
STEADY = spread(SCORES_NEXT[:ALONE], REST, 1) + spread(value_rows(0), SCORES_NEXT[ALONE:]) + spread(value_rows(1), AHEAD, 1)
WEIGHTS = [("WX", 0), ("WX", 1)]
TURNOVER = [y for x in STEADY for y in ([x] + WEIGHTS * (x == ("PV", 0, 1)))]
LAST = spread(SCORES[:ALONE], REST, 1) + spread(value_rows(0), SCORES[ALONE:]) + spread(value_rows(1), [])

RING = [x for x in STEADY if x[0] in ("S", "KV")]
THREES = 3 * (-len(RING) % 4)
BANKS = [r % 4 if r < len(RING) - THREES else (r - len(RING) + THREES) % 3 for r in range(len(RING))]
BANK_OF = dict(zip(RING, BANKS))


def before(r):
    back = next(d for d in range(1, len(RING) + 1) if BANKS[r - d] == BANKS[r])
    return RING[r - back], 0 if r >= back else -1


BEFORE = {x: before(r) for r, x in enumerate(RING)}


def scalar_order(order):
    done, late = [], []
    for x in order:
        if x[0] in ("S", "KV", "O"):
            done += late
            late = []
        if x[0] == "S":
            late = [x]
        else:
            done.append(x)
        if x[0] == "T":
            done += late
            late = []
    return done + late


def vector_order(order):
    done, late = [], []
    for last, x in zip([None] + order, order):
        if x[0] != "S" and late:
            done += late
            late = []
        if x[0] == "KV" and x[2] == 0:
            late = [x]
        elif x[0] == "S" and last and last[0] == "T":
            done.insert(len(done) - 1, x)
        else:
            done.append(x)
        if x[0] == "S":
            done += late
            late = []
    return done + late


def passes(eng, run):
    run(FIRST, -1, 0)
    with eng.Fori(0, NB - 1) as i:
        run(STEADY, i, 0)
    run(TURNOVER, NB - 1, 0)
    with eng.Fori(NB, 2 * NB - 1) as i:
        run(STEADY, i, 1)
    run(LAST, 2 * NB - 1, 1)


def cross_attention(nc, split, ident, ctx_dram, xn2T, qT_dram, w_k, w_v, oT_dram):
    with ExitStack() as stack:
        m = Space(nc, stack, "ca")
        HQ = HPS * GQ
        idn = m.sb("ident", [P, P])
        w_raw, w_hi, w_lo = split.w_raw, split.w_hi, split.w_lo
        craw, chi, clo = split.c_raw, split.c_hi, split.c_lo
        qraw = m.sb("q_raw", [P, HQ * T])
        qhi = m.sb("q_hi", [P, HQ * T], F32R)
        qlo = m.sb("q_lo", [P, HQ * T], F32R)
        khi = m.sb("k_hi", [P, HPS, KEYS], F32R)
        klo = m.sb("k_lo", [P, HPS, KEYS], F32R)
        vhi = m.sb("v_hi", [P, NCH, WC], F32R)
        vlo = m.sb("v_lo", [P, NCH, WC], F32R)
        pr = m.sb("weights", [PAIR, NT, KEYS])
        ptl = m.sb("weightsT_lo", [P, 4, NQ], F32R)
        pth = m.sb("weightsT_hi", [P, 4, NQ], F32R)
        nmax = m.sb("neg_groupmax", [PAIR, NT, NG])
        nrow = m.sb("neg_rowmax", [PAIR, NT])
        gsum = m.sb("groupsum", [PAIR, NT, NG])
        corr = m.sb("correction", [PAIR, NT, NG])
        junk = m.sb("product", [PAIR, NT, NG])
        rsum = m.sb("rowsum", [PAIR, NT])
        rinv = m.sb("inv_rowsum", [PAIR, NT])
        fac = m.sb("factor", [PAIR, NT, NG])
        ost = m.sb("out_stage", [P, HPS, NQ])
        bank = m.ps("scores", [P, 4, BANK])
        tb = m.ps("turned", [P, NTB, BANK])
        acc = m.ps("out", [P, BANK])

        wkv_in, idn_in = [m.sem("wk_in"), m.sem("wv_in")], m.sem("ident_in")
        w_hi_ok, w_lo_ok = m.sem("w_hi"), m.sem("w_lo")
        raw_in = [m.sem(f"ctx_in{r}") for r in range(2)]
        c_hi, c_lo, q_in, q_hi, q_lo = (m.sem(n) for n in ("ctx_hi", "ctx_lo", "q_in", "q_hi", "q_lo"))
        kv_ps, kv_hi, kv_lo = (m.sem(n) for n in ("kv_ps", "kv_hi", "kv_lo"))
        s_ps, gmax_ok, rmax_ok, exp_ok, corr_ok = (m.sem(n) for n in ("scores_ps", "groupmax", "rowmax", "exp", "correction"))
        sum_ok, inv_ok, fac_ok, p_ok = (m.sem(n) for n in ("rowsum", "inv_rowsum", "factor", "weights"))
        t_ps, t_hi, t_lo, pv_ok, o_ok = (m.sem(n) for n in ("turned_ps", "turned_hi", "turned_lo", "pv", "out_staged"))
        o_out = [m.sem(f"out_stored{j}") for j in range(HPS)]
        issue, p_last = m.sem("load_issued"), m.sem("last_weights")
        q_lo_0 = m.sem("first_q_lo")

        def chunk_of(c):
            g = min(c // 3, NG - 1)
            return g % 2, (c - 3 * g) * P

        block = stack.enter_context(nc.Block())

        @block.sync
        def _(sp):
            def queries(i, half):
                need(sp, q_lo, (i, 0), 1, 1)
                sp.nop().then_inc(issue, 1)
                sp.dma_start(qraw[:].rearrange("p (h t) -> p h t", h=HQ),
                             qT_dram[:, half * HQ:(half + 1) * HQ, bass.ds((i - half * NB) * T, T)]).then_inc(q_in, 16)

            def load(i, half, g):
                unit, seq = (i, 0), i - half * NB
                need(sp, c_lo, unit, NG * DC, (g + 1) * DC)
                sp.nop().then_inc(issue, 1)
                w = min(GW[g], S_CTX - g * GROUP)
                sp.dma_start(craw[:, g % 2, :, 0:w], ctx_dram[seq, :, :, g * GROUP:g * GROUP + w]).then_inc(raw_in[g % 2], 16)
                if g == 0:
                    queries(i, half)
                if g == NG - 1:
                    sp.dma_start(craw[:, g % 2, :, w:w + T], xn2T[:, :, bass.ds(seq * T, T)]).then_inc(raw_in[g % 2], 16)

            def store(i, half, j):
                need(sp, o_ok, (i, 0), HPS, j + 2)
                sp.nop().then_inc(issue, 1)
                sp.dma_start(oT_dram[:, half * HQ + j * GQ:half * HQ + (j + 1) * GQ, bass.ds((i - half * NB) * T, T)],
                             ost[:, j].rearrange("p (h t) -> p h t", h=GQ)).then_inc(o_out[j], 16)

            def turn(i, half, next_half, after_half):
                if next_half is not None:
                    load(i + 1, next_half, 2)
                store(i, half, 0)
                if next_half is not None:
                    load(i + 1, next_half, 3)
                if after_half is not None:
                    load(i + 2, after_half, 0)
                    load(i + 2, after_half, 1)
                store(i, half, 1)

            queries(0, 0)
            sp.dma_start(idn[:], ident).then_inc(idn_in, 16)
            for g in range(2):
                sp.nop().then_inc(raw_in[g], 16)
            for g in range(2, NG):
                load(0, 0, g)
            for k, w in enumerate((w_k, w_v)):
                sp.dma_start(w_raw[:, k], w[:, :, WC:2 * WC]).then_inc(wkv_in[k], 16)
            for g in range(2):
                load(1, 0, g)
            with sp.Fori(0, NB - 2) as i:
                turn(i, 0, 0, 0)
            turn(NB - 2, 0, 0, 1)
            turn(NB - 1, 0, 1, 1)
            with sp.Fori(NB, 2 * NB - 2) as i:
                turn(i, 1, 1, 1)
            turn(2 * NB - 2, 1, 1, None)
            turn(2 * NB - 1, 1, None, None)
            for j in range(HPS):
                sp.wait_ge(o_out[j], 16 * (2 * NB + 1))

        @block.gpsimd
        def _(pool):
            pool.nop().then_inc(c_lo, 2 * DC)
            pool.nop().then_inc(q_lo, 1)
            def run(order, i, half):
                for step in order:
                    unit = (i, 1)
                    if step[0] == "F3":
                        k = step[1]
                        need(pool, inv_ok, (i, 0), NT, k + 1)
                        nc.gpsimd.tensor_tensor(fac[:, k], corr[:, k], rinv[:, k:k + 1].broadcast_to([PAIR, NG]),
                                                ALU.mult).then_inc(fac_ok, 1)
                    if step[0] == "F3" and step[1] != LAST_TILE:
                        need(pool, fac_ok, (i, 0), NT, k + 1)
                        a = pr[:, k, 0:3 * GROUP].rearrange("p (g w) -> p g w", g=3)
                        nc.gpsimd.tensor_tensor(a, a, fac[:, k, 0:3].unsqueeze(2).broadcast_to([PAIR, 3, GROUP]), ALU.mult)
                        b = pr[:, k, 3 * GROUP:KEYS]
                        nc.gpsimd.tensor_tensor(b, b, fac[:, k, 3:4].broadcast_to([PAIR, GW[3]]), ALU.mult).then_inc(p_ok, 1)
                    elif step[0] == "QX" and order is FIRST:
                        pool.wait_ge(q_lo_0, 1)
                        pool.nop().then_inc(q_lo, 1)
                    elif step[0] == "CX" and step[1] < 2 and order is FIRST:
                        pool.nop().then_inc(c_lo, 1)
                    elif step[0] == "QX":
                        need(pool, q_hi, unit, 1, 1)
                        nc.gpsimd.tensor_tensor(qlo[:], qraw[:], qhi[:].bitcast(F32), ALU.subtract).then_inc(q_lo, 1)
                    elif step[0] == "CX":
                        _, g, c = step
                        w, r = GW[g], g % 2
                        need(pool, c_hi, unit, NG * DC, g * DC + c + 1)
                        nc.gpsimd.tensor_tensor(clo[:, r, c, 0:w], craw[:, r, c, 0:w], chi[:, r, c, 0:w].bitcast(F32),
                                                ALU.subtract).then_inc(c_lo, 1)

            passes(pool, run)

        @block.scalar
        def _(act):
            act.nop().then_inc(o_ok, 1)
            for j in range(HPS):
                act.nop().then_inc(o_out[j], 16)

            def run(order, i, half):
                for step in scalar_order(order):
                    if step[0] == "WX":
                        need(act, kv_ps, (i, 0), NKV, NKV)
                        k = step[1]
                        act.wait_ge(wkv_in[k], 16)
                        nc.scalar.activation(w_hi[:, k], w_raw[:, k], ACT.Copy).then_inc(w_hi_ok, 1)
                    elif step[0] == "S":
                        n, unit = step[1], (i, step[2])
                        k, g = SCORE[n]
                        need(act, gmax_ok, unit, NS2, n + 1)
                        nc.scalar.activation(pr[:, k, g * GROUP:g * GROUP + GW[g]], bank[0:PAIR, BANK_OF[step], 0:GW[g]], ACT.Exp,
                                             bias=nmax[:, k, g:g + 1], accum_out=gsum[:, k, g:g + 1]).then_inc(exp_ok, 1)
                        if g == NG - 1:
                            need(act, rmax_ok, (i, 0), NT, k + 1)
                            nc.scalar.activation(corr[:, k], nmax[:, k], ACT.Exp, bias=nrow[:, k:k + 1],
                                                 scale=-1.0).then_inc(corr_ok, 1)
                    elif step[0] == "T":
                        _, j, c = step
                        need(act, t_ps, (i, 0), 2 * NCH, NCH * j + c + 1)
                        nc.scalar.activation(pth[0:CW[c], c % 4, :], tb[0:CW[c], c % NTB, 0:NQ],
                                             ACT.Copy).then_inc(t_hi, 1)
                    elif step[0] == "QX":
                        need(act, q_in, (i, 1), 16, 16)
                        need(act, s_ps, (i, 1), NS2, 0)
                        nc.scalar.activation(qhi[:], qraw[:], ACT.Copy).then_inc(q_hi, 1)
                    elif step[0] == "CX" and step[1] < 2 and order is FIRST:
                        act.nop().then_inc(c_hi, 1)
                    elif step[0] == "CX":
                        _, g, c = step
                        w, r, unit = GW[g], g % 2, (i, 1)
                        if c == 0:
                            need(act, raw_in[r], unit, 32 + 16 * r, 16 * (g // 2 + 1) + 16 * (g == NG - 1))
                            need(act, kv_ps, unit, NKV, GROUP_DONE[g - 2] if g >= 2 else GROUP_DONE[g + 2] - NKV)
                        nc.scalar.activation(chi[:, r, c, 0:w], craw[:, r, c, 0:w], ACT.Copy).then_inc(c_hi, 1)
                    elif step[0] == "KV":
                        unit = (i, step[2])
                        need(act, kv_ps, unit, NKV, step[1] + 1)
                        kind, g, x = KV[step[1]]
                        b = BANK_OF[step]
                        if kind == "K":
                            nc.scalar.activation(khi[:, x, g * GROUP:g * GROUP + GW[g]], bank[:, b, 0:GW[g]], ACT.Copy).then_inc(kv_hi, 1)
                        else:
                            nc.scalar.activation(vhi[0:CW[x], x], bank[0:CW[x], b, 0:WC], ACT.Copy).then_inc(kv_hi, 1)
                    elif step[0] == "O":
                        j = step[1]
                        need(act, pv_ok, (i, 0), 2 * NCH, NCH * (j + 1))
                        need(act, o_out[j], (i, 0), 16, 16)
                        nc.scalar.activation(ost[:, j], acc[:, 0:NQ], ACT.Copy).then_inc(o_ok, 1)

            passes(act, run)

        @block.vector
        def _(dve):
            def run(order, i, half):
                for step in vector_order(order):
                    if step[0] == "WX":
                        k = step[1]
                        dve.wait_ge(w_hi_ok, k + 1)
                        nc.vector.tensor_tensor(w_lo[:, k], w_raw[:, k], w_hi[:, k].bitcast(F32), ALU.subtract).then_inc(w_lo_ok, 1)
                    elif step[0] == "S":
                        n, unit = step[1], (i, step[2])
                        k, g = SCORE[n]
                        need(dve, s_ps, unit, NS2, n + 1)
                        nc.vector.tensor_reduce(nmax[:, k, g:g + 1], bank[0:PAIR, BANK_OF[step], 0:GW[g]], AX_X, ALU.max,
                                                negate=True).then_inc(gmax_ok, 1)
                        if g == NG - 1:
                            need(dve, gmax_ok, unit, NS2, n + 1)
                            nc.vector.tensor_reduce(nrow[:, k:k + 1], nmax[:, k], AX_X, ALU.min).then_inc(rmax_ok, 1)
                    elif step[0] == "F1":
                        k = step[1]
                        need(dve, corr_ok, (i, 0), NT, k + 1)
                        nc.vector.tensor_tensor_reduce(junk[:, k], gsum[:, k], corr[:, k], 1.0, 0.0, ALU.mult, ALU.add,
                                                       rsum[:, k:k + 1]).then_inc(sum_ok, 1)
                    elif step[0] == "F2":
                        k = step[1]
                        need(dve, sum_ok, (i, 0), NT, k + 1)
                        nc.vector.reciprocal(rinv[:, k:k + 1], rsum[:, k:k + 1]).then_inc(inv_ok, 1)
                    elif step[0] == "W":
                        _, k, g = step
                        w = pr[:, k, g * GROUP:g * GROUP + GW[g]]
                        need(dve, fac_ok, (i, 0), NT, k + 1)
                        last = nc.vector.tensor_scalar(w, w, fac[:, k, g:g + 1], None, ALU.mult)
                        if g == NG - 1:
                            last.then_inc(p_last, 1)
                    elif step[0] == "T":
                        _, j, c = step
                        need(dve, t_hi, (i, 0), 2 * NCH, NCH * j + c + 1)
                        nc.vector.tensor_tensor(ptl[0:CW[c], c % 4, :], tb[0:CW[c], c % NTB, 0:NQ],
                                                pth[0:CW[c], c % 4, :].bitcast(F32), ALU.subtract).then_inc(t_lo, 1)
                    elif step[0] == "KV":
                        need(dve, kv_hi, (i, step[2]), NKV, step[1] + 1)
                        kind, g, x = KV[step[1]]
                        b = BANK_OF[step]
                        if kind == "K":
                            s = slice(g * GROUP, g * GROUP + GW[g])
                            nc.vector.tensor_tensor(klo[:, x, s], bank[:, b, 0:GW[g]], khi[:, x, s].bitcast(F32),
                                                    ALU.subtract).then_inc(kv_lo, 1)
                        else:
                            nc.vector.tensor_tensor(vlo[0:CW[x], x], bank[0:CW[x], b, 0:WC], vhi[0:CW[x], x].bitcast(F32),
                                                    ALU.subtract).then_inc(kv_lo, 1)

            dve.wait_ge(q_hi, 1)
            nc.vector.tensor_tensor(qlo[:], qraw[:], qhi[:].bitcast(F32), ALU.subtract).then_inc(q_lo_0, 1)
            passes(dve, run)

        @block.tensor
        def _(pe):
            pe.wait_ge(idn_in, 16)

            def bank_free(step, i):
                user, back = BEFORE[step]
                if user[0] == "S":
                    need(pe, exp_ok, (i, back + user[2]), NS2, user[1] + 1)
                else:
                    need(pe, kv_lo, (i, back + user[2]), NKV, user[1] + 1)

            def run(order, i, half):
                for step in order:
                    if step[0] == "S":
                        n, unit = step[1], (i, step[2])
                        k, g = SCORE[n]
                        if n == 0:
                            need(pe, q_lo, unit, 1, 2)
                        need(pe, kv_lo, unit, NKV, KV.index(("K", g, k // 4)) + 1)
                        bank_free(step, i)
                        j, cols = k // 4, slice(k * PAIR, (k + 1) * PAIR)
                        s = slice(g * GROUP, g * GROUP + GW[g])
                        mm3(nc, bank[0:PAIR, BANK_OF[step], 0:GW[g]], (qhi[:, cols], qlo[:, cols]), (khi[:, j, s], klo[:, j, s]),
                            True, True).then_inc(s_ps, 1)
                    elif step[0] == "T":
                        _, j, c = step
                        if c == 0:
                            need(pe, p_ok, (i, 0), NT - 1, min(4 * (j + 1), NT - 1))
                            if j == HPS - 1:
                                need(pe, p_last, (i, 0), 1, 1)
                        if c >= NTB:
                            need(pe, t_lo, (i, 0), 2 * NCH, NCH * j + c - NTB + 1)
                        for q in range(4):
                            last = nc.tensor.transpose(tb[0:CW[c], c % NTB, q * PAIR:(q + 1) * PAIR],
                                                       pr[:, 4 * j + q, c * P:c * P + CW[c]], idn[0:PAIR, 0:PAIR])
                        last.then_inc(t_ps, 1)
                    elif step[0] == "PV":
                        _, j, c = step
                        if c == 0:
                            need(pe, kv_lo, (i, 0), NKV, NKV)
                            need(pe, o_ok, (i, 0), HPS, j + 1)
                        need(pe, t_lo, (i, 0), 2 * NCH, NCH * j + c + 1)
                        w, s = CW[c], slice(j * HD2, (j + 1) * HD2)
                        mm3(nc, acc[:, 0:NQ], (vhi[0:w, c, s], vlo[0:w, c, s]), (pth[0:w, c % 4], ptl[0:w, c % 4]),
                            c == 0, c == NCH - 1).then_inc(pv_ok, 1)
                    elif step[0] == "KV":
                        n, unit = step[1], (i, step[2])
                        bank_free(step, i)
                        kind, g, x = KV[n]
                        if order is TURNOVER and step[2]:
                            pe.wait_ge(w_lo_ok, 2)
                        if (kind, x) == ("K", 0):
                            need(pe, c_lo, unit, NG * DC, (g + 3) * DC)
                        for c in range(DC):
                            st, sp_ = c == 0, c == DC - 1
                            if kind == "K":
                                s = slice(x * HD2, (x + 1) * HD2)
                                last = mm3(nc, bank[:, BANK_OF[step], 0:GW[g]], (w_hi[:, 0, c, s], w_lo[:, 0, c, s]),
                                           (chi[:, g % 2, c, 0:GW[g]], clo[:, g % 2, c, 0:GW[g]]), st, sp_)
                            else:
                                o = (x - 3 * g) * P
                                s = slice(o, o + CW[x])
                                last = mm3(nc, bank[0:CW[x], BANK_OF[step], 0:WC], (chi[:, g % 2, c, s], clo[:, g % 2, c, s]),
                                           (w_hi[:, 1, c], w_lo[:, 1, c]), st, sp_)
                        last.then_inc(kv_ps, 1)

            passes(pe, run)


def output_and_experts(nc, ident, x1, oT_dram, w_o, w_er, w_eb, out):
    with ExitStack() as ctx:
        m = Space(nc, ctx, "oe")
        NTT = NTOK // P
        KR = NE * RANK
        KC = KR // P
        NR = KR + NE
        idn = m.sb("ident", [P, P])
        zero = m.sb("zero", [P, D], F32R)
        wr = m.sb("wo_raw", [P, 2, D])
        wh = m.sb("wo_hi", [P, 2, D], F32R)
        wl = m.sb("wo_lo", [P, 2, D], F32R)
        orw = m.sb("o_raw", [P, 2, NTOK])
        oh = m.sb("o_hi", [P, 2, NTOK], F32R)
        ol = m.sb("o_lo", [P, 2, NTOK], F32R)
        er = m.sb("er_raw", [P, DC, NR])
        erh = m.sb("er_hi", [P, DC, NR], F32R)
        erl = m.sb("er_lo", [P, DC, NR], F32R)
        eb = m.sb("eb_raw", [P, KC, D])
        ebh = m.sb("eb_hi", [P, KC, D], F32R)
        ebl = m.sb("eb_lo", [P, KC, D], F32R)
        x2 = m.sb("x2", [P, NTT, D])
        xt = m.sb("x2_tile", [P, D])
        xres = m.sb("x2_residual", [P, D])
        neghalf, eps = m.sb("neghalf", [P, 1]), m.sb("eps", [P, 1])
        stat, mv, ve, rstd = m.sb("stat", [P, 6]), m.sb("meanvar", [P, 2]), m.sb("var_eps", [P, 1]), m.sb("rstd", [P, 1])
        xn = m.sb("xn", [P, D])
        xh = m.sb("xnT_hi", [P, DC, P], F32R)
        xl = m.sb("xnT_lo", [P, DC, P], F32R)
        rs = m.sb("router", [P, NE])
        top = m.sb("top", [P, 2, 8])
        rest = m.sb("rest", [P, 2, NE])
        ntop = m.sb("neg_top", [P, 1])
        ex = m.sb("exp", [P, NE])
        chosen = m.sb("chosen", [P, NE])
        gate0, gsum, ginv = m.sb("gate0", [P, NE]), m.sb("gatesum", [P, 1]), m.sb("gateinv", [P, 1])
        gate = m.sb("gate", [P, NE])
        hg = m.sb("gated", [P, NE, RANK])
        gh = m.sb("gatedT_hi", [P, KC, P], F32R)
        gl = m.sb("gatedT_lo", [P, KC, P], F32R)
        res = m.sb("result", [P, D])
        ps = m.ps("ps", [P, 8, BANK])

        x_in, e_in, x2_ok = (m.sem(n) for n in ("x1_in", "experts_in", "x2"))
        w_in = [m.sem(f"wo_in{k}") for k in range(2)]
        w_hi, w_lo, o_lo, head_ok, acc_ok = (m.sem(n) for n in ("wo_hi", "wo_lo", "o_lo", "head", "accumulated"))
        zero_ok, load_go, res_in = m.sem("zeros_set"), m.sem("load_issued"), m.sem("residual_in")
        e_hi, e_lo = m.sem("experts_hi"), m.sem("experts_lo")
        t_in, stats, passed, meanvar, vareps, rstd_ok, xn_ok = (m.sem(n) for n in (
            "tile_in", "stats", "stats_passed", "meanvar", "vareps", "rstd", "xn"))
        xt_ps, xt_hi, xt_lo, r_ps, h_ps, r_ok = (m.sem(n) for n in ("xnT_ps", "xnT_hi", "xnT_lo", "router_ps", "h_ps", "router"))
        top1, rest1, top2, rest2, go = (m.sem(n) for n in ("top1", "rest1", "top2", "rest2", "max_passed"))
        ntop_ok, ex_ok, chosen_ok, sum_ok, inv_ok, gate_ok, hg_ok = (m.sem(n) for n in (
            "negtop", "exp", "chosen", "gatesum", "gateinv", "gate", "gated"))
        gt_ps, gt_hi, gt_lo, y_ps, res_ok, stored = (m.sem(n) for n in (
            "gatedT_ps", "gatedT_hi", "gatedT_lo", "y_ps", "result", "stored"))
        out_rows = out.rearrange("b t d -> (b t) d")

        block = ctx.enter_context(nc.Block())

        @block.sync
        def _(sp):
            for k in range(2):
                sp.dma_start(wr[:, k], w_o[k]).then_inc(w_in[k], 16)
                sp.dma_start(orw[:, k], oT_dram[:, k]).then_inc(w_in[k], 16)
            sp.dma_start(idn[:], ident).then_inc(e_in, 16)
            parts = [(er[:, 0:2], w_er[:, 0:2], e_in), (er[:, 2:4], w_er[:, 2:4], e_in),
                     (eb[:, 0:4], w_eb[:, 0:4], e_in), (eb[:, 4:8], w_eb[:, 4:8], e_in),
                     (x2[:], x1.rearrange("(n p) d -> p n d", p=P), x_in)]
            per = (H2 // 2 - 1) // len(parts)
            for n, (dst, src, arrived) in enumerate(parts):
                with sp.Fori(n * per, (n + 1) * per) as i:
                    for k in range(2):
                        sp.wait_ge(w_lo, i * 2 + k + 1)
                        sp.wait_ge(o_lo, i * 2 + k + 1)
                        sp.dma_start(wr[:, k], w_o[i * 2 + (k + 2)]).then_inc(w_in[k], 16)
                        sp.dma_start(orw[:, k], oT_dram[:, i * 2 + (k + 2)]).then_inc(w_in[k], 16)
                sp.dma_start(dst, src).then_inc(arrived, 16)
            sp.wait_ge(x2_ok, NTT)
            sp.nop().then_inc(load_go, 1)
            sp.dma_start(xt[:], x2[:, 0]).then_inc(t_in, 16)
            sp.wait_ge(xn_ok, 1)
            sp.nop().then_inc(load_go, 1)
            sp.dma_start(xt[:], x2[:, 1]).then_inc(t_in, 16)

            def tile(i, more):
                sp.wait_ge(res_ok, i + 1)
                sp.nop().then_inc(load_go, 1)
                sp.dma_start(xres[:], x2[:, i]).then_inc(res_in, 16)
                if more:
                    sp.wait_ge(xn_ok, i + 2)
                    sp.nop().then_inc(load_go, 1)
                    sp.dma_start(xt[:], x2[:, i + 2]).then_inc(t_in, 16)
                sp.wait_ge(res_ok, i + 2)
                sp.nop().then_inc(load_go, 1)
                sp.dma_start(out_rows[bass.ds(i * P, P)], res[:]).then_inc(stored, 16)

            with sp.Fori(0, NTT - 2) as i:
                tile(i, True)
            for t in range(NTT - 2, NTT):
                tile(t, False)
            sp.wait_ge(stored, 16 * (NTT + 1))

        @block.gpsimd
        def _(pool):
            nc.gpsimd.memset(zero[:].bitcast(F32), 0.0).then_inc(zero_ok, 1)
            nc.gpsimd.memset(neghalf[:], -0.5)
            nc.gpsimd.memset(eps[:], EPS)
            with pool.Fori(0, H2 // 2) as i:
                for k in range(2):
                    pool.wait_ge(w_hi, i * 4 + (2 * k + 1))
                    nc.gpsimd.tensor_tensor(wl[:, k], wr[:, k], wh[:, k].bitcast(F32), ALU.subtract).then_inc(w_lo, 1)
            for c in range(DC):
                pool.wait_ge(e_hi, c + 1)
                nc.gpsimd.tensor_tensor(erl[:, c], er[:, c], erh[:, c].bitcast(F32), ALU.subtract).then_inc(e_lo, 1)
            for c in range(KC):
                pool.wait_ge(e_hi, DC + c + 1)
                nc.gpsimd.tensor_tensor(ebl[:, c], eb[:, c], ebh[:, c].bitcast(F32), ALU.subtract).then_inc(e_lo, 1)
            with pool.Fori(0, NTT) as i:
                pool.wait_ge(meanvar, i + 1)
                nc.gpsimd.tensor_tensor(ve[:], mv[:, 1:2], eps[:], ALU.add).then_inc(vareps, 1)
                pool.wait_ge(vareps, i + 1)
                nc.gpsimd.tensor_tensor(rstd[:], ve[:], neghalf[:], ALU.pow).then_inc(rstd_ok, 1)

        @block.scalar
        def _(act):
            with act.Fori(0, H2 // 2) as i:
                for k in range(2):
                    act.wait_ge(w_in[k], i * 32 + 32)
                    act.wait_ge(head_ok, i * 2 + k + 1)
                    nc.scalar.activation(wh[:, k], wr[:, k], ACT.Copy).then_inc(w_hi, 1)
                    nc.scalar.activation(oh[:, k], orw[:, k], ACT.Copy).then_inc(w_hi, 1)
            act.wait_ge(e_in, 16 * 5)
            for c in range(DC):
                nc.scalar.activation(erh[:, c], er[:, c], ACT.Copy).then_inc(e_hi, 1)
            for c in range(KC):
                nc.scalar.activation(ebh[:, c], eb[:, c], ACT.Copy).then_inc(e_hi, 1)

            def front(t):
                act.wait_ge(r_ps, t + 1)
                nc.scalar.activation(rs[:], ps[:, 3, 0:NE], ACT.Copy).then_inc(r_ok, 1)
                act.wait_ge(ntop_ok, t + 1)
                act.wait_ge(r_ok, t + 1)
                nc.scalar.activation(ex[:], rs[:], ACT.Exp, bias=ntop[:, 0:1]).then_inc(ex_ok, 1)

            def tokens(t):
                act.wait_ge(xt_ps, t + 1)
                nc.scalar.activation(xh[:].rearrange("p c t -> p (c t)"), ps[:, 0], ACT.Copy).then_inc(xt_hi, 1)

            def back(i):
                for h in range(2):
                    act.wait_ge(gt_ps, i * 2 + h + 1)
                    nc.scalar.activation(gh[:, 4 * h:4 * h + 4].rearrange("p c t -> p (c t)"), ps[:, 4 + h], ACT.Copy).then_inc(gt_hi, 1)

            tokens(0)
            front(0)
            with act.Fori(0, NTT - 1) as i:
                back(i)
                tokens(i + 1)
                front(i + 1)
            back(NTT - 1)

        @block.vector
        def _(dve):
            dve.nop().then_inc(res_ok, 1)
            with dve.Fori(0, H2 // 2) as i:
                for k in range(2):
                    dve.wait_ge(w_hi, i * 4 + (2 * k + 2))
                    nc.vector.tensor_tensor(ol[:, k], orw[:, k], oh[:, k].bitcast(F32), ALU.subtract).then_inc(o_lo, 1)
            dve.wait_ge(x_in, 16)
            dve.wait_ge(acc_ok, 1)
            for t in range(NTT):
                nc.vector.tensor_tensor(x2[:, t], ps[:, t], x2[:, t], ALU.add).then_inc(x2_ok, 1)
            dve.wait_ge(e_lo, DC + KC)

            def normalize(i):
                dve.wait_ge(t_in, i * 16 + 16)
                nc.vector.bn_stats(stat[:], xt[:]).then_inc(stats, 1)
                dve.wait_ge(stats, i + 1)
                dve.nop().then_inc(passed, 1)
                nc.vector.bn_aggr(mv[:], stat[:]).then_inc(meanvar, 1)
                dve.wait_ge(rstd_ok, i + 1)
                nc.vector.tensor_scalar(xn[:], xt[:], mv[:, 0:1], rstd[:, 0:1], ALU.subtract, ALU.mult).then_inc(xn_ok, 1)

            def tokens(i):
                dve.wait_ge(xt_hi, i + 1)
                nc.vector.tensor_tensor(xl[:].rearrange("p c t -> p (c t)"), ps[:, 0],
                                        xh[:].rearrange("p c t -> p (c t)").bitcast(F32), ALU.subtract).then_inc(xt_lo, 1)

            def route(i):
                dve.wait_ge(r_ok, i + 1)
                dve.nop().then_inc(go, 1)
                nc.vector.max(top[:, 0], rs[:]).then_inc(top1, 1)
                dve.wait_ge(top1, i + 1)
                nc.vector.tensor_scalar(ntop[:], top[:, 0, 0:1], -1.0, None, ALU.mult).then_inc(ntop_ok, 1)
                nc.vector.match_replace(rest[:, 0], top[:, 0], rs[:], LOWEST).then_inc(rest1, 1)
                dve.wait_ge(rest1, i + 1)
                dve.nop().then_inc(go, 1)
                nc.vector.max(top[:, 1], rest[:, 0]).then_inc(top2, 1)
                dve.wait_ge(top2, i + 1)
                dve.nop().then_inc(go, 1)
                nc.vector.match_replace(rest[:, 1], top[:, 1], rest[:, 0], LOWEST).then_inc(rest2, 1)
                dve.wait_ge(rest2, i + 1)
                nc.vector.tensor_tensor(chosen[:], rest[:, 1], rs[:], ALU.not_equal).then_inc(chosen_ok, 1)
                dve.wait_ge(chosen_ok, i + 1)
                dve.wait_ge(ex_ok, i + 1)
                nc.vector.tensor_tensor_reduce(gate0[:], ex[:], chosen[:], 1.0, 0.0, ALU.mult, ALU.add, gsum[:]).then_inc(sum_ok, 1)
                dve.wait_ge(sum_ok, i + 1)
                nc.vector.reciprocal(ginv[:], gsum[:]).then_inc(inv_ok, 1)
                dve.wait_ge(inv_ok, i + 1)
                nc.vector.tensor_scalar(gate[:], gate0[:], ginv[:, 0:1], SCALING, ALU.mult, ALU.mult).then_inc(gate_ok, 1)
                dve.wait_ge(gate_ok, i + 1)

            def gated(i):
                for h in range(2):
                    dve.wait_ge(h_ps, i * 2 + h + 1)
                    e = slice(h * NE // 2, (h + 1) * NE // 2)
                    nc.vector.tensor_tensor(hg[:, e], ps[:, 1 + h].rearrange("p (e r) -> p e r", r=RANK),
                                            gate[:, e].unsqueeze(2).broadcast_to([P, NE // 2, RANK]), ALU.mult).then_inc(hg_ok, 1)

            def gated_low(i):
                for h in range(2):
                    dve.wait_ge(gt_hi, i * 2 + h + 1)
                    nc.vector.tensor_tensor(gl[:, 4 * h:4 * h + 4].rearrange("p c t -> p (c t)"), ps[:, 4 + h],
                                            gh[:, 4 * h:4 * h + 4].rearrange("p c t -> p (c t)").bitcast(F32),
                                            ALU.subtract).then_inc(gt_lo, 1)

            def result(i):
                dve.wait_ge(y_ps, i + 1)
                dve.wait_ge(res_in, i * 16 + 16)
                dve.wait_ge(stored, i * 16 + 16)
                nc.vector.tensor_tensor(res[:], ps[:, 6], xres[:], ALU.add).then_inc(res_ok, 1)

            normalize(0)
            tokens(0)
            route(0)
            with dve.Fori(0, NTT - 1) as i:
                normalize(i + 1)
                gated(i)
                gated_low(i)
                tokens(i + 1)
                result(i)
                route(i + 1)
            gated(NTT - 1)
            gated_low(NTT - 1)
            result(NTT - 1)

        @block.tensor
        def _(pe):
            for _ in range(2):
                pe.nop().then_inc(head_ok, 1)
            pe.nop().then_inc(stored, 16)
            pe.wait_ge(zero_ok, 1)
            for t in range(NTT):
                nc.tensor.matmul(ps[:, t], zero[:, 0:P], zero[:], start=True, stop=False)
            with pe.Fori(0, H2 // 2) as i:
                for k in range(2):
                    pe.wait_ge(w_lo, i * 2 + k + 1)
                    pe.wait_ge(o_lo, i * 2 + k + 1)
                    for t in range(NTT):
                        s = slice(t * P, (t + 1) * P)
                        last = mm3(nc, ps[:, t], (oh[:, k, s], ol[:, k, s]), (wh[:, k], wl[:, k]), False, False)
                    last.then_inc(head_ok, 1)
            for t in range(NTT):
                last = nc.tensor.matmul(ps[:, t], zero[:, 0:P], zero[:], start=False, stop=True)
            last.then_inc(acc_ok, 1)
            pe.wait_ge(e_in, 16 * 5)
            pe.wait_ge(x2_ok, NTT)
            pe.wait_ge(e_lo, DC + KC)

            def turn_tokens(i):
                pe.wait_ge(xn_ok, i + 1)
                for c in range(DC):
                    last = nc.tensor.transpose(ps[:, 0, c * P:(c + 1) * P], xn[:, c * P:(c + 1) * P], idn[:])
                last.then_inc(xt_ps, 1)

            def router_and_h(i):
                pe.wait_ge(xt_lo, i + 1)
                for c in range(DC):
                    last = mm3(nc, ps[:, 3, 0:NE], (xh[:, c], xl[:, c]), (erh[:, c, KR:NR], erl[:, c, KR:NR]), c == 0, c == DC - 1)
                last.then_inc(r_ps, 1)
                for h in range(2):
                    s = slice(h * KR // 2, (h + 1) * KR // 2)
                    for c in range(DC):
                        last = mm3(nc, ps[:, 1 + h], (xh[:, c], xl[:, c]), (erh[:, c, s], erl[:, c, s]), c == 0, c == DC - 1)
                    last.then_inc(h_ps, 1)

            def turn_gated(i):
                for h in range(2):
                    pe.wait_ge(hg_ok, i * 2 + h + 1)
                    for c in range(4):
                        e = (4 * h + c) * (P // RANK)
                        last = nc.tensor.transpose(ps[:, 4 + h, c * P:(c + 1) * P],
                                                   hg[:, e:e + P // RANK].rearrange("p e r -> p (e r)"), idn[:])
                    last.then_inc(gt_ps, 1)

            def experts_out(i):
                for c in range(KC):
                    if c % 4 == 0:
                        pe.wait_ge(gt_lo, i * 2 + c // 4 + 1)
                    last = mm3(nc, ps[:, 6], (gh[:, c], gl[:, c]), (ebh[:, c], ebl[:, c]), c == 0, c == KC - 1)
                last.then_inc(y_ps, 1)

            turn_tokens(0)
            router_and_h(0)
            with pe.Fori(0, NTT - 1) as i:
                turn_tokens(i + 1)
                turn_gated(i)
                experts_out(i)
                router_and_h(i + 1)
            turn_gated(NTT - 1)
            experts_out(NTT - 1)


def build(nc, x, mats, out):
    self_attention(nc, x, mats["ident"], mats["mask"], mats["headmask"], mats["w_qkv"], mats["b_q"], mats["b_k"],
                   mats["b_v"], mats["w_o"], mats["b_o"], mats["x1"], mats["xn2T"])
    with ExitStack() as ctx:
        split = Split(Space(nc, ctx, "split"))
        query_projection(nc, mats["xn2T"], mats["w_q"], mats["qT"], split, mats["w_k"], mats["w_v"], mats["ctx"])
        cross_attention(nc, split, mats["ident"], mats["ctx"], mats["xn2T"], mats["qT"], mats["w_k"], mats["w_v"], mats["oT"])
    output_and_experts(nc, mats["ident"], mats["x1"], mats["oT"], mats["w_o2"], mats["w_er"], mats["w_eb"], out)


def kernel(**inputs):
    import numpy as np
    import concourse.bacc as bacc
    from concourse.bass_utils import run_bass_kernel_spmd as run

    a = {k: np.asarray(v) for k, v in inputs.items()}

    def rows(w):
        return np.ascontiguousarray(w.reshape(-1, P, w.shape[1]).transpose(1, 0, 2))

    t = np.arange(PAIR)
    allowed = (t[:, None] // T == t[None] // T) & (t[:, None] >= t[None])
    lay = {
        "x": a["x"].reshape(NTOK, D),
        "ident": np.eye(P, dtype=np.float32),
        "mask": np.tile(np.where(allowed, 0.0, NEG).astype(np.float32), (1, 4)),
        "headmask": np.repeat(np.eye(HPC, dtype=np.float32), HD1, 0),
        "w_qkv": rows(np.concatenate([a["L0_attn_wq_w"].T, np.tile(a["L0_attn_wk_w"].T, (1, HPC)), a["L0_attn_wv_w"].T], 1)),
        "b_q": a["L0_attn_wq_b"].reshape(DC, P).T,
        "b_k": np.tile(a["L0_attn_wk_b"], HPC).reshape(P, 1),
        "b_v": np.tile(a["L0_attn_wv_b"], (PAIR, 1)),
        "w_o": rows(a["L0_attn_wo_w"].T),
        "b_o": np.tile(a["L0_attn_wo_b"], (PAIR, 1)),
        "w_q": a["L0_xattn_Wq"].reshape(DC, P, H2, HD2).transpose(2, 1, 0, 3),
        "w_k": rows(a["L0_xattn_Wk"]),
        "w_v": rows(a["L0_xattn_Wv"]),
        "w_o2": a["L0_xattn_Wo"].reshape(H2, HD2, D),
        "ctx": a["ctx_4096"].reshape(NB, S_CTX, DC, P).transpose(0, 3, 2, 1),
        "w_er": rows(np.concatenate([a["L0_ffn_A"].reshape(NE * RANK, D).T, a["L0_ffn_Wr"].T], 1)),
        "w_eb": rows(a["L0_ffn_B"].transpose(0, 2, 1).reshape(NE * RANK, D)),
    }
    lay = {k: np.ascontiguousarray(v) for k, v in lay.items()}
    nc = bacc.Bacc("TRN2", target_bir_lowering=False, num_devices=1)
    mats = {k: nc.dram_tensor(k, v.shape, mybir.dt.float32, kind="ExternalInput").ap() for k, v in lay.items()}
    for name, shape in (("x1", (NTOK, D)), ("xn2T", (P, DC, NTOK)), ("qT", (P, H2, NTOK)), ("oT", (P, H2, NTOK))):
        mats[name] = nc.dram_tensor(name, shape, mybir.dt.float32, kind="Internal").ap()
    out = nc.dram_tensor("out_0", (NB, T, D), mybir.dt.float32, kind="ExternalOutput").ap()
    build(nc, mats["x"], mats, out)
    r = run(nc, [lay], core_ids=[0])
    return r.results[0]["out_0"]
```
